# Optimizing a Trainium2 kernel written in Bass

```python
import numpy as np
import jax
import jax.numpy as jnp

def _softmax(x, axis=-1):
    return jax.nn.softmax(x, axis=axis)

def _gelu(x):
    return jax.nn.gelu(x, approximate=True)

def _silu(x):
    return jax.nn.silu(x)

def _sigmoid(x):
    return jax.nn.sigmoid(x)

def _layernorm(x, axis=-1, eps=1e-05):
    m = jnp.mean(x, axis=axis, keepdims=True)
    v = jnp.var(x, axis=axis, keepdims=True)
    return (x - m) / jnp.sqrt(v + eps)

def _scatter_add(tgt, idx, src, axis=0):
    return tgt.at[idx].add(src)

def _segment_sum(src, seg, n):
    return jax.ops.segment_sum(src, seg, n)
kernel_name = 'mk_sandwich_d4_jaxref_r8_2a1848'

def setup_inputs(seed: int=0):
    np.random.seed(seed)
    _w = jnp.asarray

    def _L0_attn_setup():
        import jax, jax.numpy as jnp
        import numpy as np
        B, T, C, H = (8, 64, 128, 16)
        N = C // H
        DW, DA, DG = (64, 64, 128)

        def _ln(x, w, b, eps=1e-05):
            mu = x.mean(-1, keepdims=True)
            var = ((x - mu) ** 2).mean(-1, keepdims=True)
            return (x - mu) * jax.lax.rsqrt(var + eps) * w + b

        def _gn_heads(x, w, b, eps=0.00064):
            xh = x.reshape(x.shape[0], x.shape[1], H, N)
            mu = xh.mean(-1, keepdims=True)
            var = ((xh - mu) ** 2).mean(-1, keepdims=True)
            xh = (xh - mu) * jax.lax.rsqrt(var + eps)
            return xh.reshape(x.shape) * w + b

        def _shift(x):
            return jnp.concatenate([jnp.zeros_like(x[:, :1]), x[:, :-1]], axis=1)

        def _wkv7(r, w_log, k, v, a, b):
            decay = jnp.exp(-jnp.exp(w_log))

            def step(state, inp):
                r_t, d_t, k_t, v_t, a_t, b_t = inp
                sa = jnp.einsum('bhij,bhj->bhi', state, a_t)
                state = state * d_t[:, :, None, :] + sa[..., None] * b_t[:, :, None, :] + v_t[..., None] * k_t[:, :, None, :]
                return (state, jnp.einsum('bhij,bhj->bhi', state, r_t))
            xs = tuple((jnp.moveaxis(t, 1, 0) for t in (r, decay, k, v, a, b)))
            s0 = jnp.zeros((r.shape[0], H, N, N), r.dtype)
            _, out = jax.lax.scan(step, s0, xs)
            return jnp.moveaxis(out, 0, 1)

        def _reference_tuple_inner(x, v_first, ln_pre_w, ln_pre_b, ln_attn_w, ln_attn_b, ln_ffn_w, ln_ffn_b, x_r, x_w, x_k, x_v, x_a, x_g, w0, w1, w2, a0, a1, a2, g1, g2, k_k, k_a, r_k, W_r, W_k, W_v, W_o, gn_w, gn_b, ffn_x_k, W_ffn1, W_ffn2):
            Bx, Tx = (x.shape[0], x.shape[1])
            x = _ln(x, ln_pre_w, ln_pre_b)
            xn = _ln(x, ln_attn_w, ln_attn_b)
            dx = _shift(xn) - xn
            xr = xn + dx * x_r
            xw = xn + dx * x_w
            xk = xn + dx * x_k
            xv = xn + dx * x_v
            xa = xn + dx * x_a
            xg = xn + dx * x_g
            r = xr @ W_r
            w_log = -jax.nn.softplus(-(w0 + jnp.tanh(xw @ w1) @ w2)) - 0.5
            k = xk @ W_k
            v = xv @ W_v
            v_first = v
            a = jax.nn.sigmoid(a0 + xa @ a1 @ a2)
            g = jax.nn.sigmoid(xg @ g1) @ g2
            kk = (k * k_k).reshape(Bx, Tx, H, N)
            kk = kk / jnp.maximum(jnp.linalg.norm(kk, axis=-1, keepdims=True), 1e-12)
            k = k * (1.0 + (a - 1.0) * k_a)
            rh = r.reshape(Bx, Tx, H, N)
            kh = k.reshape(Bx, Tx, H, N)
            vh = v.reshape(Bx, Tx, H, N)
            ah = a.reshape(Bx, Tx, H, N)
            o = _wkv7(rh, w_log.reshape(Bx, Tx, H, N), kh, vh, -kk, kk * ah)
            o = _gn_heads(o.reshape(Bx, Tx, C), gn_w, gn_b)
            o = o + ((rh * kh * r_k).sum(-1, keepdims=True) * vh).reshape(Bx, Tx, C)
            x = x + o * g @ W_o
            xf = _ln(x, ln_ffn_w, ln_ffn_b)
            kf = xf + (_shift(xf) - xf) * ffn_x_k
            x = x + jnp.square(jax.nn.relu(kf @ W_ffn1)) @ W_ffn2
            return (x, v_first)
        key = jax.random.key(seed)
        ks = iter(jax.random.split(key, 40))

        def nrm(shape, s=0.02):
            return jax.random.normal(next(ks), shape, jnp.float32) * s
        f32 = jnp.float32
        d = {'x': jax.random.normal(next(ks), (B, T, C), f32), 'v_first': jnp.zeros((B, T, C), f32), 'ln_pre_w': jnp.ones((C,), f32), 'ln_pre_b': jnp.zeros((C,), f32), 'ln_attn_w': jnp.ones((C,), f32), 'ln_attn_b': jnp.zeros((C,), f32), 'ln_ffn_w': jnp.ones((C,), f32), 'ln_ffn_b': jnp.zeros((C,), f32), 'x_r': nrm((C,), 0.1), 'x_w': nrm((C,), 0.1), 'x_k': nrm((C,), 0.1), 'x_v': nrm((C,), 0.1), 'x_a': nrm((C,), 0.1), 'x_g': nrm((C,), 0.1), 'w0': nrm((C,), 0.5), 'w1': nrm((C, DW)), 'w2': nrm((DW, C)), 'a0': nrm((C,), 0.1), 'a1': nrm((C, DA)), 'a2': nrm((DA, C)), 'g1': nrm((C, DG)), 'g2': nrm((DG, C)), 'k_k': 0.85 * jnp.ones((C,), f32) + nrm((C,), 0.05), 'k_a': jnp.ones((C,), f32), 'r_k': nrm((H, N), 0.1), 'W_r': nrm((C, C)), 'W_k': nrm((C, C)), 'W_v': nrm((C, C)), 'W_o': nrm((C, C)), 'gn_w': jnp.ones((C,), f32), 'gn_b': jnp.zeros((C,), f32), 'ffn_x_k': nrm((C,), 0.1), 'W_ffn1': nrm((C, 4 * C)), 'W_ffn2': nrm((4 * C, C))}
        return d
    _L0_attn_in = _L0_attn_setup()

    def _L0_ffn_setup():
        import jax, jax.numpy as jnp
        import numpy as np
        D_MODEL = 128
        D_FF = 512
        N_EXPERTS = 8
        TOP_K = 2

        def _ffn(x, w1, b1, w2, b2):
            h = jax.nn.gelu(x @ w1.T + b1)
            return h @ w2.T + b2
        key = jax.random.key(seed)
        ks = jax.random.split(key, 12)
        s = 0.02
        x = jax.random.normal(ks[0], (4, 256, D_MODEL), dtype=jnp.float32)
        shared_w1 = jax.random.normal(ks[1], (D_FF, D_MODEL), dtype=jnp.float32) * s
        shared_b1 = jnp.zeros((D_FF,), dtype=jnp.float32)
        shared_w2 = jax.random.normal(ks[2], (D_MODEL, D_FF), dtype=jnp.float32) * s
        shared_b2 = jnp.zeros((D_MODEL,), dtype=jnp.float32)
        router_w = jax.random.normal(ks[3], (N_EXPERTS, D_MODEL), dtype=jnp.float32) * s
        router_b = jnp.zeros((N_EXPERTS,), dtype=jnp.float32)
        spec_w1 = jax.random.normal(ks[4], (N_EXPERTS, D_FF, D_MODEL), dtype=jnp.float32) * s
        spec_b1 = jnp.zeros((N_EXPERTS, D_FF), dtype=jnp.float32)
        spec_w2 = jax.random.normal(ks[5], (N_EXPERTS, D_MODEL, D_FF), dtype=jnp.float32) * s
        spec_b2 = jnp.zeros((N_EXPERTS, D_MODEL), dtype=jnp.float32)
        return dict(x=x, shared_w1=shared_w1, shared_b1=shared_b1, shared_w2=shared_w2, shared_b2=shared_b2, router_w=router_w, router_b=router_b, spec_w1=spec_w1, spec_b1=spec_b1, spec_w2=spec_w2, spec_b2=spec_b2)
    _L0_ffn_in = _L0_ffn_setup()

    def _L1_attn_setup():
        import jax, jax.numpy as jnp
        import numpy as np
        import math
        B, N, D, H, G = (4, 256, 128, 16, 256)
        HD = D // H
        MAX_SEQ = 256
        STRIDE = (G - 1) / max(MAX_SEQ - 1, 1)

        def _forward(x, Wqkvg, bqkvg, wave_frequency, wave_damping, wave_phase, field_coupling, Wout, bout):
            b, n, d = x.shape
            qkvg = x @ Wqkvg.T + bqkvg
            q, k, v, gate_raw = jnp.split(qkvg, 4, axis=-1)
            to_heads = lambda t: t.reshape(b, n, H, HD).transpose(0, 2, 1, 3)
            q, k, v = (to_heads(q), to_heads(k), to_heads(v))
            seq_pos = jnp.arange(n, dtype=jnp.float32)
            field_pos = jnp.clip(seq_pos * STRIDE, 0.0, G - 2)
            idx_lo = jnp.clip(field_pos.astype(jnp.int32), 0, G - 2)
            idx_hi = idx_lo + 1
            frac = jnp.clip(field_pos - idx_lo.astype(jnp.float32), 0.0, 1.0)
            w_lo = (1.0 - frac)[None, None, :, None]
            w_hi = frac[None, None, :, None]
            q_feat = jax.nn.elu(q) + 1.0
            k_feat = jax.nn.elu(k) + 1.0
            deposit = k_feat * v
            field = jnp.zeros((b, H, G, HD), deposit.dtype)
            field = field.at[:, :, idx_lo, :].add(deposit * w_lo)
            field = field.at[:, :, idx_hi, :].add(deposit * w_hi)
            t = jnp.arange(G, dtype=jnp.float32)
            alpha = jax.nn.softplus(wave_damping)[:, None]
            omega = wave_frequency[:, None]
            phi = wave_phase[:, None]
            kernels = jnp.exp(-alpha * t[None, :]) * jnp.cos(omega * t[None, :] + phi)
            kernels = kernels / jnp.clip(jnp.sum(jnp.abs(kernels), axis=1, keepdims=True), 1e-08)
            kernel_fft = jnp.fft.rfft(kernels, n=2 * G, axis=-1)
            field_fft = jnp.fft.rfft(field, n=2 * G, axis=2)
            convolved = jnp.fft.irfft(field_fft * kernel_fft[None, :, :, None], n=2 * G, axis=2)[:, :, :G, :]
            coupling = jax.nn.softmax(field_coupling, axis=-1)
            field_c = jnp.einsum('ij,bjgd->bigd', coupling, convolved)
            gathered = field_c[:, :, idx_lo, :] * w_lo + field_c[:, :, idx_hi, :] * w_hi
            wave_output = q_feat * gathered
            gate = jax.nn.sigmoid(gate_raw).reshape(b, n, H, HD).transpose(0, 2, 1, 3)
            output = (wave_output * gate).transpose(0, 2, 1, 3).reshape(b, n, d)
            return output @ Wout.T + bout
        key = jax.random.key(seed)
        ks = jax.random.split(key, 5)
        x = jax.random.normal(ks[0], (B, N, D), jnp.float32)
        Wqkvg = jax.random.normal(ks[1], (4 * D, D), jnp.float32) * 0.02
        Wqkvg = Wqkvg.at[3 * D:].set(0.0)
        bqkvg = jnp.concatenate([jnp.zeros(3 * D, jnp.float32), jnp.full((D,), 2.0, jnp.float32)])
        wave_frequency = jnp.linspace(0.3, 4.0, H, dtype=jnp.float32)
        wave_damping = jnp.linspace(-3.0, 0.5, H, dtype=jnp.float32)
        wave_phase = jnp.linspace(0.0, math.pi, H, dtype=jnp.float32)
        field_coupling = jnp.eye(H, dtype=jnp.float32) + jax.random.normal(ks[2], (H, H), jnp.float32) * 0.01
        Wout = jax.random.normal(ks[3], (D, D), jnp.float32) * 0.02
        bout = jnp.zeros(D, jnp.float32)
        return dict(x=x, Wqkvg=Wqkvg, bqkvg=bqkvg, wave_frequency=wave_frequency, wave_damping=wave_damping, wave_phase=wave_phase, field_coupling=field_coupling, Wout=Wout, bout=bout)
    _L1_attn_in = _L1_attn_setup()

    def _L1_ffn_setup():
        import jax, jax.numpy as jnp
        import numpy as np
        DIM = 128
        DEPTH = 2
        HEADS = 8
        DIM_HEAD = 64
        WINDOW = 64
        INNER = HEADS * DIM_HEAD
        HID = int(DIM * 4 * 2 / 3)
        B, N = (2, 1024)
        QK_SCALE = 8.0

        def shift_token(t):
            t1, t2 = jnp.split(t, 2, axis=-1)
            t2 = jnp.pad(t2, ((0, 0), (1, 0), (0, 0)))[:, :-1]
            return jnp.concatenate([t1, t2], axis=-1)

        def l2norm(t):
            return t / jnp.clip(jnp.linalg.norm(t, axis=-1, keepdims=True), 1e-12)

        def rotate_half(x):
            x1, x2 = jnp.split(x, 2, axis=-1)
            return jnp.concatenate([-x2, x1], axis=-1)

        def rotary_xpos(q, k):
            n = q.shape[-2]
            half_idx = jnp.arange(0, DIM_HEAD, 2, dtype=jnp.float32)
            inv_freq = 1.0 / 10000.0 ** (half_idx / DIM_HEAD)
            t = jnp.arange(n, dtype=jnp.float32)
            freqs = t[:, None] * inv_freq[None, :]
            freqs = jnp.concatenate([freqs, freqs], axis=-1)
            base = (half_idx + 0.4 * DIM_HEAD) / (1.4 * DIM_HEAD)
            power = (t - n // 2) / float(WINDOW // 2)
            scale = base[None, :] ** power[:, None]
            scale = jnp.concatenate([scale, scale], axis=-1)
            cos, sin = (jnp.cos(freqs), jnp.sin(freqs))
            q = q * cos * scale + rotate_half(q) * sin * scale
            k = k * cos / scale + rotate_half(k) * sin / scale
            return (q, k)

        def local_attention(q, k, v):
            b, h, n, d = q.shape
            w = n // WINDOW
            bq = q.reshape(b, h, w, WINDOW, d) * QK_SCALE
            bk = k.reshape(b, h, w, WINDOW, d)
            bv = v.reshape(b, h, w, WINDOW, d)

            def look_around(t):
                p = jnp.pad(t, ((0, 0), (0, 0), (1, 0), (0, 0), (0, 0)))
                return jnp.concatenate([p[:, :, :w], p[:, :, 1:]], axis=3)
            bk, bv = (look_around(bk), look_around(bv))
            bt = jnp.arange(n).reshape(w, WINDOW)
            btp = jnp.pad(bt, ((1, 0), (0, 0)), constant_values=-1)
            btk = jnp.concatenate([btp[:w], btp[1:]], axis=1)
            sim = jnp.einsum('bhwid,bhwjd->bhwij', bq, bk)
            i = bt[:, :, None]
            j = btk[:, None, :]
            mask = (i < j) | (i > j + WINDOW) | (j == -1)
            sim = jnp.where(mask, -jnp.finfo(sim.dtype).max, sim)
            attn = jax.nn.softmax(sim, axis=-1)
            out = jnp.einsum('bhwij,bhwjd->bhwid', attn, bv)
            return out.reshape(b, h, n, d)

        def _layer(x, wqkv, qs, ksc, wo, lg, lb, w1, b1, w2, b2):
            b, n, _ = x.shape
            h = shift_token(x)
            qkv = h @ wqkv
            q, k, v = jnp.split(qkv, 3, axis=-1)
            to_heads = lambda t: t.reshape(b, n, HEADS, DIM_HEAD).transpose(0, 2, 1, 3)
            q, k, v = (to_heads(q), to_heads(k), to_heads(v))
            q = l2norm(q) * qs
            k = l2norm(k) * ksc
            q, k = rotary_xpos(q, k)
            o = local_attention(q, k, v)
            o = o.transpose(0, 2, 1, 3).reshape(b, n, INNER)
            x = x + o @ wo
            h = shift_token(x)
            mu = h.mean(-1, keepdims=True)
            var = h.var(-1, keepdims=True)
            h = (h - mu) / jnp.sqrt(var + 1e-05) * lg + lb
            h = h @ w1 + b1
            a, g = jnp.split(h, 2, axis=-1)
            h = a * jax.nn.gelu(g, approximate=False)
            x = x + h @ w2 + b2
            return x
        key = jax.random.key(seed)
        ks = jax.random.split(key, 6)
        return {'x': jax.random.normal(ks[0], (B, N, DIM), jnp.float32), 'wqkv': jax.random.normal(ks[1], (DEPTH, DIM, 3 * INNER), jnp.float32) * 0.02, 'q_scale': jnp.ones((DEPTH, DIM_HEAD), jnp.float32), 'k_scale': jnp.ones((DEPTH, DIM_HEAD), jnp.float32), 'wo': jax.random.normal(ks[2], (DEPTH, INNER, DIM), jnp.float32) * 0.02, 'ln_g': jnp.ones((DEPTH, DIM), jnp.float32), 'ln_b': jnp.zeros((DEPTH, DIM), jnp.float32), 'w1': jax.random.normal(ks[3], (DEPTH, DIM, 2 * HID), jnp.float32) * 0.02, 'b1': jnp.zeros((DEPTH, 2 * HID), jnp.float32), 'w2': jax.random.normal(ks[4], (DEPTH, HID, DIM), jnp.float32) * 0.02, 'b2': jnp.zeros((DEPTH, DIM), jnp.float32)}
    _L1_ffn_in = _L1_ffn_setup()

    def _L2_attn_setup():
        import jax, jax.numpy as jnp
        import numpy as np
        D_MODEL = 128
        D_STATE = 64
        D_CONV = 4
        EXPAND = 2
        N_HEADS = 16
        D_INNER = D_MODEL * EXPAND
        HEAD_DIM = D_INNER // N_HEADS
        Z_DIM = D_INNER + 2 * D_STATE * N_HEADS + N_HEADS
        RMS_EPS = 1.1920928955078125e-07

        def _ssm_scan(x, dt, B_mat, C_mat, delta_param):
            delta = jax.nn.softplus(dt + delta_param[None, None, :])
            a_bar = jnp.exp(-delta * jnp.abs(dt))
            Bsz, L, nh, dh = x.shape
            ds = B_mat.shape[-1]
            h0 = jnp.zeros((Bsz, nh, dh, ds), dtype=x.dtype)

            def step(h, inp):
                a_t, x_t, b_t, c_t = inp
                h = a_t[:, :, None, None] * h + x_t[..., None] * b_t[:, :, None, :]
                y_t = jnp.einsum('bhds,bhs->bhd', h, c_t)
                return (h, y_t)
            xs = (jnp.moveaxis(a_bar, 1, 0), jnp.moveaxis(x, 1, 0), jnp.moveaxis(B_mat, 1, 0), jnp.moveaxis(C_mat, 1, 0))
            _, ys = jax.lax.scan(step, h0, xs)
            return jnp.moveaxis(ys, 0, 1)

        def _forward(u, W_in, conv_w, conv_b, delta_param, W_gate, norm_w, W_out):
            B, L, _ = u.shape
            z = u @ W_in
            x = z[..., :D_INNER]
            o = D_INNER
            B_mat = z[..., o:o + D_STATE * N_HEADS].reshape(B, L, N_HEADS, D_STATE)
            o += D_STATE * N_HEADS
            C_mat = z[..., o:o + D_STATE * N_HEADS].reshape(B, L, N_HEADS, D_STATE)
            o += D_STATE * N_HEADS
            dt = z[..., o:o + N_HEADS]
            pad = D_CONV - 1
            xp = jnp.pad(x, ((0, 0), (pad, 0), (0, 0)))
            x_conv = conv_b[None, None, :]
            for k in range(D_CONV):
                x_conv = x_conv + xp[:, k:k + L, :] * conv_w[None, None, :, k]
            x = jax.nn.silu(x_conv)
            x_ssm = x.reshape(B, L, N_HEADS, HEAD_DIM)
            y = _ssm_scan(x_ssm, dt, B_mat, C_mat, delta_param)
            y = y.reshape(B, L, D_INNER)
            gate = jax.nn.sigmoid(u @ W_gate)
            y = gate * y
            y = y * jax.lax.rsqrt(jnp.mean(y * y, axis=-1, keepdims=True) + RMS_EPS) * norm_w
            return y @ W_out
        key = jax.random.key(seed)
        ks = jax.random.split(key, 6)
        s = 0.02
        u = jax.random.normal(ks[0], (2, 512, D_MODEL), dtype=jnp.float32)
        W_in = jax.random.normal(ks[1], (D_MODEL, Z_DIM), dtype=jnp.float32) * s
        conv_w = jax.random.normal(ks[2], (D_INNER, D_CONV), dtype=jnp.float32) * s
        conv_b = jnp.zeros((D_INNER,), dtype=jnp.float32)
        delta_param = jnp.zeros((N_HEADS,), dtype=jnp.float32)
        W_gate = jax.random.normal(ks[3], (D_MODEL, D_INNER), dtype=jnp.float32) * s
        norm_w = jnp.ones((D_INNER,), dtype=jnp.float32)
        W_out = jax.random.normal(ks[4], (D_INNER, D_MODEL), dtype=jnp.float32) * s
        return {'u': u, 'W_in': W_in, 'conv_w': conv_w, 'conv_b': conv_b, 'delta_param': delta_param, 'W_gate': W_gate, 'norm_w': norm_w, 'W_out': W_out}
    _L2_attn_in = _L2_attn_setup()

    def _L2_ffn_setup():
        import jax, jax.numpy as jnp
        import numpy as np
        NUM_EXPERTS = 8
        TOP_K = 2
        key = jax.random.key(seed)
        ks = jax.random.split(key, 6)
        B, S, D, F = (2, 256, 128, 512)
        E = NUM_EXPERTS
        sd = 1.0 / np.sqrt(D)
        sf = 1.0 / np.sqrt(F)
        return {'x': jax.random.normal(ks[0], (B, S, D), dtype=jnp.float32), 'gate_w': jax.random.normal(ks[1], (E, D), dtype=jnp.float32) * sd, 'w1': jax.random.uniform(ks[2], (F, E, D), dtype=jnp.float32, minval=-sd, maxval=sd), 'b1': jax.random.uniform(ks[3], (E, F), dtype=jnp.float32, minval=-sd, maxval=sd), 'w2': jax.random.uniform(ks[4], (D, E, F), dtype=jnp.float32, minval=-sf, maxval=sf), 'b2': jax.random.uniform(ks[5], (E, D), dtype=jnp.float32, minval=-sf, maxval=sf)}
    _L2_ffn_in = _L2_ffn_setup()

    def _L3_attn_setup():
        import jax, jax.numpy as jnp
        import numpy as np
        N_EMBD = 128
        EXPAND = 2
        D_INNER = N_EMBD * EXPAND
        D_STATE = 64
        N_HEADS = D_INNER // D_STATE
        HEAD_DIM = D_INNER // N_HEADS
        N_GROUPS = 1
        D_CONV = 4
        N_LAYERS = 48
        BATCH, SEQ = (1, 64)
        PROJ_SIZE = 2 * D_INNER + N_HEADS + 2 * N_GROUPS * D_STATE
        EPS = 1e-06

        def _mamba_fwd(x, norm_scale, w_in, conv_weight, conv_bias, A_log, dt_bias, w_out):
            b, T, _ = x.shape
            residual = x
            xn = x * jax.lax.rsqrt(jnp.mean(x * x, axis=-1, keepdims=True) + EPS) * norm_scale
            proj = xn @ w_in
            gate = proj[..., :D_INNER]
            ssm_in = proj[..., D_INNER:2 * D_INNER]
            dt_raw = proj[..., 2 * D_INNER:2 * D_INNER + N_HEADS]
            gs = N_GROUPS * D_STATE
            B = proj[..., 2 * D_INNER + N_HEADS:2 * D_INNER + N_HEADS + gs].reshape(b, T, N_GROUPS, D_STATE)
            C = proj[..., 2 * D_INNER + N_HEADS + gs:].reshape(b, T, N_GROUPS, D_STATE)
            xp = jnp.pad(ssm_in, ((0, 0), (D_CONV - 1, 0), (0, 0)))
            conv = conv_bias + sum((conv_weight[k] * xp[:, k:k + T, :] for k in range(D_CONV)))
            h = jax.nn.silu(conv)
            dt = jax.nn.softplus(dt_raw + dt_bias)
            A = -jnp.exp(A_log)
            A_bar = jnp.exp(A[None, None, :] * dt)
            hpg = N_HEADS // N_GROUPS
            xh = h.reshape(b, T, N_HEADS, HEAD_DIM)
            Bh = jnp.repeat(B, hpg, axis=2)
            Ch = jnp.repeat(C, hpg, axis=2)
            Bu = Bh[:, :, :, None, :] * (dt[..., None, None] * xh[..., None])

            def _binary_op(left, right):
                a_l, b_l = left
                a_r, b_r = right
                return (a_l * a_r, a_r * b_l + b_r)
            _, states = jax.lax.associative_scan(_binary_op, (A_bar[..., None, None], Bu), axis=1)
            y = jnp.einsum('bthpn,bthn->bthp', states, Ch).reshape(b, T, D_INNER)
            y = y * jax.nn.silu(gate)
            y = y @ w_out
            return residual + y
        key = jax.random.key(seed)
        ks = jax.random.split(key, 6)
        init_std = 0.02
        proj_std = 0.02 / np.sqrt(2 * N_LAYERS)
        return {'x': jax.random.normal(ks[0], (BATCH, SEQ, N_EMBD), jnp.float32), 'norm_scale': jnp.ones((N_EMBD,), jnp.float32), 'w_in': jax.random.normal(ks[1], (N_EMBD, PROJ_SIZE), jnp.float32) * init_std, 'conv_weight': jax.random.normal(ks[2], (D_CONV, D_INNER), jnp.float32) * 0.02, 'conv_bias': jnp.zeros((D_INNER,), jnp.float32), 'A_log': jnp.log(0.5 + jnp.arange(N_HEADS, dtype=jnp.float32) * 0.5 / N_HEADS), 'dt_bias': jax.random.normal(ks[3], (N_HEADS,), jnp.float32) * 0.1, 'w_out': jax.random.normal(ks[4], (D_INNER, N_EMBD), jnp.float32) * proj_std}
    _L3_attn_in = _L3_attn_setup()

    def _L3_ffn_setup():
        import jax, jax.numpy as jnp
        import numpy as np
        NH, NKV, E, K = (16, 4, 8, 2)
        CAP_FACTOR = 1.25
        LN_EPS = 1e-05

        def _layer_norm(x, w, b):
            mu = jnp.mean(x, axis=-1, keepdims=True)
            var = jnp.mean(jnp.square(x - mu), axis=-1, keepdims=True)
            return (x - mu) * jax.lax.rsqrt(var + LN_EPS) * w + b
        key = jax.random.key(seed)
        ks = jax.random.split(key, 6)
        S, B, H, F = (256, 1, 128, 256)
        HD = H // NH
        qkv_out = NKV * (NH // NKV + 2) * HD
        f32 = jnp.float32
        return {'hidden_states': jax.random.normal(ks[0], (S, B, H), f32), 'ln1_weight': jnp.ones((H,), f32), 'ln1_bias': jnp.zeros((H,), f32), 'ln2_weight': jnp.ones((H,), f32), 'ln2_bias': jnp.zeros((H,), f32), 'qkv_weight': jax.random.normal(ks[1], (qkv_out, H), f32) * 0.02, 'proj_weight': jax.random.normal(ks[2], (H, H), f32) * 0.02, 'router_weight': jax.random.normal(ks[3], (H, E), f32) * 0.02, 'moe_w1': jax.random.normal(ks[4], (E, H, F), f32) * 0.02, 'moe_w2': jax.random.normal(ks[5], (F and E, F, H), f32)[:E] * 0.02 if False else jax.random.normal(ks[5], (E, F, H), f32) * 0.02}
    _L3_ffn_in = _L3_ffn_setup()
    _d = {'L0_attn_x': _L0_attn_in['x'], 'L0_attn_v_first': _L0_attn_in['v_first'], 'L0_attn_ln_pre_w': _L0_attn_in['ln_pre_w'], 'L0_attn_ln_pre_b': _L0_attn_in['ln_pre_b'], 'L0_attn_ln_attn_w': _L0_attn_in['ln_attn_w'], 'L0_attn_ln_attn_b': _L0_attn_in['ln_attn_b'], 'L0_attn_ln_ffn_w': _L0_attn_in['ln_ffn_w'], 'L0_attn_ln_ffn_b': _L0_attn_in['ln_ffn_b'], 'L0_attn_x_r': _L0_attn_in['x_r'], 'L0_attn_x_w': _L0_attn_in['x_w'], 'L0_attn_x_k': _L0_attn_in['x_k'], 'L0_attn_x_v': _L0_attn_in['x_v'], 'L0_attn_x_a': _L0_attn_in['x_a'], 'L0_attn_x_g': _L0_attn_in['x_g'], 'L0_attn_w0': _L0_attn_in['w0'], 'L0_attn_w1': _L0_attn_in['w1'], 'L0_attn_w2': _L0_attn_in['w2'], 'L0_attn_a0': _L0_attn_in['a0'], 'L0_attn_a1': _L0_attn_in['a1'], 'L0_attn_a2': _L0_attn_in['a2'], 'L0_attn_g1': _L0_attn_in['g1'], 'L0_attn_g2': _L0_attn_in['g2'], 'L0_attn_k_k': _L0_attn_in['k_k'], 'L0_attn_k_a': _L0_attn_in['k_a'], 'L0_attn_r_k': _L0_attn_in['r_k'], 'L0_attn_W_r': _L0_attn_in['W_r'], 'L0_attn_W_k': _L0_attn_in['W_k'], 'L0_attn_W_v': _L0_attn_in['W_v'], 'L0_attn_W_o': _L0_attn_in['W_o'], 'L0_attn_gn_w': _L0_attn_in['gn_w'], 'L0_attn_gn_b': _L0_attn_in['gn_b'], 'L0_attn_ffn_x_k': _L0_attn_in['ffn_x_k'], 'L0_attn_W_ffn1': _L0_attn_in['W_ffn1'], 'L0_attn_W_ffn2': _L0_attn_in['W_ffn2'], 'L0_ffn_shared_w1': _L0_ffn_in['shared_w1'], 'L0_ffn_shared_b1': _L0_ffn_in['shared_b1'], 'L0_ffn_shared_w2': _L0_ffn_in['shared_w2'], 'L0_ffn_shared_b2': _L0_ffn_in['shared_b2'], 'L0_ffn_router_w': _L0_ffn_in['router_w'], 'L0_ffn_router_b': _L0_ffn_in['router_b'], 'L0_ffn_spec_w1': _L0_ffn_in['spec_w1'], 'L0_ffn_spec_b1': _L0_ffn_in['spec_b1'], 'L0_ffn_spec_w2': _L0_ffn_in['spec_w2'], 'L0_ffn_spec_b2': _L0_ffn_in['spec_b2'], 'L1_attn_Wqkvg': _L1_attn_in['Wqkvg'], 'L1_attn_bqkvg': _L1_attn_in['bqkvg'], 'L1_attn_wave_frequency': _L1_attn_in['wave_frequency'], 'L1_attn_wave_damping': _L1_attn_in['wave_damping'], 'L1_attn_wave_phase': _L1_attn_in['wave_phase'], 'L1_attn_field_coupling': _L1_attn_in['field_coupling'], 'L1_attn_Wout': _L1_attn_in['Wout'], 'L1_attn_bout': _L1_attn_in['bout'], 'L1_ffn_wqkv': _L1_ffn_in['wqkv'], 'L1_ffn_q_scale': _L1_ffn_in['q_scale'], 'L1_ffn_k_scale': _L1_ffn_in['k_scale'], 'L1_ffn_wo': _L1_ffn_in['wo'], 'L1_ffn_ln_g': _L1_ffn_in['ln_g'], 'L1_ffn_ln_b': _L1_ffn_in['ln_b'], 'L1_ffn_w1': _L1_ffn_in['w1'], 'L1_ffn_b1': _L1_ffn_in['b1'], 'L1_ffn_w2': _L1_ffn_in['w2'], 'L1_ffn_b2': _L1_ffn_in['b2'], 'L2_attn_W_in': _L2_attn_in['W_in'], 'L2_attn_conv_w': _L2_attn_in['conv_w'], 'L2_attn_conv_b': _L2_attn_in['conv_b'], 'L2_attn_delta_param': _L2_attn_in['delta_param'], 'L2_attn_W_gate': _L2_attn_in['W_gate'], 'L2_attn_norm_w': _L2_attn_in['norm_w'], 'L2_attn_W_out': _L2_attn_in['W_out'], 'L2_ffn_gate_w': _L2_ffn_in['gate_w'], 'L2_ffn_w1': _L2_ffn_in['w1'], 'L2_ffn_b1': _L2_ffn_in['b1'], 'L2_ffn_w2': _L2_ffn_in['w2'], 'L2_ffn_b2': _L2_ffn_in['b2'], 'L3_attn_norm_scale': _L3_attn_in['norm_scale'], 'L3_attn_w_in': _L3_attn_in['w_in'], 'L3_attn_conv_weight': _L3_attn_in['conv_weight'], 'L3_attn_conv_bias': _L3_attn_in['conv_bias'], 'L3_attn_A_log': _L3_attn_in['A_log'], 'L3_attn_dt_bias': _L3_attn_in['dt_bias'], 'L3_attn_w_out': _L3_attn_in['w_out'], 'L3_ffn_ln1_weight': _L3_ffn_in['ln1_weight'], 'L3_ffn_ln1_bias': _L3_ffn_in['ln1_bias'], 'L3_ffn_ln2_weight': _L3_ffn_in['ln2_weight'], 'L3_ffn_ln2_bias': _L3_ffn_in['ln2_bias'], 'L3_ffn_qkv_weight': _L3_ffn_in['qkv_weight'], 'L3_ffn_proj_weight': _L3_ffn_in['proj_weight'], 'L3_ffn_router_weight': _L3_ffn_in['router_weight'], 'L3_ffn_moe_w1': _L3_ffn_in['moe_w1'], 'L3_ffn_moe_w2': _L3_ffn_in['moe_w2']}
    _x0 = _d['L0_attn_x']
    _d['L0_attn_x'] = jax.random.normal(jax.random.fold_in(jax.random.key(seed), 1), (16, 256, 128), dtype=_x0.dtype)
    del _x0
    return _d

def reference(L0_attn_x, L0_attn_v_first, L0_attn_ln_pre_w, L0_attn_ln_pre_b, L0_attn_ln_attn_w, L0_attn_ln_attn_b, L0_attn_ln_ffn_w, L0_attn_ln_ffn_b, L0_attn_x_r, L0_attn_x_w, L0_attn_x_k, L0_attn_x_v, L0_attn_x_a, L0_attn_x_g, L0_attn_w0, L0_attn_w1, L0_attn_w2, L0_attn_a0, L0_attn_a1, L0_attn_a2, L0_attn_g1, L0_attn_g2, L0_attn_k_k, L0_attn_k_a, L0_attn_r_k, L0_attn_W_r, L0_attn_W_k, L0_attn_W_v, L0_attn_W_o, L0_attn_gn_w, L0_attn_gn_b, L0_attn_ffn_x_k, L0_attn_W_ffn1, L0_attn_W_ffn2, L0_ffn_shared_w1, L0_ffn_shared_b1, L0_ffn_shared_w2, L0_ffn_shared_b2, L0_ffn_router_w, L0_ffn_router_b, L0_ffn_spec_w1, L0_ffn_spec_b1, L0_ffn_spec_w2, L0_ffn_spec_b2, L1_attn_Wqkvg, L1_attn_bqkvg, L1_attn_wave_frequency, L1_attn_wave_damping, L1_attn_wave_phase, L1_attn_field_coupling, L1_attn_Wout, L1_attn_bout, L1_ffn_wqkv, L1_ffn_q_scale, L1_ffn_k_scale, L1_ffn_wo, L1_ffn_ln_g, L1_ffn_ln_b, L1_ffn_w1, L1_ffn_b1, L1_ffn_w2, L1_ffn_b2, L2_attn_W_in, L2_attn_conv_w, L2_attn_conv_b, L2_attn_delta_param, L2_attn_W_gate, L2_attn_norm_w, L2_attn_W_out, L2_ffn_gate_w, L2_ffn_w1, L2_ffn_b1, L2_ffn_w2, L2_ffn_b2, L3_attn_norm_scale, L3_attn_w_in, L3_attn_conv_weight, L3_attn_conv_bias, L3_attn_A_log, L3_attn_dt_bias, L3_attn_w_out, L3_ffn_ln1_weight, L3_ffn_ln1_bias, L3_ffn_ln2_weight, L3_ffn_ln2_bias, L3_ffn_qkv_weight, L3_ffn_proj_weight, L3_ffn_router_weight, L3_ffn_moe_w1, L3_ffn_moe_w2):

    def _L0_attn_ref(x, v_first, ln_pre_w, ln_pre_b, ln_attn_w, ln_attn_b, ln_ffn_w, ln_ffn_b, x_r, x_w, x_k, x_v, x_a, x_g, w0, w1, w2, a0, a1, a2, g1, g2, k_k, k_a, r_k, W_r, W_k, W_v, W_o, gn_w, gn_b, ffn_x_k, W_ffn1, W_ffn2):
        import jax, jax.numpy as jnp
        import numpy as np
        B, T, C, H = (8, 64, 128, 16)
        N = C // H
        DW, DA, DG = (64, 64, 128)

        def _ln(x, w, b, eps=1e-05):
            mu = x.mean(-1, keepdims=True)
            var = ((x - mu) ** 2).mean(-1, keepdims=True)
            return (x - mu) * jax.lax.rsqrt(var + eps) * w + b

        def _gn_heads(x, w, b, eps=0.00064):
            xh = x.reshape(x.shape[0], x.shape[1], H, N)
            mu = xh.mean(-1, keepdims=True)
            var = ((xh - mu) ** 2).mean(-1, keepdims=True)
            xh = (xh - mu) * jax.lax.rsqrt(var + eps)
            return xh.reshape(x.shape) * w + b

        def _shift(x):
            return jnp.concatenate([jnp.zeros_like(x[:, :1]), x[:, :-1]], axis=1)

        def _wkv7(r, w_log, k, v, a, b):
            decay = jnp.exp(-jnp.exp(w_log))

            def step(state, inp):
                r_t, d_t, k_t, v_t, a_t, b_t = inp
                sa = jnp.einsum('bhij,bhj->bhi', state, a_t)
                state = state * d_t[:, :, None, :] + sa[..., None] * b_t[:, :, None, :] + v_t[..., None] * k_t[:, :, None, :]
                return (state, jnp.einsum('bhij,bhj->bhi', state, r_t))
            xs = tuple((jnp.moveaxis(t, 1, 0) for t in (r, decay, k, v, a, b)))
            s0 = jnp.zeros((r.shape[0], H, N, N), r.dtype)
            _, out = jax.lax.scan(step, s0, xs)
            return jnp.moveaxis(out, 0, 1)

        def _reference_tuple_inner(x, v_first, ln_pre_w, ln_pre_b, ln_attn_w, ln_attn_b, ln_ffn_w, ln_ffn_b, x_r, x_w, x_k, x_v, x_a, x_g, w0, w1, w2, a0, a1, a2, g1, g2, k_k, k_a, r_k, W_r, W_k, W_v, W_o, gn_w, gn_b, ffn_x_k, W_ffn1, W_ffn2):
            Bx, Tx = (x.shape[0], x.shape[1])
            x = _ln(x, ln_pre_w, ln_pre_b)
            xn = _ln(x, ln_attn_w, ln_attn_b)
            dx = _shift(xn) - xn
            xr = xn + dx * x_r
            xw = xn + dx * x_w
            xk = xn + dx * x_k
            xv = xn + dx * x_v
            xa = xn + dx * x_a
            xg = xn + dx * x_g
            r = xr @ W_r
            w_log = -jax.nn.softplus(-(w0 + jnp.tanh(xw @ w1) @ w2)) - 0.5
            k = xk @ W_k
            v = xv @ W_v
            v_first = v
            a = jax.nn.sigmoid(a0 + xa @ a1 @ a2)
            g = jax.nn.sigmoid(xg @ g1) @ g2
            kk = (k * k_k).reshape(Bx, Tx, H, N)
            kk = kk / jnp.maximum(jnp.linalg.norm(kk, axis=-1, keepdims=True), 1e-12)
            k = k * (1.0 + (a - 1.0) * k_a)
            rh = r.reshape(Bx, Tx, H, N)
            kh = k.reshape(Bx, Tx, H, N)
            vh = v.reshape(Bx, Tx, H, N)
            ah = a.reshape(Bx, Tx, H, N)
            o = _wkv7(rh, w_log.reshape(Bx, Tx, H, N), kh, vh, -kk, kk * ah)
            o = _gn_heads(o.reshape(Bx, Tx, C), gn_w, gn_b)
            o = o + ((rh * kh * r_k).sum(-1, keepdims=True) * vh).reshape(Bx, Tx, C)
            x = x + o * g @ W_o
            xf = _ln(x, ln_ffn_w, ln_ffn_b)
            kf = xf + (_shift(xf) - xf) * ffn_x_k
            x = x + jnp.square(jax.nn.relu(kf @ W_ffn1)) @ W_ffn2
            return (x, v_first)
        return _reference_tuple_inner(x, v_first, ln_pre_w, ln_pre_b, ln_attn_w, ln_attn_b, ln_ffn_w, ln_ffn_b, x_r, x_w, x_k, x_v, x_a, x_g, w0, w1, w2, a0, a1, a2, g1, g2, k_k, k_a, r_k, W_r, W_k, W_v, W_o, gn_w, gn_b, ffn_x_k, W_ffn1, W_ffn2)[0]

    def _L0_ffn_ref(x, shared_w1, shared_b1, shared_w2, shared_b2, router_w, router_b, spec_w1, spec_b1, spec_w2, spec_b2):
        import jax, jax.numpy as jnp
        import numpy as np
        D_MODEL = 128
        D_FF = 512
        N_EXPERTS = 8
        TOP_K = 2

        def _ffn(x, w1, b1, w2, b2):
            h = jax.nn.gelu(x @ w1.T + b1)
            return h @ w2.T + b2
        B, T, D = x.shape
        xf = x.reshape(-1, D)
        U = xf.shape[0]
        logits = xf @ router_w.T + router_b
        routing = jax.nn.softmax(logits, axis=-1)
        sel_w, sel_idx = jax.lax.top_k(routing, TOP_K)
        sel_w = sel_w / sel_w.sum(axis=-1, keepdims=True)
        comb = jnp.zeros_like(routing).at[jnp.arange(U)[:, None], sel_idx].set(sel_w)
        shared_out = _ffn(xf, shared_w1, shared_b1, shared_w2, shared_b2)

        def body(acc, params):
            w1, b1, w2, b2, we = params
            return (acc + we[:, None] * _ffn(xf, w1, b1, w2, b2), None)
        acc0 = jnp.zeros_like(shared_out)
        acc, _ = jax.lax.scan(body, acc0, (spec_w1, spec_b1, spec_w2, spec_b2, comb.T))
        return (shared_out + acc).reshape(B, T, D)

    def _L1_attn_ref(x, Wqkvg, bqkvg, wave_frequency, wave_damping, wave_phase, field_coupling, Wout, bout):
        import jax, jax.numpy as jnp
        import numpy as np
        import math
        B, N, D, H, G = (4, 256, 128, 16, 256)
        HD = D // H
        MAX_SEQ = 256
        STRIDE = (G - 1) / max(MAX_SEQ - 1, 1)

        def _forward(x, Wqkvg, bqkvg, wave_frequency, wave_damping, wave_phase, field_coupling, Wout, bout):
            b, n, d = x.shape
            qkvg = x @ Wqkvg.T + bqkvg
            q, k, v, gate_raw = jnp.split(qkvg, 4, axis=-1)
            to_heads = lambda t: t.reshape(b, n, H, HD).transpose(0, 2, 1, 3)
            q, k, v = (to_heads(q), to_heads(k), to_heads(v))
            seq_pos = jnp.arange(n, dtype=jnp.float32)
            field_pos = jnp.clip(seq_pos * STRIDE, 0.0, G - 2)
            idx_lo = jnp.clip(field_pos.astype(jnp.int32), 0, G - 2)
            idx_hi = idx_lo + 1
            frac = jnp.clip(field_pos - idx_lo.astype(jnp.float32), 0.0, 1.0)
            w_lo = (1.0 - frac)[None, None, :, None]
            w_hi = frac[None, None, :, None]
            q_feat = jax.nn.elu(q) + 1.0
            k_feat = jax.nn.elu(k) + 1.0
            deposit = k_feat * v
            field = jnp.zeros((b, H, G, HD), deposit.dtype)
            field = field.at[:, :, idx_lo, :].add(deposit * w_lo)
            field = field.at[:, :, idx_hi, :].add(deposit * w_hi)
            t = jnp.arange(G, dtype=jnp.float32)
            alpha = jax.nn.softplus(wave_damping)[:, None]
            omega = wave_frequency[:, None]
            phi = wave_phase[:, None]
            kernels = jnp.exp(-alpha * t[None, :]) * jnp.cos(omega * t[None, :] + phi)
            kernels = kernels / jnp.clip(jnp.sum(jnp.abs(kernels), axis=1, keepdims=True), 1e-08)
            kernel_fft = jnp.fft.rfft(kernels, n=2 * G, axis=-1)
            field_fft = jnp.fft.rfft(field, n=2 * G, axis=2)
            convolved = jnp.fft.irfft(field_fft * kernel_fft[None, :, :, None], n=2 * G, axis=2)[:, :, :G, :]
            coupling = jax.nn.softmax(field_coupling, axis=-1)
            field_c = jnp.einsum('ij,bjgd->bigd', coupling, convolved)
            gathered = field_c[:, :, idx_lo, :] * w_lo + field_c[:, :, idx_hi, :] * w_hi
            wave_output = q_feat * gathered
            gate = jax.nn.sigmoid(gate_raw).reshape(b, n, H, HD).transpose(0, 2, 1, 3)
            output = (wave_output * gate).transpose(0, 2, 1, 3).reshape(b, n, d)
            return output @ Wout.T + bout
        return _forward(x, Wqkvg, bqkvg, wave_frequency, wave_damping, wave_phase, field_coupling, Wout, bout)

    def _L1_ffn_ref(x, wqkv, q_scale, k_scale, wo, ln_g, ln_b, w1, b1, w2, b2):
        import jax, jax.numpy as jnp
        import numpy as np
        DIM = 128
        DEPTH = 2
        HEADS = 8
        DIM_HEAD = 64
        WINDOW = 64
        INNER = HEADS * DIM_HEAD
        HID = int(DIM * 4 * 2 / 3)
        B, N = (2, 1024)
        QK_SCALE = 8.0

        def shift_token(t):
            t1, t2 = jnp.split(t, 2, axis=-1)
            t2 = jnp.pad(t2, ((0, 0), (1, 0), (0, 0)))[:, :-1]
            return jnp.concatenate([t1, t2], axis=-1)

        def l2norm(t):
            return t / jnp.clip(jnp.linalg.norm(t, axis=-1, keepdims=True), 1e-12)

        def rotate_half(x):
            x1, x2 = jnp.split(x, 2, axis=-1)
            return jnp.concatenate([-x2, x1], axis=-1)

        def rotary_xpos(q, k):
            n = q.shape[-2]
            half_idx = jnp.arange(0, DIM_HEAD, 2, dtype=jnp.float32)
            inv_freq = 1.0 / 10000.0 ** (half_idx / DIM_HEAD)
            t = jnp.arange(n, dtype=jnp.float32)
            freqs = t[:, None] * inv_freq[None, :]
            freqs = jnp.concatenate([freqs, freqs], axis=-1)
            base = (half_idx + 0.4 * DIM_HEAD) / (1.4 * DIM_HEAD)
            power = (t - n // 2) / float(WINDOW // 2)
            scale = base[None, :] ** power[:, None]
            scale = jnp.concatenate([scale, scale], axis=-1)
            cos, sin = (jnp.cos(freqs), jnp.sin(freqs))
            q = q * cos * scale + rotate_half(q) * sin * scale
            k = k * cos / scale + rotate_half(k) * sin / scale
            return (q, k)

        def local_attention(q, k, v):
            b, h, n, d = q.shape
            w = n // WINDOW
            bq = q.reshape(b, h, w, WINDOW, d) * QK_SCALE
            bk = k.reshape(b, h, w, WINDOW, d)
            bv = v.reshape(b, h, w, WINDOW, d)

            def look_around(t):
                p = jnp.pad(t, ((0, 0), (0, 0), (1, 0), (0, 0), (0, 0)))
                return jnp.concatenate([p[:, :, :w], p[:, :, 1:]], axis=3)
            bk, bv = (look_around(bk), look_around(bv))
            bt = jnp.arange(n).reshape(w, WINDOW)
            btp = jnp.pad(bt, ((1, 0), (0, 0)), constant_values=-1)
            btk = jnp.concatenate([btp[:w], btp[1:]], axis=1)
            sim = jnp.einsum('bhwid,bhwjd->bhwij', bq, bk)
            i = bt[:, :, None]
            j = btk[:, None, :]
            mask = (i < j) | (i > j + WINDOW) | (j == -1)
            sim = jnp.where(mask, -jnp.finfo(sim.dtype).max, sim)
            attn = jax.nn.softmax(sim, axis=-1)
            out = jnp.einsum('bhwij,bhwjd->bhwid', attn, bv)
            return out.reshape(b, h, n, d)

        def _layer(x, wqkv, qs, ksc, wo, lg, lb, w1, b1, w2, b2):
            b, n, _ = x.shape
            h = shift_token(x)
            qkv = h @ wqkv
            q, k, v = jnp.split(qkv, 3, axis=-1)
            to_heads = lambda t: t.reshape(b, n, HEADS, DIM_HEAD).transpose(0, 2, 1, 3)
            q, k, v = (to_heads(q), to_heads(k), to_heads(v))
            q = l2norm(q) * qs
            k = l2norm(k) * ksc
            q, k = rotary_xpos(q, k)
            o = local_attention(q, k, v)
            o = o.transpose(0, 2, 1, 3).reshape(b, n, INNER)
            x = x + o @ wo
            h = shift_token(x)
            mu = h.mean(-1, keepdims=True)
            var = h.var(-1, keepdims=True)
            h = (h - mu) / jnp.sqrt(var + 1e-05) * lg + lb
            h = h @ w1 + b1
            a, g = jnp.split(h, 2, axis=-1)
            h = a * jax.nn.gelu(g, approximate=False)
            x = x + h @ w2 + b2
            return x
        for l in range(DEPTH):
            x = _layer(x, wqkv[l], q_scale[l], k_scale[l], wo[l], ln_g[l], ln_b[l], w1[l], b1[l], w2[l], b2[l])
        return x

    def _L2_attn_ref(u, W_in, conv_w, conv_b, delta_param, W_gate, norm_w, W_out):
        import jax, jax.numpy as jnp
        import numpy as np
        D_MODEL = 128
        D_STATE = 64
        D_CONV = 4
        EXPAND = 2
        N_HEADS = 16
        D_INNER = D_MODEL * EXPAND
        HEAD_DIM = D_INNER // N_HEADS
        Z_DIM = D_INNER + 2 * D_STATE * N_HEADS + N_HEADS
        RMS_EPS = 1.1920928955078125e-07

        def _ssm_scan(x, dt, B_mat, C_mat, delta_param):
            delta = jax.nn.softplus(dt + delta_param[None, None, :])
            a_bar = jnp.exp(-delta * jnp.abs(dt))
            Bsz, L, nh, dh = x.shape
            ds = B_mat.shape[-1]
            h0 = jnp.zeros((Bsz, nh, dh, ds), dtype=x.dtype)

            def step(h, inp):
                a_t, x_t, b_t, c_t = inp
                h = a_t[:, :, None, None] * h + x_t[..., None] * b_t[:, :, None, :]
                y_t = jnp.einsum('bhds,bhs->bhd', h, c_t)
                return (h, y_t)
            xs = (jnp.moveaxis(a_bar, 1, 0), jnp.moveaxis(x, 1, 0), jnp.moveaxis(B_mat, 1, 0), jnp.moveaxis(C_mat, 1, 0))
            _, ys = jax.lax.scan(step, h0, xs)
            return jnp.moveaxis(ys, 0, 1)

        def _forward(u, W_in, conv_w, conv_b, delta_param, W_gate, norm_w, W_out):
            B, L, _ = u.shape
            z = u @ W_in
            x = z[..., :D_INNER]
            o = D_INNER
            B_mat = z[..., o:o + D_STATE * N_HEADS].reshape(B, L, N_HEADS, D_STATE)
            o += D_STATE * N_HEADS
            C_mat = z[..., o:o + D_STATE * N_HEADS].reshape(B, L, N_HEADS, D_STATE)
            o += D_STATE * N_HEADS
            dt = z[..., o:o + N_HEADS]
            pad = D_CONV - 1
            xp = jnp.pad(x, ((0, 0), (pad, 0), (0, 0)))
            x_conv = conv_b[None, None, :]
            for k in range(D_CONV):
                x_conv = x_conv + xp[:, k:k + L, :] * conv_w[None, None, :, k]
            x = jax.nn.silu(x_conv)
            x_ssm = x.reshape(B, L, N_HEADS, HEAD_DIM)
            y = _ssm_scan(x_ssm, dt, B_mat, C_mat, delta_param)
            y = y.reshape(B, L, D_INNER)
            gate = jax.nn.sigmoid(u @ W_gate)
            y = gate * y
            y = y * jax.lax.rsqrt(jnp.mean(y * y, axis=-1, keepdims=True) + RMS_EPS) * norm_w
            return y @ W_out
        return _forward(u, W_in, conv_w, conv_b, delta_param, W_gate, norm_w, W_out)

    def _L2_ffn_ref(x, gate_w, w1, b1, w2, b2):
        import jax, jax.numpy as jnp
        import numpy as np
        NUM_EXPERTS = 8
        TOP_K = 2
        logits = jnp.einsum('bsd,ed->bse', x, gate_w)
        probs = jax.nn.softmax(logits, axis=-1)
        topk_probs, topk_idx = jax.lax.top_k(probs, TOP_K)
        oh = jax.nn.one_hot(topk_idx, NUM_EXPERTS, dtype=x.dtype)
        h = jnp.einsum('bsd,fed,bske->bskf', x, w1, oh)
        h = h + jnp.take(b1, topk_idx, axis=0)
        h = jax.nn.gelu(h)
        y = jnp.einsum('bskf,def,bske->bskd', h, w2, oh)
        y = y + jnp.take(b2, topk_idx, axis=0)
        out = jnp.sum(y * topk_probs[..., None], axis=-2)
        return out

    def _L3_attn_ref(x, norm_scale, w_in, conv_weight, conv_bias, A_log, dt_bias, w_out):
        import jax, jax.numpy as jnp
        import numpy as np
        N_EMBD = 128
        EXPAND = 2
        D_INNER = N_EMBD * EXPAND
        D_STATE = 64
        N_HEADS = D_INNER // D_STATE
        HEAD_DIM = D_INNER // N_HEADS
        N_GROUPS = 1
        D_CONV = 4
        N_LAYERS = 48
        BATCH, SEQ = (1, 64)
        PROJ_SIZE = 2 * D_INNER + N_HEADS + 2 * N_GROUPS * D_STATE
        EPS = 1e-06

        def _mamba_fwd(x, norm_scale, w_in, conv_weight, conv_bias, A_log, dt_bias, w_out):
            b, T, _ = x.shape
            residual = x
            xn = x * jax.lax.rsqrt(jnp.mean(x * x, axis=-1, keepdims=True) + EPS) * norm_scale
            proj = xn @ w_in
            gate = proj[..., :D_INNER]
            ssm_in = proj[..., D_INNER:2 * D_INNER]
            dt_raw = proj[..., 2 * D_INNER:2 * D_INNER + N_HEADS]
            gs = N_GROUPS * D_STATE
            B = proj[..., 2 * D_INNER + N_HEADS:2 * D_INNER + N_HEADS + gs].reshape(b, T, N_GROUPS, D_STATE)
            C = proj[..., 2 * D_INNER + N_HEADS + gs:].reshape(b, T, N_GROUPS, D_STATE)
            xp = jnp.pad(ssm_in, ((0, 0), (D_CONV - 1, 0), (0, 0)))
            conv = conv_bias + sum((conv_weight[k] * xp[:, k:k + T, :] for k in range(D_CONV)))
            h = jax.nn.silu(conv)
            dt = jax.nn.softplus(dt_raw + dt_bias)
            A = -jnp.exp(A_log)
            A_bar = jnp.exp(A[None, None, :] * dt)
            hpg = N_HEADS // N_GROUPS
            xh = h.reshape(b, T, N_HEADS, HEAD_DIM)
            Bh = jnp.repeat(B, hpg, axis=2)
            Ch = jnp.repeat(C, hpg, axis=2)
            Bu = Bh[:, :, :, None, :] * (dt[..., None, None] * xh[..., None])

            def _binary_op(left, right):
                a_l, b_l = left
                a_r, b_r = right
                return (a_l * a_r, a_r * b_l + b_r)
            _, states = jax.lax.associative_scan(_binary_op, (A_bar[..., None, None], Bu), axis=1)
            y = jnp.einsum('bthpn,bthn->bthp', states, Ch).reshape(b, T, D_INNER)
            y = y * jax.nn.silu(gate)
            y = y @ w_out
            return residual + y
        return _mamba_fwd(x, norm_scale, w_in, conv_weight, conv_bias, A_log, dt_bias, w_out)

    def _L3_ffn_ref(hidden_states, ln1_weight, ln1_bias, ln2_weight, ln2_bias, qkv_weight, proj_weight, router_weight, moe_w1, moe_w2):
        import jax, jax.numpy as jnp
        import numpy as np
        NH, NKV, E, K = (16, 4, 8, 2)
        CAP_FACTOR = 1.25
        LN_EPS = 1e-05

        def _layer_norm(x, w, b):
            mu = jnp.mean(x, axis=-1, keepdims=True)
            var = jnp.mean(jnp.square(x - mu), axis=-1, keepdims=True)
            return (x - mu) * jax.lax.rsqrt(var + LN_EPS) * w + b
        S, B, H = hidden_states.shape
        HD = H // NH
        q_per_kv = NH // NKV
        ln1 = _layer_norm(hidden_states, ln1_weight, ln1_bias)
        qkv = jnp.einsum('sbh,oh->sbo', ln1, qkv_weight)
        qkv = qkv.reshape(S, B, NKV, (q_per_kv + 2) * HD)
        q = qkv[..., :q_per_kv * HD].reshape(S, B, NH, HD)
        k = qkv[..., q_per_kv * HD:(q_per_kv + 1) * HD]
        v = qkv[..., (q_per_kv + 1) * HD:]
        qb = jnp.transpose(q, (1, 2, 0, 3)).reshape(B, NKV, q_per_kv, S, HD)
        kb = jnp.transpose(k, (1, 2, 0, 3))
        vb = jnp.transpose(v, (1, 2, 0, 3))
        scale = 1.0 / np.sqrt(HD).astype(np.float32)
        scores = jnp.einsum('bgqsd,bgtd->bgqst', qb, kb) * scale
        causal = jnp.tril(jnp.ones((S, S), bool))
        scores = jnp.where(causal, scores, jnp.finfo(scores.dtype).min)
        attn = jax.nn.softmax(scores, axis=-1)
        ao = jnp.einsum('bgqst,bgtd->bgqsd', attn, vb)
        ao = ao.reshape(B, NH, S, HD)
        ao = jnp.transpose(ao, (2, 0, 1, 3)).reshape(S, B, H)
        proj = jnp.einsum('sbh,oh->sbo', ao, proj_weight)
        h1 = hidden_states + proj
        ln2 = _layer_norm(h1, ln2_weight, ln2_bias)
        x = ln2.reshape(-1, H)
        N = x.shape[0]
        logits = x @ router_weight
        probs = jax.nn.softmax(logits, axis=-1)
        top_p, top_i = jax.lax.top_k(probs, K)
        top_p = top_p / jnp.sum(top_p, axis=-1, keepdims=True)
        exp_idx = top_i.reshape(-1)
        exp_p = top_p.reshape(-1)
        order = jnp.argsort(exp_idx, stable=True)
        sorted_exp = exp_idx[order]
        counts = jnp.bincount(exp_idx, length=E)
        offsets = jnp.concatenate([jnp.zeros((1,), counts.dtype), jnp.cumsum(counts)[:-1]])
        within = jnp.arange(N * K) - offsets[sorted_exp]
        cap = int(np.ceil(N * K / E * CAP_FACTOR))
        T = E * cap
        valid = within < cap
        dst = jnp.where(valid, sorted_exp * cap + within, T)
        padded_tokens = jnp.zeros((T, H), x.dtype).at[dst].set(x[order // K], mode='drop')
        padded_probs = jnp.zeros((T,), exp_p.dtype).at[dst].set(exp_p[order], mode='drop')
        padded_tid = jnp.zeros((T,), jnp.int32).at[dst].set((order // K).astype(jnp.int32), mode='drop')
        xt = padded_tokens.reshape(E, cap, H)
        fc1 = jax.nn.gelu(jnp.einsum('ech,ehf->ecf', xt, moe_w1))
        fc2 = jnp.einsum('ecf,efh->ech', fc1, moe_w2).reshape(T, H)
        weighted = fc2 * padded_probs[:, None]
        moe_out = jnp.zeros((N, H), hidden_states.dtype).at[padded_tid].add(weighted)
        return h1 + moe_out.reshape(S, B, H)
    x = L0_attn_x
    x = x + _layernorm(_L0_attn_ref(_layernorm(x, axis=-1), L0_attn_v_first, L0_attn_ln_pre_w, L0_attn_ln_pre_b, L0_attn_ln_attn_w, L0_attn_ln_attn_b, L0_attn_ln_ffn_w, L0_attn_ln_ffn_b, L0_attn_x_r, L0_attn_x_w, L0_attn_x_k, L0_attn_x_v, L0_attn_x_a, L0_attn_x_g, L0_attn_w0, L0_attn_w1, L0_attn_w2, L0_attn_a0, L0_attn_a1, L0_attn_a2, L0_attn_g1, L0_attn_g2, L0_attn_k_k, L0_attn_k_a, L0_attn_r_k, L0_attn_W_r, L0_attn_W_k, L0_attn_W_v, L0_attn_W_o, L0_attn_gn_w, L0_attn_gn_b, L0_attn_ffn_x_k, L0_attn_W_ffn1, L0_attn_W_ffn2), axis=-1)
    x = x + _layernorm(_L0_ffn_ref(_layernorm(x, axis=-1), L0_ffn_shared_w1, L0_ffn_shared_b1, L0_ffn_shared_w2, L0_ffn_shared_b2, L0_ffn_router_w, L0_ffn_router_b, L0_ffn_spec_w1, L0_ffn_spec_b1, L0_ffn_spec_w2, L0_ffn_spec_b2), axis=-1)
    x = x + _layernorm(_L1_attn_ref(_layernorm(x, axis=-1), L1_attn_Wqkvg, L1_attn_bqkvg, L1_attn_wave_frequency, L1_attn_wave_damping, L1_attn_wave_phase, L1_attn_field_coupling, L1_attn_Wout, L1_attn_bout), axis=-1)
    x = x + _layernorm(_L1_ffn_ref(_layernorm(x, axis=-1), L1_ffn_wqkv, L1_ffn_q_scale, L1_ffn_k_scale, L1_ffn_wo, L1_ffn_ln_g, L1_ffn_ln_b, L1_ffn_w1, L1_ffn_b1, L1_ffn_w2, L1_ffn_b2), axis=-1)
    x = x + _layernorm(_L2_attn_ref(_layernorm(x, axis=-1), L2_attn_W_in, L2_attn_conv_w, L2_attn_conv_b, L2_attn_delta_param, L2_attn_W_gate, L2_attn_norm_w, L2_attn_W_out), axis=-1)
    x = x + _layernorm(_L2_ffn_ref(_layernorm(x, axis=-1), L2_ffn_gate_w, L2_ffn_w1, L2_ffn_b1, L2_ffn_w2, L2_ffn_b2), axis=-1)
    x = x + _layernorm(_L3_attn_ref(_layernorm(x, axis=-1), L3_attn_norm_scale, L3_attn_w_in, L3_attn_conv_weight, L3_attn_conv_bias, L3_attn_A_log, L3_attn_dt_bias, L3_attn_w_out), axis=-1)
    x = x + _layernorm(_L3_ffn_ref(_layernorm(x, axis=-1), L3_ffn_ln1_weight, L3_ffn_ln1_bias, L3_ffn_ln2_weight, L3_ffn_ln2_bias, L3_ffn_qkv_weight, L3_ffn_proj_weight, L3_ffn_router_weight, L3_ffn_moe_w1, L3_ffn_moe_w2), axis=-1)
    return x

_drawn_inputs = setup_inputs


def setup_inputs(seed=0):
    import zlib

    import numpy as np

    out = dict(_drawn_inputs(seed))
    spreads = {'L0_attn_v_first': (0.0, 0.1),
     'L0_attn_ln_pre_w': (1.0, 0.2),
     'L0_attn_ln_pre_b': (0.0, 0.1),
     'L0_attn_ln_attn_w': (1.0, 0.6),
     'L0_attn_ln_attn_b': (0.0, 0.677),
     'L0_attn_ln_ffn_w': (1.0, 0.6),
     'L0_attn_ln_ffn_b': (0.0, 0.469),
     'L0_attn_k_a': (1.0, 0.6),
     'L0_attn_gn_w': (1.0, 0.6),
     'L0_attn_gn_b': (0.0, 0.682),
     'L0_ffn_shared_b1': (0.0, 0.1),
     'L0_ffn_shared_b2': (0.0, 0.1),
     'L0_ffn_router_b': (0.0, 0.1),
     'L0_ffn_spec_b1': (0.0, 0.1),
     'L0_ffn_spec_b2': (0.0, 0.1),
     'L1_attn_bout': (0.0, 0.1),
     'L1_ffn_q_scale': (1.0, 0.6),
     'L1_ffn_k_scale': (1.0, 0.6),
     'L1_ffn_ln_g': (1.0, 0.6),
     'L1_ffn_ln_b': (0.0, 0.8),
     'L1_ffn_b1': (0.0, 0.691),
     'L1_ffn_b2': (0.0, 0.1),
     'L2_attn_conv_b': (0.0, 0.1),
     'L2_attn_delta_param': (0.0, 0.285),
     'L2_attn_norm_w': (1.0, 0.2),
     'L3_attn_norm_scale': (1.0, 0.6),
     'L3_attn_conv_bias': (0.0, 0.8),
     'L3_ffn_ln1_weight': (1.0, 0.6),
     'L3_ffn_ln1_bias': (0.0, 0.8),
     'L3_ffn_ln2_weight': (1.0, 0.6),
     'L3_ffn_ln2_bias': (0.0, 0.8)}
    factors = {'L0_attn_x_r': 6.969,
     'L0_attn_x_w': 8.0,
     'L0_attn_x_k': 6.293,
     'L0_attn_x_v': 5.119,
     'L0_attn_x_a': 8.0,
     'L0_attn_x_g': 8.0,
     'L0_attn_w0': 6.651,
     'L0_attn_w1': 8.0,
     'L0_attn_w2': 8.0,
     'L0_attn_a0': 8.0,
     'L0_attn_a1': 8.0,
     'L0_attn_a2': 8.0,
     'L0_attn_g1': 8.0,
     'L0_attn_k_k': 8.0,
     'L0_attn_r_k': 8.0,
     'L0_attn_ffn_x_k': 3.671,
     'L1_attn_field_coupling': 3.468,
     'L1_ffn_w1': 4.007,
     'L1_ffn_w2': 4.478,
     'L3_attn_w_in': 8.0,
     'L3_attn_conv_weight': 8.0,
     'L3_attn_A_log': 8.0,
     'L3_attn_dt_bias': 8.0,
     'L3_attn_w_out': 8.0,
     'L3_ffn_qkv_weight': 8.0,
     'L3_ffn_proj_weight': 8.0,
     'L3_ffn_router_weight': 8.0,
     'L3_ffn_moe_w1': 8.0,
     'L3_ffn_moe_w2': 8.0}
    for name, (base, spread) in spreads.items():
        noise = np.random.default_rng([zlib.crc32(name.encode()), seed]).standard_normal(out[name].shape)
        drawn = base * np.exp(spread * noise) if base else spread * noise
        out[name] = jnp.asarray(drawn.astype(out[name].dtype))
    for name, factor in factors.items():
        out[name] = (out[name] * factor).astype(out[name].dtype)
    return out
```

```python
from contextlib import ExitStack

import numpy as np
import concourse.bass as bass
from concourse import mybir

F32 = mybir.dt.float32
BF16 = mybir.dt.bfloat16
ALU = mybir.AluOpType
ACT = mybir.ActivationFunctionType
AX = mybir.AxisListType

SEQS, SEQ, C = 16, 256, 128
P = 128
TILES = SEQS * SEQ // P
PAIRS = SEQS // 2
PT = 4
PN = PT * P
EPS = 1e-5
BIG = 1e30


class Core:

    def __init__(self, nc, ctx, dram):
        self.nc, self.ctx, self.dram = nc, ctx, dram
        self.semaphores = []
        self.x = self.sb("x", [P, TILES, C])
        self.normed = self.sb("normed", [P, TILES, C])
        self.normed_t = self.sb("normed_t", [C, TILES * P])
        self.ident = self.sb("ident", [P, P])
        self.minus_half = self.sb("minus_half", [P, 16])
        self.eps = self.sb("eps", [P, 16])
        self.ones_row = self.sb("ones_row", [1, P])
        self.branch = self.sb("branch", [P, PT, C])
        self.fresh = self.sb("fresh", [P, PT, C])
        self.branch_norm = self.norm_buffers("branch_norm", PT)
        self.x_norm = self.norm_buffers("x_norm", PT)
        self.bank = [ctx.enter_context(nc.psum_tensor(f"bank{i}", [P, 512], F32)) for i in range(8)]

    def norm_buffers(self, name, rows, ctx=None):
        return [self.sb(f"{name}_parts", [P, rows, 6], ctx=ctx), self.sb(f"{name}_moments", [P, rows, 2], ctx=ctx),
                self.sb(f"{name}_rstd", [P, rows], ctx=ctx), self.sb(f"{name}_shifted", [P, rows], ctx=ctx)]

    def sb(self, name, shape, dtype=F32, ctx=None):
        return (ctx or self.ctx).enter_context(self.nc.sbuf_tensor(name, shape, dtype))

    def sem(self, name):
        handle = self.nc.alloc_semaphore(name)
        self.semaphores.append(handle)
        return handle

    def end_of_block(self):
        self.nc.clear_and_free_semaphores(self.semaphores)
        self.nc.all_engine_barrier()
        self.semaphores = []


class Norm:

    def __init__(self, core, name, rows, eps, buffers):
        self.core, self.rows, self.eps = core, rows, eps
        self.parts, self.moments, self.rstd, self.shifted = buffers
        self.moments_ready = core.sem(f"{name}_moments_ready")
        self.rstd_ready = core.sem(f"{name}_rstd_ready")

    def find_moments(self, dve, row_of):
        for r in range(self.rows):
            dve.bn_stats(self.parts[:, r, :], row_of(r))
        dve.drain()
        for r in range(self.rows):
            last = dve.bn_aggr(self.moments[:, r, :], self.parts[:, r, :])
        last.then_inc(self.moments_ready, 1)
        dve.drain()

    def power(self, pool, turn):
        pool.wait_ge(self.moments_ready, turn + 1)
        pool.tensor_tensor(self.shifted[:], self.moments[:, :, 1], self.eps[:, 0:self.rows], ALU.add)
        pool.drain()
        pool.tensor_tensor(self.rstd[:], self.shifted[:], self.core.minus_half[:, 0:self.rows],
                           ALU.pow).then_inc(self.rstd_ready, 1)

    def apply(self, dve, turn, out_of, row_of):
        dve.wait_ge(self.rstd_ready, turn + 1)
        for r in range(self.rows):
            last = dve.tensor_scalar(out_of(r), row_of(r), self.moments[:, r, 0:1], self.rstd[:, r:r + 1],
                                     ALU.subtract, ALU.mult)
        return last


class Tail:

    def __init__(self, core, name, keep_rows, turned, last=False, bank=7):
        self.core, self.keep_rows, self.turned, self.last = core, keep_rows, turned, last
        self.turn_bank = core.bank[bank]
        self.of_branch = Norm(core, f"{name}_branch", PT, core.eps, core.branch_norm)
        self.of_x = Norm(core, f"{name}_x", PT, core.eps, core.x_norm)
        self.fresh_ready = core.sem(f"{name}_fresh_ready")
        self.fresh_turned = core.sem(f"{name}_fresh_turned")
        self.turned_stored = core.sem(f"{name}_turned_stored")
        self.fresh_kept = core.sem(f"{name}_fresh_kept")
        self.x_final = core.sem(f"{name}_x_final")

    def dve(self, dve, i):
        core = self.core
        self.of_branch.find_moments(dve, lambda r: core.branch[:, r, :])
        self.of_branch.apply(dve, i, lambda r: core.branch[:, r, :], lambda r: core.branch[:, r, :])
        dve.drain()
        x = core.x[:, bass.ds(i * PT, PT), :]
        last = dve.tensor_tensor(x, x, core.branch[:], ALU.add)
        if self.last:
            last.then_inc(self.x_final, 1)
            dve.drain()
            return
        dve.drain()
        self.of_x.find_moments(dve, lambda r: core.x[:, i * PT + r, :])
        if self.turned:
            dve.wait_ge(self.fresh_turned, i)
        if self.keep_rows:
            dve.wait_ge(self.fresh_kept, i)
        self.of_x.apply(dve, i, lambda r: core.fresh[:, r, :],
                        lambda r: core.x[:, i * PT + r, :]).then_inc(self.fresh_ready, 1)
        dve.drain()

    def pool(self, pool, i):
        self.of_branch.power(pool, i)
        if self.last:
            return
        self.of_x.power(pool, i)
        if self.keep_rows:
            pool.wait_ge(self.fresh_ready, i + 1)
            pool.tensor_copy(self.core.normed[:, bass.ds(i * PT, PT), :],
                             self.core.fresh[:]).then_inc(self.fresh_kept, 1)

    def pe(self, pe, i):
        pe.wait_ge(self.fresh_ready, i + 1)
        pe.wait_ge(self.turned_stored, i)
        for t in range(PT):
            last = pe.transpose(self.turn_bank[:, t * P:(t + 1) * P], self.core.fresh[:, t, :], self.core.ident[:])
        last.then_inc(self.fresh_turned, 1)

    def act(self, act, i):
        act.wait_ge(self.fresh_turned, i + 1)
        act.activation(self.core.normed_t[:, bass.ds(i * PN, PN)], self.turn_bank[:],
                       ACT.Identity).then_inc(self.turned_stored, 1)


def prologue(core, x_dram):
    nc, dram = core.nc, core.dram
    with ExitStack() as ctx:
        norm = Norm(core, "first", PT, core.eps, core.x_norm)
        x_loaded, consts = core.sem("x_loaded"), core.sem("consts_loaded")
        fresh_ready, fresh_turned = core.sem("first_ready"), core.sem("first_turned")
        stored, kept = core.sem("first_stored"), core.sem("first_kept")
        block = ctx.enter_context(nc.Block())

        @block.sync
        def _(sp):
            sp.dma_start(core.ident[:], dram["identity"]).then_inc(consts, 16)
            sp.dma_start(core.x[:], x_dram.rearrange("b (h p) c -> p (b h) c", p=P)).then_inc(x_loaded, 16)

        @block.gpsimd
        def _(pool):
            pool.memset(core.minus_half[:], -0.5)
            pool.memset(core.eps[:], EPS)
            pool.memset(core.ones_row[:], 1.0)
            pool.drain()
            with pool.Fori(0, PAIRS) as i:
                norm.power(pool, i)
                pool.wait_ge(fresh_ready, i + 1)
                pool.tensor_copy(core.normed[:, bass.ds(i * PT, PT), :], core.fresh[:]).then_inc(kept, 1)

        @block.vector
        def _(dve):
            dve.wait_ge(x_loaded, 16)
            with dve.Fori(0, PAIRS) as i:
                norm.find_moments(dve, lambda r: core.x[:, i * PT + r, :])
                dve.wait_ge(fresh_turned, i)
                dve.wait_ge(kept, i)
                norm.apply(dve, i, lambda r: core.fresh[:, r, :],
                           lambda r: core.x[:, i * PT + r, :]).then_inc(fresh_ready, 1)
                dve.drain()

        @block.tensor
        def _(pe):
            pe.wait_ge(consts, 16)
            with pe.Fori(0, PAIRS) as i:
                pe.wait_ge(fresh_ready, i + 1)
                pe.wait_ge(stored, i)
                for t in range(PT):
                    last = pe.transpose(core.bank[7][:, t * P:(t + 1) * P], core.fresh[:, t, :], core.ident[:])
                last.then_inc(fresh_turned, 1)

        @block.scalar
        def _(act):
            with act.Fori(0, PAIRS) as i:
                act.wait_ge(fresh_turned, i + 1)
                act.activation(core.normed_t[:, bass.ds(i * PN, PN)], core.bank[7][:],
                               ACT.Identity).then_inc(stored, 1)


EXPERTS = 8


def top_two(core, name, ctx, logits, weights, normalised, act_exp):
    shape = [P, TILES, EXPERTS]
    work = core.sb(f"{name}_gate_work", shape, ctx=ctx)
    rest = core.sb(f"{name}_gate_rest", shape, ctx=ctx)
    picked = core.sb(f"{name}_gate_picked", shape, ctx=ctx)
    order = core.sb(f"{name}_gate_order", [P, EXPERTS], ctx=ctx)
    best = core.sb(f"{name}_gate_best", [P, TILES], ctx=ctx)
    first = core.sb(f"{name}_gate_first", [P, TILES], ctx=ctx)

    def wide(small):
        return small[:].unsqueeze(2).broadcast_to(shape)

    ranks = order[:].unsqueeze(1).broadcast_to(shape)

    def run(dve):
        for e in range(EXPERTS):
            dve.memset(order[:, e:e + 1], float(EXPERTS - e))
        dve.drain()
        for k in range(2):
            source = logits if k == 0 else rest
            dve.tensor_reduce(best[:], source[:], AX.X, ALU.max)
            dve.drain()
            dve.tensor_tensor(work[:], source[:], wide(best), ALU.is_equal)
            if k == 0:
                dve.tensor_tensor(weights[:], logits[:], wide(best), ALU.subtract)
            dve.drain()
            dve.tensor_tensor(work[:], work[:], ranks, ALU.mult)
            dve.drain()
            dve.tensor_reduce(first[:], work[:], AX.X, ALU.max)
            dve.drain()
            dve.tensor_tensor(work[:], ranks, wide(first), ALU.is_equal)
            dve.drain()
            if k == 0:
                dve.tensor_copy(picked[:], work[:])
                dve.scalar_tensor_tensor(rest[:], work[:], -BIG, logits[:], ALU.mult, ALU.add)
            else:
                dve.tensor_tensor(picked[:], picked[:], work[:], ALU.add)
            dve.drain()
        act_exp(dve)
        if normalised:
            dve.tensor_tensor(weights[:], weights[:], picked[:], ALU.mult)
            dve.drain()
        dve.tensor_reduce(best[:], weights[:], AX.X, ALU.add)
        dve.drain()
        dve.reciprocal(first[:], best[:])
        dve.drain()
        if not normalised:
            dve.tensor_tensor(weights[:], weights[:], picked[:], ALU.mult)
            dve.drain()
        dve.tensor_tensor(weights[:], weights[:], wide(first), ALU.mult)
        dve.drain()

    return run, picked


def moe_block(core, name, tail, shared, bias, normalised, chunks, capacity=None, source_t=None, base=None):
    nc, dram = core.nc, core.dram
    heads = EXPERTS + (1 if shared else 0)
    first_routed = heads - EXPERTS
    hidden = chunks * P
    source_t = source_t or core.normed_t
    with ExitStack() as ctx:
        w1 = core.sb(f"{name}_w1", [P, heads, hidden], ctx=ctx)
        w2 = core.sb(f"{name}_w2", [P, heads, chunks, C], ctx=ctx)
        router = core.sb(f"{name}_router", [P, EXPERTS], ctx=ctx)
        logits = core.sb(f"{name}_logits", [P, TILES, EXPERTS], ctx=ctx)
        weights = core.sb(f"{name}_weights", [P, TILES, EXPERTS], ctx=ctx)
        logit_rows = core.sb(f"{name}_logit_rows", [EXPERTS, PN], ctx=ctx)
        hid = core.sb(f"{name}_hidden", [P, 2, chunks, PN], ctx=ctx)
        if bias:
            b1 = core.sb(f"{name}_b1", [P, heads * chunks], ctx=ctx)
            b2 = core.sb(f"{name}_b2", [heads, C], ctx=ctx)
            pair_weights = core.sb(f"{name}_pair_weights", [P, PT, heads], ctx=ctx)
            weight_rows = core.sb(f"{name}_weight_rows", [heads, PN], ctx=ctx)
        if shared:
            router_b = core.sb(f"{name}_router_b", [EXPERTS, 1], ctx=ctx)
        if capacity:
            earlier = core.sb(f"{name}_earlier", [P, P], ctx=ctx)
            ones = core.sb(f"{name}_ones", [P, P], ctx=ctx)
            counts = core.sb(f"{name}_counts", [P, TILES, EXPERTS], ctx=ctx)
            before = core.sb(f"{name}_before", [P, TILES, EXPERTS], ctx=ctx)
            fits = core.sb(f"{name}_fits", [P, TILES, EXPERTS], ctx=ctx)
            picks_ready, ranks_ready = core.sem(f"{name}_picks_ready"), core.sem(f"{name}_ranks_ready")
            ranks_taken = core.sem(f"{name}_ranks_taken")
        weights_in = core.sem(f"{name}_weights_in")
        logit_rows_up, logit_rows_down = core.sem(f"{name}_logit_rows_up"), core.sem(f"{name}_logit_rows_down")
        logits_up, logits_down = core.sem(f"{name}_logits_up"), core.sem(f"{name}_logits_down")
        exp_asked, exp_done = core.sem(f"{name}_exp_asked"), core.sem(f"{name}_exp_done")
        hidden_up, hidden_done = core.sem(f"{name}_hidden_up"), core.sem(f"{name}_hidden_done")
        out_up, out_taken = core.sem(f"{name}_out_up"), core.sem(f"{name}_out_taken")
        if bias:
            pair_staged, pair_turned = core.sem(f"{name}_pair_staged"), core.sem(f"{name}_pair_turned")
            rows_staged = core.sem(f"{name}_rows_staged")
            bias_up, bias_taken = core.sem(f"{name}_bias_up"), core.sem(f"{name}_bias_taken")
        hbank, obank, small = core.bank[0:4], core.bank[4:6], core.bank[6]
        loads = 3 + (2 if bias else 0) + (1 if shared else 0) + (2 if capacity else 0)
        per_pair = heads * chunks

        def act_exp(dve):
            dve.sem_inc(exp_asked, 1)
            dve.wait_ge(exp_done, 1)

        gate, picked = top_two(core, name, ctx, logits, weights, normalised, act_exp)
        block = ctx.enter_context(nc.Block())

        def slot_turn(i, e):
            back = 1 if heads % 2 and e == 0 else 2
            if isinstance(i, int) and i * heads + e < back:
                return None
            return i * heads + e - back + 1

        @block.sync
        def _(sp):
            sp.dma_start(router[:], dram[f"{name}_router"]).then_inc(weights_in, 16)
            sp.dma_start(w1[:], dram[f"{name}_w1"]).then_inc(weights_in, 16)
            sp.dma_start(w2[:], dram[f"{name}_w2"]).then_inc(weights_in, 16)
            if bias:
                sp.dma_start(b1[:], dram[f"{name}_b1"]).then_inc(weights_in, 16)
                sp.dma_start(b2[:], dram[f"{name}_b2"]).then_inc(weights_in, 16)
            if shared:
                sp.dma_start(router_b[:], dram[f"{name}_router_b"]).then_inc(weights_in, 16)
            if capacity:
                sp.dma_start(earlier[:], dram["earlier"]).then_inc(weights_in, 16)
                sp.dma_start(ones[:], dram["ones"]).then_inc(weights_in, 16)

        @block.tensor
        def _(pe):
            pe.wait_ge(weights_in, 16 * loads)
            with pe.Fori(0, PAIRS) as i:
                pe.wait_ge(logit_rows_down, i)
                pe.matmul(small[0:EXPERTS, :], router[:], source_t[:, bass.ds(i * PN, PN)],
                          start=True, stop=True).then_inc(logit_rows_up, 1)
                pe.wait_ge(logit_rows_down, i + 1)
                pe.wait_ge(logits_down, i)
                for t in range(PT):
                    last = pe.matmul(obank[0][:, t * EXPERTS:(t + 1) * EXPERTS], logit_rows[:, t * P:(t + 1) * P],
                                     core.ident[0:EXPERTS, 0:EXPERTS], start=True, stop=True)
                last.then_inc(logits_up, 1)
            if capacity:
                pe.wait_ge(picks_ready, 1)
                flat = picked[:].rearrange("p t e -> p (t e)")
                pe.matmul(hbank[0][:, 0:TILES * EXPERTS], earlier[:], flat, start=True, stop=True)
                pe.matmul(hbank[1][:, 0:TILES * EXPERTS], ones[:], flat, start=True,
                          stop=True).then_inc(ranks_ready, 1)
                pe.wait_ge(ranks_taken, 1)
            pe.wait_ge(logits_down, PAIRS)

            def pair(i, has_tail):
                def up(e):
                    for f in range(chunks):
                        n = e * chunks + f
                        if not (isinstance(i, int) and n < 4):
                            pe.wait_ge(hidden_done, i * per_pair + n - 3)
                        pe.matmul(hbank[n % 4][:], w1[:, e, f * P:(f + 1) * P], source_t[:, bass.ds(i * PN, PN)],
                                  start=True, stop=True).then_inc(hidden_up, 1)

                def down(e):
                    pe.wait_ge(hidden_done, i * per_pair + (e + 1) * chunks)
                    if (turn := slot_turn(i, e)) is not None:
                        pe.wait_ge(out_taken, turn)
                    for t in range(PT):
                        for f in range(chunks):
                            last = pe.matmul(obank[e % 2][:, t * P:(t + 1) * P], hid[:, e % 2, f, t * P:(t + 1) * P],
                                             w2[:, e, f, :], start=(f == 0), stop=(f == chunks - 1))
                    last.then_inc(out_up, 1)

                up(0)
                if bias:
                    pe.wait_ge(pair_staged, i + 1)
                    pe.wait_ge(bias_taken, i)
                    for t in range(PT):
                        last = pe.transpose(small[0:heads, t * P:(t + 1) * P], pair_weights[:, t, :], core.ident[:])
                    last.then_inc(pair_turned, 1)
                for e in range(1, heads + 1):
                    if e < heads:
                        up(e)
                    if e == 1 and bias:
                        pe.wait_ge(rows_staged, i + 1)
                        for t in range(PT):
                            last = pe.matmul(small[:, t * P:(t + 1) * P], weight_rows[:, t * P:(t + 1) * P], b2[:],
                                             start=True, stop=True)
                        last.then_inc(bias_up, 1)
                    down(e - 1)
                    if e == 3 and has_tail and tail.turned:
                        tail.pe(pe, i - 1)

            pair(0, False)
            with pe.Fori(1, PAIRS) as i:
                pair(i, True)
            if tail.turned:
                tail.pe(pe, PAIRS - 1)

        @block.scalar
        def _(act):
            act.wait_ge(weights_in, 16 * loads)
            with act.Fori(0, PAIRS) as i:
                act.wait_ge(logit_rows_up, i + 1)
                act.wait_ge(logits_up, i)
                act.activation(logit_rows[:], small[0:EXPERTS, :], ACT.Identity,
                               bias=router_b[:, 0:1] if shared else 0.0).then_inc(logit_rows_down, 1)
            act.wait_ge(exp_asked, 1)
            act.activation(weights[:], weights[:], ACT.Exp).then_inc(exp_done, 1)

            def pair(i, has_tail):
                for e in range(heads):
                    if (turn := slot_turn(i, e)) is not None:
                        act.wait_ge(out_up, turn)
                    for f in range(chunks):
                        n = e * chunks + f
                        act.wait_ge(hidden_up, i * per_pair + n + 1)
                        act.activation(hid[:, e % 2, f, :], hbank[n % 4][:], ACT.Gelu_apprx_tanh,
                                       bias=b1[:, n:n + 1] if bias else 0.0).then_inc(hidden_done, 1)
                    if e == 0 and bias:
                        act.wait_ge(pair_turned, i + 1)
                        act.wait_ge(bias_up, i)
                        act.activation(weight_rows[:], small[0:heads, :], ACT.Identity).then_inc(rows_staged, 1)
                    if e == 3 and has_tail and tail.turned:
                        tail.act(act, i - 1)

            pair(0, False)
            with act.Fori(1, PAIRS) as i:
                pair(i, True)
            if tail.turned:
                tail.act(act, PAIRS - 1)

        @block.gpsimd
        def _(pool):
            with pool.Fori(0, PAIRS) as i:
                tail.pool(pool, i)

        @block.vector
        def _(dve):
            with dve.Fori(0, PAIRS) as i:
                dve.wait_ge(logits_up, i + 1)
                dve.tensor_copy(logits[:, bass.ds(i * PT, PT), :],
                                obank[0][:, 0:PT * EXPERTS].rearrange("p (t e) -> p t e", e=EXPERTS)
                                ).then_inc(logits_down, 1)
            dve.drain()
            gate(dve)
            if capacity:
                dve.sem_inc(picks_ready, 1)
                dve.wait_ge(weights_in, 16 * loads)
                dve.wait_ge(ranks_ready, 1)
                dve.tensor_copy(counts[:].rearrange("p t e -> p (t e)"), hbank[1][:, 0:TILES * EXPERTS])
                dve.memset(before[:], 0.0)
                dve.drain()
                for e in range(EXPERTS):
                    dve.tensor_tensor_scan(before[:, 1:TILES, e], ones[:, 0:TILES - 1], counts[:, 0:TILES - 1, e], 0.0,
                                           ALU.mult, ALU.add)
                dve.drain()
                dve.tensor_tensor(before[:], before[:],
                                  hbank[0][:, 0:TILES * EXPERTS].rearrange("p (t e) -> p t e", e=EXPERTS),
                                  ALU.add).then_inc(ranks_taken, 1)
                dve.drain()
                dve.tensor_scalar(fits[:], before[:], float(capacity), None, ALU.is_lt)
                dve.drain()
                dve.tensor_tensor(weights[:], weights[:], fits[:], ALU.mult)
                dve.drain()
            if bias and shared:
                dve.memset(pair_weights[:], 1.0)
                dve.drain()

            with dve.Fori(0, PAIRS) as i:
                if bias:
                    dve.wait_ge(pair_turned, i)
                    dve.tensor_copy(pair_weights[:, :, first_routed:heads],
                                    weights[:, bass.ds(i * PT, PT), :]).then_inc(pair_staged, 1)
                    dve.wait_ge(bias_up, i + 1)
                    dve.tensor_copy(core.branch[:].rearrange("p t c -> p (t c)"), small[:]).then_inc(bias_taken, 1)
                else:
                    dve.tensor_copy(core.branch[:], base[:, bass.ds(i * PT, PT), :])
                dve.drain()
                for e in range(heads):
                    dve.wait_ge(out_up, i * heads + e + 1)
                    if e < first_routed:
                        last = dve.tensor_tensor(core.branch[:].rearrange("p t c -> p (t c)"), obank[e % 2][:],
                                                 core.branch[:].rearrange("p t c -> p (t c)"), ALU.add)
                    else:
                        for t in range(PT):
                            last = dve.scalar_tensor_tensor(
                                core.branch[:, t, :], obank[e % 2][:, t * P:(t + 1) * P],
                                weights[:, i * PT + t, e - first_routed:e - first_routed + 1],
                                core.branch[:, t, :], ALU.mult, ALU.add)
                    last.then_inc(out_taken, 1)
                    dve.drain()
                tail.dve(dve, i)


class TurnedNorm:

    def __init__(self, core, name, ctx, bank, eps=None):
        self.core, self.bank = core, bank
        self.norm = Norm(core, name, PT, core.eps if eps is None else eps, core.norm_buffers(name, PT, ctx))
        self.rows = core.sb(f"{name}_rows", [P, PT, C], ctx=ctx)
        self.rows_ready, self.turned = core.sem(f"{name}_rows_ready"), core.sem(f"{name}_turned")
        self.taken = core.sem(f"{name}_taken")

    def dve(self, dve, i, row_of):
        self.norm.find_moments(dve, row_of)
        dve.wait_ge(self.turned, i)
        self.norm.apply(dve, i, lambda r: self.rows[:, r, :], row_of).then_inc(self.rows_ready, 1)

    def pool(self, pool, i):
        self.norm.power(pool, i)

    def pe(self, pe, i):
        pe.wait_ge(self.rows_ready, i + 1)
        pe.wait_ge(self.taken, i)
        for t in range(PT):
            last = pe.transpose(self.bank[:, t * P:(t + 1) * P], self.rows[:, t, :], self.core.ident[:])
        last.then_inc(self.turned, 1)

    def act(self, act, i, out, scale, shift):
        act.wait_ge(self.turned, i + 1)
        return act.activation(out, self.bank[:], ACT.Identity, bias=shift, scale=scale).then_inc(self.taken, 1)


def attention_over_sequences(core):
    nc, dram = core.nc, core.dram
    HEADS, GROUPS, HD = 16, 4, 8
    PER = HEADS // GROUPS
    GW = (PER + 2) * HD
    LAGS = SEQS
    SCALE = float(1.0 / np.sqrt(HD).astype(np.float32))
    with ExitStack() as ctx:
        qkv = core.sb("attn_qkv", [P, TILES, GROUPS * GW], ctx=ctx)
        scores = core.sb("attn_scores", [P, TILES * HEADS, LAGS], ctx=ctx)
        mixed = core.sb("attn_mixed", [P, TILES, C], ctx=ctx)
        products = core.sb("attn_products", [P, 2, TILES * PER * HD], ctx=ctx)
        top = core.sb("attn_top", [P, TILES * HEADS], ctx=ctx)
        share = core.sb("attn_share", [P, TILES * HEADS], ctx=ctx)
        cols = core.sb("attn_cols", [P, 4], ctx=ctx)
        wqkv = core.sb("attn_wqkv", [P, GROUPS * GW], ctx=ctx)
        wproj = core.sb("attn_wproj", [P, C], ctx=ctx)
        xt = core.sb("attn_xt", [P, PN], ctx=ctx)
        weights_in = core.sem("attn_weights_in")

        with ExitStack() as inner:
            ln1 = TurnedNorm(core, "attn_ln1", inner, core.bank[0])
            xt_ready, qkv_up, qkv_down = core.sem("attn_xt_ready"), core.sem("attn_qkv_up"), core.sem("attn_qkv_down")
            block = inner.enter_context(nc.Block())

            @block.sync
            def _(sp):
                sp.dma_start(cols[:], dram["attn_cols"]).then_inc(weights_in, 16)
                sp.dma_start(wqkv[:], dram["attn_wqkv"]).then_inc(weights_in, 16)
                sp.dma_start(wproj[:], dram["attn_wproj"]).then_inc(weights_in, 16)

            @block.vector
            def _(dve):
                with dve.Fori(0, PAIRS) as i:
                    ln1.dve(dve, i, lambda r: core.normed[:, i * PT + r, :])
                    dve.wait_ge(qkv_up, i + 1)
                    for h in range(2):
                        last = dve.tensor_copy(qkv[:, bass.ds(i * PT + 2 * h, 2), :],
                                               core.bank[1 + h][:, 0:2 * GROUPS * GW].rearrange(
                                                   "p (t c) -> p t c", t=2))
                    last.then_inc(qkv_down, 1)

            @block.gpsimd
            def _(pool):
                with pool.Fori(0, PAIRS) as i:
                    ln1.pool(pool, i)

            @block.tensor
            def _(pe):
                pe.wait_ge(weights_in, 48)
                with pe.Fori(0, PAIRS) as i:
                    ln1.pe(pe, i)
                    pe.wait_ge(xt_ready, i + 1)
                    pe.wait_ge(qkv_down, i)
                    for t in range(PT):
                        last = pe.matmul(core.bank[1 + t // 2][:, (t % 2) * GROUPS * GW:(t % 2 + 1) * GROUPS * GW],
                                         xt[:, t * P:(t + 1) * P], wqkv[:], start=True, stop=True)
                    last.then_inc(qkv_up, 1)

            @block.scalar
            def _(act):
                act.wait_ge(weights_in, 48)
                with act.Fori(0, PAIRS) as i:
                    act.wait_ge(qkv_up, i)
                    ln1.act(act, i, xt[:], cols[:, 0:1], cols[:, 1:2])
                    act.drain()
                    act.sem_inc(xt_ready, 1)

        with ExitStack() as inner:
            product_ready, product_used = core.sem("attn_product_ready"), core.sem("attn_product_used")
            share_ready = core.sem("attn_share_ready")
            exp_asked, exp_done = core.sem("attn_exp_asked"), core.sem("attn_exp_done")
            block = inner.enter_context(nc.Block())
            steps = [(lag, g) for lag in range(LAGS) for g in range(GROUPS)]
            by_group = qkv[:].rearrange("p t (g c) -> p t g c", g=GROUPS)
            by_head = scores[:].rearrange("p (t h) l -> p t h l", h=HEADS)

            def product(n, count):
                return products[:, n % 2, 0:count * PER * HD].rearrange("p (t q d) -> p t q d", q=PER, d=HD)

            @block.gpsimd
            def _(pool):
                for n, (lag, g) in enumerate(steps):
                    count = TILES - 2 * lag
                    if n >= 2:
                        pool.wait_ge(product_used, n - 1)
                    queries = by_group[:, 2 * lag:, g, 0:PER * HD].rearrange("p t (q d) -> p t q d", d=HD)
                    keys = by_group[:, 0:count, g, PER * HD:(PER + 1) * HD].unsqueeze(2)
                    pool.tensor_tensor(product(n, count), queries,
                                       keys.broadcast_to([P, count, PER, HD]), ALU.mult).then_inc(product_ready, 1)
                pool.wait_ge(share_ready, 1)
                for n, (lag, g) in enumerate(steps):
                    count = TILES - 2 * lag
                    pool.wait_ge(product_used, len(steps) + n - 1)
                    share_of = by_head[:, 2 * lag:, g * PER:(g + 1) * PER, lag].unsqueeze(3)
                    values = by_group[:, 0:count, g, (PER + 1) * HD:].unsqueeze(2)
                    pool.tensor_tensor(product(n, count), share_of.broadcast_to([P, count, PER, HD]),
                                       values.broadcast_to([P, count, PER, HD]), ALU.mult).then_inc(product_ready, 1)

            @block.scalar
            def _(act):
                act.wait_ge(exp_asked, 1)
                act.activation(scores[:], scores[:], ACT.Exp).then_inc(exp_done, 1)

            @block.vector
            def _(dve):
                dve.memset(scores[:], -BIG)
                dve.drain()
                for n, (lag, g) in enumerate(steps):
                    count = TILES - 2 * lag
                    dve.wait_ge(product_ready, n + 1)
                    dve.tensor_reduce(by_head[:, 2 * lag:, g * PER:(g + 1) * PER, lag], product(n, count),
                                      AX.X, ALU.add).then_inc(product_used, 1)
                dve.drain()
                dve.tensor_reduce(top[:], scores[:], AX.X, ALU.max)
                dve.drain()
                dve.tensor_tensor(scores[:], scores[:],
                                  top[:].unsqueeze(2).broadcast_to([P, TILES * HEADS, LAGS]), ALU.subtract)
                dve.drain()
                dve.tensor_scalar(scores[:], scores[:], SCALE, None, ALU.mult)
                dve.drain()
                dve.sem_inc(exp_asked, 1)
                dve.wait_ge(exp_done, 1)
                dve.tensor_reduce(top[:], scores[:], AX.X, ALU.add)
                dve.drain()
                dve.reciprocal(share[:], top[:])
                dve.sem_inc(share_ready, 1)
                for n, (lag, g) in enumerate(steps):
                    count = TILES - 2 * lag
                    dve.wait_ge(product_ready, len(steps) + n + 1)
                    mix = mixed[:, 2 * lag:, g * PER * HD:(g + 1) * PER * HD].rearrange("p t (q d) -> p t q d", d=HD)
                    if lag == 0:
                        last = dve.tensor_copy(mix, product(n, count))
                    else:
                        last = dve.tensor_tensor(mix, mix, product(n, count), ALU.add)
                    last.then_inc(product_used, 1)
                    if g == GROUPS - 1:
                        dve.drain()

        with ExitStack() as inner:
            ln2 = TurnedNorm(core, "attn_ln2", inner, core.bank[0])
            scaled = core.sb("attn_scaled", [P, PT, C], ctx=inner)
            scaled_ready, scaled_turned = core.sem("attn_scaled_ready"), core.sem("attn_scaled_turned")
            mix_t_ready = core.sem("attn_mix_t_ready")
            proj_up, proj_down = core.sem("attn_proj_up"), core.sem("attn_proj_down")
            block = inner.enter_context(nc.Block())

            @block.vector
            def _(dve):
                share_rows = share[:].rearrange("p (t h) -> p t h", h=HEADS)
                with dve.Fori(0, PAIRS) as i:
                    dve.wait_ge(scaled_turned, i)
                    for t in range(PT):
                        last = dve.tensor_tensor(scaled[:, t, :].rearrange("p (h d) -> p h d", d=HD),
                                                 mixed[:, i * PT + t, :].rearrange("p (h d) -> p h d", d=HD),
                                                 share_rows[:, i * PT + t, :].unsqueeze(2).broadcast_to([P, HEADS, HD]),
                                                 ALU.mult)
                    last.then_inc(scaled_ready, 1)
                    dve.wait_ge(proj_up, i + 1)
                    h1 = core.normed[:, bass.ds(i * PT, PT), :]
                    dve.tensor_tensor(h1, core.bank[1][:].rearrange("p (t c) -> p t c", c=C), h1,
                                      ALU.add).then_inc(proj_down, 1)
                    dve.drain()
                    ln2.dve(dve, i, lambda r: core.normed[:, i * PT + r, :])

            @block.gpsimd
            def _(pool):
                with pool.Fori(0, PAIRS) as i:
                    ln2.pool(pool, i)

            @block.tensor
            def _(pe):
                with pe.Fori(0, PAIRS) as i:
                    pe.wait_ge(scaled_ready, i + 1)
                    pe.wait_ge(mix_t_ready, i)
                    for t in range(PT):
                        last = pe.transpose(core.bank[2][:, t * P:(t + 1) * P], scaled[:, t, :], core.ident[:])
                    last.then_inc(scaled_turned, 1)
                    pe.wait_ge(mix_t_ready, i + 1)
                    pe.wait_ge(proj_down, i)
                    for t in range(PT):
                        last = pe.matmul(core.bank[1][:, t * P:(t + 1) * P], xt[:, t * P:(t + 1) * P], wproj[:],
                                         start=True, stop=True)
                    last.then_inc(proj_up, 1)
                    ln2.pe(pe, i)

            @block.scalar
            def _(act):
                with act.Fori(0, PAIRS) as i:
                    act.wait_ge(scaled_turned, i + 1)
                    act.wait_ge(proj_up, i)
                    act.activation(xt[:], core.bank[2][:], ACT.Identity).then_inc(mix_t_ready, 1)
                    ln2.act(act, i, core.normed_t[:, bass.ds(i * PN, PN)], cols[:, 2:3], cols[:, 3:4])


class Rms(Norm):

    def power(self, pool, turn):
        core, n = self.core, self.rows
        pool.wait_ge(self.moments_ready, turn + 1)
        pool.tensor_tensor(self.rstd[:], self.moments[:, :, 0], self.moments[:, :, 0], ALU.mult)
        pool.tensor_tensor(self.shifted[:], self.moments[:, :, 1], self.eps[:, 0:n], ALU.add)
        pool.drain()
        pool.tensor_tensor(self.shifted[:], self.shifted[:], self.rstd[:], ALU.add)
        pool.drain()
        pool.tensor_tensor(self.rstd[:], self.shifted[:], core.minus_half[:, 0:n], ALU.pow).then_inc(self.rstd_ready, 1)

    def scale(self, dve, turn, out_of, row_of):
        dve.wait_ge(self.rstd_ready, turn + 1)
        for r in range(self.rows):
            last = dve.tensor_scalar(out_of(r), row_of(r), self.rstd[:, r:r + 1], None, ALU.mult)
        return last


def ssm_block(core, name, tail, heads, mamba):
    nc, dram = core.nc, core.dram
    INNER, STATE, TAPS = 2 * C, 64, 4
    HD = INNER // heads
    CH = INNER // P
    bc_items = 2 if mamba else 2 * heads * STATE // P
    units = 2 * heads
    SPAN = 3 * P
    items = ([("turn_in", 0)] if mamba else []) + [("x", c) for c in range(CH)] + [("dt", 0)]
    items += [("bc", b) for b in range(bc_items)] + [("gate", g) for g in range(2)]
    items += ([("turn_dt", 0)] if mamba else []) + [("turn_x", c) for c in range(CH)]
    items += [("turn_y", j) for j in range(2)] + [("out", 0)]
    W = len(items)
    assert W % 2 == 0
    with ExitStack() as ctx:
        sb = lambda n, shape, dtype=F32: core.sb(f"{name}_{n}", shape, dtype, ctx=ctx)
        sem = lambda n: core.sem(f"{name}_{n}")
        wx, wdt = sb("wx", [P, INNER]), sb("wdt", [P, heads])
        wbc, wgate = sb("wbc", [P, bc_items, P if not mamba else STATE]), sb("wgate", [P, INNER])
        wout, taps, cols = sb("wout", [P, CH, C]), sb("taps", [P, CH, TAPS + 1]), sb("cols", [P, CH])
        head_cols = sb("head_cols", [heads, 2])
        pick, unpick = sb("pick", [96, heads, P], BF16), sb("unpick", [96, heads], BF16)
        ident16, future = sb("ident16", [P, P], BF16), sb("future", [P, P], BF16)
        padded = sb("padded", [P, CH, 2, SEQ + TAPS - 1])
        conv = sb("conv", [P, CH, 2, SEQ])
        x_rows = sb("x_rows", [P, PT, INNER])
        bc = sb("bc", [P, bc_items, PN])
        gate = sb("gate", [P, PT, INNER])
        raw, bent, delta, logs, cum = (sb(n, [heads, PN]) for n in ("raw", "bent", "delta", "logs", "cum"))
        ones_dt = sb("ones_dt", [heads, SEQ])
        part16, parts = sb("part16", [heads, PN], BF16), sb("parts", [96, PN], BF16)
        decay, mixer = sb("decay", [P, 2, SPAN]), sb("mixer", [P, 2, SPAN])
        gated, gated_t = sb("gated", [P, PT, INNER]), sb("gated_t", [P, PT, CH, P])
        if mamba:
            dt_rows, scores = sb("dt_rows", [P, PT, heads]), sb("scores", [P, SPAN])
            scaled, in_t = sb("scaled", [P, PT, C]), sb("in_t", [P, PN])
            rms_eps = sb("rms_eps", [P, 16])
            rms = Rms(core, f"{name}_rms", PT, rms_eps, core.norm_buffers(f"{name}_rms", PT, ctx))
            scaled_ready = sem("scaled_ready")
            in_rows = in_t
        else:
            magnitude = sb("magnitude", [heads, PN])
            in_rows, staged = sb("in_rows", [P, PN]), sem("staged")
            rms_eps = sb("rms_eps", [P, 16])
            rms = Rms(core, f"{name}_rms", PT, rms_eps, core.norm_buffers(f"{name}_rms", PT, ctx))
        weights_in, ready = sem("weights_in"), sem("ready")
        up = sem("work_up")
        down = [sem("work_down_even"), sem("work_down_odd")]
        padded_ready, conv_ready, x_bent = sem("padded_ready"), sem("conv_ready"), sem("x_bent")
        raw_ready, soft_ready, parts_ready = sem("raw_ready"), sem("soft_ready"), sem("parts_ready")
        delta_ready = sem("delta_ready")
        decay_up, decay_done = sem("decay_up"), sem("decay_done")
        scores_up, scores_taken = sem("scores_up"), sem("scores_taken")
        mixer_done, y_up, y_taken = sem("mixer_done"), sem("y_up"), sem("y_taken")
        gated_ready, folded = sem("gated_ready"), sem("folded")
        dbank, gbank, ybank, work = core.bank[0:2], core.bank[2:4], core.bank[4], core.bank[5:7]
        loads = 12
        block = ctx.enter_context(nc.Block())
        index = {item: w for w, item in enumerate(items)}

        def taken(w, i):
            return i * (W // 2) + w // 2

        @block.sync
        def _(sp):
            for to, what in ((wx, "wx"), (wdt, "wdt"), (wbc, "wbc"), (wgate, "wgate"), (wout, "wout"), (taps, "taps"),
                             (cols, "cols"), (head_cols, "head_cols"), (pick, "pick"), (unpick, "unpick"),):
                sp.dma_start(to[:], dram[f"{name}_{what}"]).then_inc(weights_in, 16)
            sp.dma_start(ident16[:], dram["identity16"]).then_inc(weights_in, 16)
            sp.dma_start(future[:], dram["future"]).then_inc(weights_in, 16)

        @block.gpsimd
        def _(pool):
            pool.memset(rms_eps[:], 1e-6 if mamba else 1.1920928955078125e-07)
            pool.memset(ones_dt[:], 1.0)
            pool.memset(parts[:], 0.0)
            pool.memset(padded[:], 0.0)
            pool.drain()
            pool.sem_inc(ready, 1)
            with pool.Fori(0, PAIRS) as i:
                rms.power(pool, i)
                tail.pool(pool, i)

        @block.tensor
        def _(pe):
            pe.wait_ge(weights_in, 16 * loads)
            pe.wait_ge(folded, 1)

            def pair(i, has_tail):
                source = in_rows[:]

                def turn(w):
                    if not (isinstance(i, int) and w < 2):
                        pe.wait_ge(down[w % 2], taken(w, i))
                    return work[w % 2]

                def item(kind, n):
                    w = index[kind, n]
                    bank = turn(w)
                    if kind == "turn_in":
                        pe.wait_ge(scaled_ready, i + 1)
                        for t in range(PT):
                            last = pe.transpose(bank[:, t * P:(t + 1) * P], scaled[:, t, :], core.ident[:])
                    elif kind == "x":
                        if mamba and n == 0:
                            pe.wait_ge(down[0], i * (W // 2) + 1)
                        last = pe.matmul(bank[:], wx[:, n * P:(n + 1) * P], source, start=True, stop=True)
                    elif kind == "dt":
                        last = pe.matmul(bank[0:heads, :], wdt[:], source, start=True, stop=True)
                    elif kind == "bc":
                        rows = STATE if mamba else P
                        last = pe.matmul(bank[0:rows, :], wbc[:, n, :], source, start=True, stop=True)
                    elif kind == "gate":
                        for t in range(2):
                            tile = 2 * n + t
                            last = pe.matmul(bank[:, t * INNER:(t + 1) * INNER], in_rows[:, tile * P:(tile + 1) * P],
                                             wgate[:], start=True, stop=True)
                    elif kind == "turn_x":
                        pe.wait_ge(x_bent, i * CH + n + 1)
                        flat = conv[:, n].rearrange("p j t -> p (j t)")
                        for t in range(PT):
                            last = pe.transpose(bank[:, t * P:(t + 1) * P], flat[:, t * P:(t + 1) * P], core.ident[:])
                    elif kind == "turn_dt":
                        pe.wait_ge(delta_ready, i + 1)
                        for t in range(PT):
                            last = pe.matmul(bank[:, t * heads:(t + 1) * heads], delta[:, t * P:(t + 1) * P],
                                             core.ident[0:heads, 0:heads], start=True, stop=True)
                    elif kind == "turn_y":
                        pe.wait_ge(gated_ready, i * 2 + n + 1)
                        for t in range(2):
                            for c in range(CH):
                                last = pe.transpose(bank[:, (t * CH + c) * P:(t * CH + c + 1) * P],
                                                    gated[:, 2 * n + t, c * P:(c + 1) * P], core.ident[:])
                    else:
                        for before in (w - 2, w - 1):
                            pe.wait_ge(down[before % 2], i * (W // 2) + before // 2 + 1)
                        for t in range(PT):
                            for c in range(CH):
                                last = pe.matmul(bank[:, t * P:(t + 1) * P], gated_t[:, t, c, :], wout[:, c, :],
                                                 start=(c == 0), stop=(c == CH - 1))
                    last.then_inc(up, 1)

                def unit(u):
                    j, h = divmod(u, heads)
                    n = i * units + u
                    s = [j * SEQ, j * SEQ + P]
                    bank = dbank[u % 2]
                    if not (isinstance(i, int) and u < 2):
                        pe.wait_ge(decay_done, n - 1)
                    for col, rows, width in ((0, s[0], SEQ), (SEQ, s[1], P)):
                        pe.matmul(bank[:, col:col + width], pick[:, h, :], parts[:, rows:rows + width],
                                  start=True, stop=False)
                        pe.matmul(bank[:, col:col + width], parts[:, rows:rows + P],
                                  unpick[:, h:h + 1].broadcast_to([96, width]), start=False, stop=False)
                        last = pe.matmul(bank[:, col:col + P], ident16[:], future[:], start=False, stop=True)
                    last.then_inc(decay_up, 1)
                    if mamba and h:
                        return
                    if mamba:
                        b, c = bc[0:STATE, 0, :], bc[0:STATE, 1, :]
                        turn_no = i * 2 + j
                        skip = isinstance(i, int) and j < 1
                        need = turn_no
                        gb = gbank[0]
                    else:
                        low = STATE * (h % 2)
                        b, c = bc[low:low + STATE, h // 2, :], bc[low:low + STATE, bc_items // 2 + h // 2, :]
                        skip = isinstance(i, int) and u < 2
                        need = n - 1
                        gb = gbank[u % 2]
                    if not skip:
                        pe.wait_ge(scores_taken, need)
                    pe.matmul(gb[:, 0:SEQ], b[:, s[0]:s[0] + P], c[:, s[0]:s[0] + SEQ], start=True, stop=True)
                    pe.matmul(gb[:, SEQ:SPAN], b[:, s[1]:s[1] + P], c[:, s[1]:s[1] + P], start=True,
                              stop=True).then_inc(scores_up, 1)

                def mix(u):
                    j, h = divmod(u, heads)
                    pe.wait_ge(mixer_done, i * units + u + 1)
                    if h == 0 and not (isinstance(i, int) and j == 0):
                        pe.wait_ge(y_taken, i * 2 + j)
                    m = mixer[:, u % 2, :]
                    at = [slice(t * INNER + h * HD, t * INNER + (h + 1) * HD) for t in range(2)]
                    x = [x_rows[:, 2 * j + t, h * HD:(h + 1) * HD] for t in range(2)]
                    pe.matmul(ybank[:, at[0]], m[:, 0:P], x[0], start=True, stop=True)
                    pe.matmul(ybank[:, at[1]], m[:, P:SEQ], x[0], start=True, stop=False)
                    pe.matmul(ybank[:, at[1]], m[:, SEQ:SPAN], x[1], start=False, stop=True).then_inc(y_up, 1)

                if not mamba:
                    pe.wait_ge(staged, i + 1)
                for kind, n in items:
                    if kind == "turn_y":
                        break
                    item(kind, n)
                pe.wait_ge(parts_ready, i + 1)
                for b in range(2):
                    last_item = max(w for w, (kind, _) in enumerate(items) if kind not in ("turn_y", "out") and w % 2 == b)
                    pe.wait_ge(down[b], i * (W // 2) + last_item // 2 + 1)
                unit(0)
                for u in range(units):
                    if u + 1 < units:
                        unit(u + 1)
                    if u == heads:
                        item("turn_y", 0)
                    mix(u)
                    if u == 2 and has_tail and tail.turned:
                        tail.pe(pe, i - 1)
                item("turn_y", 1)
                item("out", 0)

            pair(0, False)
            with pe.Fori(1, PAIRS) as i:
                pair(i, True)
            if tail.turned:
                tail.pe(pe, PAIRS - 1)

        @block.scalar
        def _(act):
            act.wait_ge(weights_in, 16 * loads)
            act.wait_ge(ready, 1)
            if mamba:
                act.activation(head_cols[:, 1:2], head_cols[:, 1:2], ACT.Exp).then_inc(soft_ready, 1)

            def pair(i, has_tail):
                def take(kind, n):
                    w = index[kind, n]
                    act.wait_ge(up, i * W + w + 1)
                    return work[w % 2], down[w % 2]

                if mamba:
                    bank, sign = take("turn_in", 0)
                    act.activation(in_t[:], bank[:], ACT.Identity, scale=cols[:, 0:1]).then_inc(sign, 1)
                for c in range(CH):
                    bank, sign = take("x", c)
                    act.wait_ge(conv_ready, i * CH)
                    ins = act.activation(padded[:, c, :, TAPS - 1:], bank[:].rearrange("p (j t) -> p j t", j=2),
                                         ACT.Identity)
                    ins.then_inc(sign, 1)
                act.drain()
                act.sem_inc(padded_ready, 1)
                bank, sign = take("dt", 0)
                act.wait_ge(parts_ready, i)
                act.activation(raw[:], bank[0:heads, :], ACT.Identity).then_inc(sign, 1)
                act.drain()
                act.activation(bent[:], raw[:], ACT.Abs, bias=head_cols[:, 0:1])
                if not mamba:
                    act.activation(magnitude[:], raw[:], ACT.Abs)
                act.drain()
                act.activation(bent[:], bent[:], ACT.Exp, scale=-1.0)
                act.drain()
                act.activation(bent[:], bent[:], ACT.Ln, bias=1.0)
                act.drain()
                act.sem_inc(raw_ready, 1)
                for b in range(bc_items):
                    bank, sign = take("bc", b)
                    rows = STATE if mamba else P
                    if b == 0:
                        act.wait_ge(scores_up, i * (2 if mamba else units))
                    act.activation(bc[0:rows, b, :], bank[0:rows, :], ACT.Identity).then_inc(sign, 1)
                for g in range(2):
                    bank, sign = take("gate", g)
                    act.wait_ge(y_taken, 2 * i)
                    act.activation(gate[:, 2 * g:2 * g + 2, :].rearrange("p t c -> p (t c)"), bank[:],
                                   ACT.Silu if mamba else ACT.Sigmoid).then_inc(sign, 1)
                for c in range(CH):
                    act.wait_ge(conv_ready, i * CH + c + 1)
                    flat = conv[:, c].rearrange("p j t -> p (j t)")
                    act.activation(flat, flat, ACT.Silu).then_inc(x_bent, 1)
                for u in range(units):
                    n = i * units + u
                    act.wait_ge(decay_up, n + 1)
                    if not (isinstance(i, int) and u < 2):
                        act.wait_ge(mixer_done, n - 1)
                    act.activation(decay[:, u % 2, :], dbank[u % 2][:, 0:SPAN], ACT.Exp).then_inc(decay_done, 1)
                    if u == heads + 1:
                        turned_y(i, 0)
                    if u == 2 and has_tail and tail.turned:
                        tail.act(act, i - 1)
                turned_y(i, 1)

            def turned_y(i, j):
                w = index["turn_y", j]
                act.wait_ge(up, i * W + w + 1)
                act.activation(gated_t[:, 2 * j:2 * j + 2].rearrange("p t c k -> p (t c k)"), work[w % 2][:],
                               ACT.Identity).then_inc(down[w % 2], 1)

            pair(0, False)
            with act.Fori(1, PAIRS) as i:
                pair(i, True)
            if tail.turned:
                tail.act(act, PAIRS - 1)

        @block.vector
        def _(dve):
            dve.wait_ge(weights_in, 16 * loads)
            dve.wait_ge(ready, 1)
            if mamba:
                dve.wait_ge(soft_ready, 1)
                dve.tensor_scalar(head_cols[:, 1:2], head_cols[:, 1:2], -1.0, None, ALU.mult)
            else:
                for c in range(CH):
                    dve.tensor_scalar(wout[:, c, :], wout[:, c, :], cols[:, c:c + 1], None, ALU.mult)
            dve.drain()
            dve.sem_inc(folded, 1)

            with dve.Fori(0, PAIRS) as i:
                if mamba:
                    rms.find_moments(dve, lambda r: core.normed[:, i * PT + r, :])
                    dve.wait_ge(up, i * W)
                    rms.scale(dve, i, lambda r: scaled[:, r, :],
                              lambda r: core.normed[:, i * PT + r, :]).then_inc(scaled_ready, 1)
                else:
                    dve.wait_ge(up, i * W)
                    dve.tensor_copy(in_rows[:], core.normed_t[:, bass.ds(i * PN, PN)]).then_inc(staged, 1)
                dve.wait_ge(padded_ready, i + 1)
                dve.wait_ge(up, i * W)
                for k in range(TAPS):
                    for c in range(CH):
                        tap = taps[:, c, k:k + 1]
                        shifted = padded[:, c, :, k:k + SEQ]
                        if k == 0:
                            ins = dve.tensor_scalar(conv[:, c], shifted, tap, taps[:, c, TAPS:TAPS + 1],
                                                    ALU.mult, ALU.add)
                        else:
                            ins = dve.scalar_tensor_tensor(conv[:, c], shifted, tap, conv[:, c], ALU.mult, ALU.add)
                        if k == TAPS - 1:
                            ins.then_inc(conv_ready, 1)
                    dve.drain()
                dve.wait_ge(raw_ready, i + 1)
                dve.wait_ge(y_up, i * units)
                dve.tensor_scalar(delta[:], raw[:], head_cols[:, 0:1], 0.0, ALU.add, ALU.max)
                dve.drain()
                dve.tensor_tensor(delta[:], delta[:], bent[:], ALU.add).then_inc(delta_ready, 1)
                dve.drain()
                if mamba:
                    dve.tensor_scalar(logs[:], delta[:], head_cols[:, 1:2], None, ALU.mult)
                else:
                    dve.scalar_tensor_tensor(logs[:], delta[:], -1.0, magnitude[:], ALU.mult, ALU.mult)
                dve.drain()
                for j in range(2):
                    at = slice(j * SEQ, (j + 1) * SEQ)
                    dve.tensor_tensor_scan(cum[:, at], ones_dt[:], logs[:, at], 0.0, ALU.mult, ALU.add)
                dve.drain()
                for part in range(3):
                    dve.tensor_copy(part16[:], cum[:])
                    dve.drain()
                    dve.tensor_copy(parts[32 * part:32 * part + heads, :], part16[:])
                    if part < 2:
                        dve.tensor_tensor(cum[:], cum[:], part16[:], ALU.subtract)
                    dve.drain()
                dve.sem_inc(parts_ready, 1)
                if mamba:
                    w = index["turn_dt", 0]
                    dve.wait_ge(up, i * W + w + 1)
                    dve.tensor_copy(dt_rows[:].rearrange("p t h -> p (t h)"),
                                    work[w % 2][:, 0:PT * heads]).then_inc(down[w % 2], 1)
                    dve.drain()
                for c in range(CH):
                    w = index["turn_x", c]
                    dve.wait_ge(up, i * W + w + 1)
                    out = x_rows[:, :, c * P:(c + 1) * P]
                    bank = work[w % 2][:].rearrange("p (t k) -> p t k", t=PT)
                    if mamba:
                        for t in range(PT):
                            each = heads // CH
                            ins = dve.tensor_tensor(out[:, t].rearrange("p (h d) -> p h d", d=HD),
                                                    bank[:, t].rearrange("p (h d) -> p h d", d=HD),
                                                    dt_rows[:, t, c * each:(c + 1) * each].unsqueeze(2).broadcast_to(
                                                        [P, each, HD]), ALU.mult)
                    else:
                        ins = dve.tensor_copy(out, bank)
                    ins.then_inc(down[w % 2], 1)
                for u in range(units):
                    j, h = divmod(u, heads)
                    n = i * units + u
                    if not mamba:
                        dve.wait_ge(scores_up, n + 1)
                        scored = gbank[u % 2][:, 0:SPAN]
                    elif h == 0:
                        dve.wait_ge(scores_up, i * 2 + j + 1)
                        dve.tensor_copy(scores[:], gbank[0][:, 0:SPAN]).then_inc(scores_taken, 1)
                        dve.drain()
                    if mamba:
                        scored = scores[:]
                    dve.wait_ge(decay_done, n + 1)
                    if u >= 2:
                        dve.wait_ge(y_up, n - 1)
                    ins = dve.tensor_tensor(mixer[:, u % 2, :], decay[:, u % 2, :], scored, ALU.mult)
                    ins.then_inc(mixer_done, 1)
                    if not mamba:
                        dve.drain()
                        dve.sem_inc(scores_taken, 1)
                    if h == heads - 1:
                        dve.wait_ge(y_up, n + 1)
                        dve.tensor_tensor(gated[:, 2 * j:2 * j + 2, :].rearrange("p t c -> p (t c)"), ybank[:],
                                          gate[:, 2 * j:2 * j + 2, :].rearrange("p t c -> p (t c)"),
                                          ALU.mult).then_inc(gated_ready, 1)
                        dve.drain()
                        dve.sem_inc(y_taken, 1)
                w = index["out", 0]
                if not mamba:
                    rms.find_moments(dve, lambda r: gated[:, r, :])
                dve.wait_ge(up, i * W + w + 1)
                bank = work[w % 2]
                if mamba:
                    ins = dve.tensor_tensor(core.branch[:].rearrange("p t c -> p (t c)"), bank[:],
                                            core.normed[:, bass.ds(i * PT, PT), :].rearrange("p t c -> p (t c)"),
                                            ALU.add)
                else:
                    ins = rms.scale(dve, i, lambda r: core.branch[:, r, :], lambda r: bank[:, r * P:(r + 1) * P])
                ins.then_inc(down[w % 2], 1)
                dve.drain()
                tail.dve(dve, i)


class Carry(Tail):

    def dve(self, dve, i):
        core = self.core
        dve.tensor_copy(core.normed[:, bass.ds(i * PT, PT), :], core.branch[:])
        dve.wait_ge(self.fresh_turned, i)
        dve.tensor_copy(core.fresh[:], core.branch[:]).then_inc(self.fresh_ready, 1)
        dve.drain()

    def pool(self, pool, i):
        pass


def local_layer(core, layer, tail):
    nc, dram = core.nc, core.dram
    name = f"local{layer}"
    HEADS, HD = 8, 64
    INNER = HEADS * HD
    CH = INNER // P
    HID = int(C * 4 * 2 / 3)
    FC = -(-HID // P)
    HALF = C // 2
    SPAN = 3 * P
    units = 2 * HEADS
    items = [(kind, t) for t in range(PT) for kind in "qkv"]
    items += [(kind, t) for t in range(PT) for kind in ("turn_q", "turn_k")]
    first_late = len(items)
    items += [("turn_o", t) for t in range(PT)] + [("wo", 0), ("turn_x", 0), ("rows", 0), ("turn_z", 0)]
    items += [(kind, c) for c in range(FC) for kind in ("up_g", "up_a")]
    W = len(items)
    assert W % 2 == 0 and first_late % 2 == 0
    index = {item: w for w, item in enumerate(items)}
    with ExitStack() as ctx:
        sb = lambda n, shape, dtype=F32: core.sb(f"{name}_{n}", shape, dtype, ctx=ctx)
        sem = lambda n: core.sem(f"{name}_{n}")
        wqkv, wo = sb("wqkv", [P, 3 * INNER]), sb("wo", [P, CH, C])
        w1, w2 = sb("w1", [P, FC, 2, P]), sb("w2", [P, FC, C])
        cols, b2 = sb("cols", [P, 2 + 2 * FC]), sb("b2", [1, C])
        tables, scales = sb("tables", [P, 2, 2, 2, HD]), sb("scales", [P, 2, 2, HD])
        ident16, masks = sb("ident16", [P, P], BF16), sb("masks", [P, SPAN], BF16)
        shifted = sb("shifted", [P, 2, SEQ])
        raw = sb("raw", [P, PT, 2, INNER])
        squares, turned_part = sb("squares", [P, 2, INNER]), sb("turned_part", [P, 2, INNER])
        size = sb("size", [P, PT, 2, HEADS])
        qk_t = sb("qk_t", [P, 2, CH, PN])
        values = sb("values", [P, PT, INNER])
        peak, total = sb("peak", [P, 2, 2]), sb("total", [P, PT, HEADS])
        probs, probs_t = sb("probs", [P, 2, SPAN]), sb("probs_t", [P, 2, SPAN])
        mixed, mixed_t = sb("mixed", [P, PT, INNER]), sb("mixed_t", [P, PT, CH, P])
        z, z_t = sb("z", [P, PT, C]), sb("z_t", [P, PN])
        bent, hidden = sb("bent", [P, 2, PN]), sb("hidden", [P, FC, PN])
        norm = Norm(core, f"{name}_norm", PT, core.eps, core.norm_buffers(f"{name}_norm", PT, ctx))
        weights_in = sem("weights_in")
        up, down = sem("up"), [sem("down_even"), sem("down_odd")]
        shifted_ready, squared, sized, rooted = sem("shifted_ready"), sem("squared"), sem("sized"), sem("rooted")
        part_ready, part_used, rotated = sem("part_ready"), sem("part_used"), sem("rotated")
        tables_ready, part_asked = sem("tables_ready"), sem("part_asked")
        scores_up, peaked, probs_done = sem("scores_up"), sem("peaked"), sem("probs_done")
        probs_turned, probs_t_done = sem("probs_turned"), sem("probs_t_done")
        o_up, mixed_ready = sem("o_up"), sem("mixed_ready")
        x1_ready, z_ready = sem("x1_ready"), sem("z_ready")
        hidden_ready, out_up, out_taken = sem("hidden_ready"), sem("out_up"), sem("out_taken")
        work, pbank, obank, fbank = core.bank[0:2], [core.bank[2], core.bank[5]], core.bank[3:5], core.bank[6]
        widths = [min(P, HID - c * P) for c in range(FC)]
        loads = 10
        block = ctx.enter_context(nc.Block())

        @block.sync
        def _(sp):
            for to, what in ((wqkv, "wqkv"), (wo, "wo"), (w1, "w1"), (w2, "w2"), (cols, "cols"), (b2, "b2")):
                sp.dma_start(to[:], dram[f"{name}_{what}"]).then_inc(weights_in, 16)
            sp.dma_start(tables[:], dram["rotary"]).then_inc(weights_in, 16)
            sp.dma_start(scales[:].rearrange("p a b d -> p (a b d)"),
                         dram[f"{name}_scales"].partition_broadcast(P)).then_inc(weights_in, 16)
            sp.dma_start(ident16[:], dram["identity16"]).then_inc(weights_in, 16)
            sp.dma_start(masks[:], dram["window"]).then_inc(weights_in, 16)

        @block.tensor
        def _(pe):
            pe.wait_ge(weights_in, 16 * loads)

            def pair(i, has_tail):
                ht = shifted[:].rearrange("p j t -> p (j t)")

                def done(kind, n):
                    w = index[kind, n]
                    pe.wait_ge(down[w % 2], i * (W // 2) + w // 2 + 1)

                def item(kind, n):
                    w = index[kind, n]
                    if not (isinstance(i, int) and w < 2):
                        pe.wait_ge(down[w % 2], i * (W // 2) + w // 2)
                    bank = work[w % 2]
                    if kind in ("q", "k", "v"):
                        part = "qkv".index(kind)
                        last = pe.matmul(bank[:], ht[:, n * P:(n + 1) * P], wqkv[:, part * INNER:(part + 1) * INNER],
                                         start=True, stop=True)
                    elif kind in ("turn_q", "turn_k"):
                        part = int(kind == "turn_k")
                        pe.wait_ge(rotated, i * 2 * PT + 2 * n + part + 1)
                        for c in range(CH):
                            last = pe.transpose(bank[:, c * P:(c + 1) * P], raw[:, n, part, c * P:(c + 1) * P],
                                                core.ident[:])
                    elif kind == "turn_o":
                        pe.wait_ge(mixed_ready, i * PT + n + 1)
                        for c in range(CH):
                            last = pe.transpose(bank[:, c * P:(c + 1) * P], mixed[:, n, c * P:(c + 1) * P],
                                                core.ident[:])
                    elif kind == "wo":
                        for t in range(PT):
                            done("turn_o", t)
                        for t in range(PT):
                            for c in range(CH):
                                last = pe.matmul(bank[:, t * P:(t + 1) * P], mixed_t[:, t, c, :], wo[:, c, :],
                                                 start=(c == 0), stop=(c == CH - 1))
                    elif kind == "turn_x":
                        pe.wait_ge(x1_ready, i + 1)
                        for t in range(PT):
                            last = pe.transpose(bank[:, t * P:(t + 1) * P], x1[:, t, :], core.ident[:])
                    elif kind == "rows":
                        done("turn_x", 0)
                        for t in range(PT):
                            last = pe.transpose(bank[:, t * P:(t + 1) * P], ht[:, t * P:(t + 1) * P], core.ident[:])
                    elif kind == "turn_z":
                        pe.wait_ge(z_ready, i + 1)
                        for t in range(PT):
                            last = pe.transpose(bank[:, t * P:(t + 1) * P], z[:, t, :], core.ident[:])
                    else:
                        if kind == "up_g" and n == 0:
                            done("turn_z", 0)
                        last = pe.matmul(bank[0:widths[n], :], w1[:, n, int(kind == "up_g"), 0:widths[n]], z_t[:],
                                         start=True, stop=True)
                    last.then_inc(up, 1)

                x1 = core.branch
                pe.wait_ge(shifted_ready, i + 1)
                for kind, n in items[:first_late]:
                    item(kind, n)
                for t in (PT - 1,):
                    done("turn_q", t)
                    done("turn_k", t)

                def scores(u):
                    j, h = divmod(u, HEADS)
                    n = i * units + u
                    low = HD * (h % 2)
                    q, k = (qk_t[low:low + HD, part, h // 2, j * SEQ:(j + 1) * SEQ] for part in (0, 1))
                    bank = work[u % 2]
                    if u >= 2:
                        pe.wait_ge(probs_done, n - 1)
                    pe.matmul(bank[:, 0:P], q[:, 0:P], k[:, 0:P], start=True, stop=False)
                    pe.matmul(bank[:, 0:P], ident16[:], masks[:, 0:P], start=False, stop=True)
                    pe.matmul(bank[:, P:SPAN], q[:, P:SEQ], k[:], start=True, stop=False)
                    pe.matmul(bank[:, P:SPAN], ident16[:], masks[:, P:SPAN], start=False, stop=True).then_inc(
                        scores_up, 1)

                def turn(u):
                    n = i * units + u
                    pe.wait_ge(probs_done, n + 1)
                    if not (isinstance(i, int) and u < 2):
                        pe.wait_ge(probs_t_done, n - 1)
                    for b in range(3):
                        last = pe.transpose(pbank[u % 2][:, b * P:(b + 1) * P], probs[:, u % 2, b * P:(b + 1) * P],
                                            core.ident[:])
                    last.then_inc(probs_turned, 1)

                def mix(u):
                    j, h = divmod(u, HEADS)
                    n = i * units + u
                    pe.wait_ge(probs_t_done, n + 1)
                    if h == 0 and not (isinstance(i, int) and j == 0):
                        pe.wait_ge(mixed_ready, i * PT + 2 * j)
                    p = probs_t[:, u % 2, :]
                    at = slice(h * HD, (h + 1) * HD)
                    v = [values[:, 2 * j + t, at] for t in range(2)]
                    pe.matmul(obank[0][:, at], p[:, 0:P], v[0], start=True, stop=True)
                    pe.matmul(obank[1][:, at], p[:, P:2 * P], v[0], start=True, stop=False)
                    pe.matmul(obank[1][:, at], p[:, 2 * P:SPAN], v[1], start=False, stop=True).then_inc(o_up, 1)

                scores(0)
                scores(1)
                turn(0)
                for u in range(units):
                    if u + 2 < units:
                        scores(u + 2)
                    if u + 1 < units:
                        turn(u + 1)
                    mix(u)
                    if u == 2 and has_tail:
                        tail.pe(pe, i - 1)
                for kind, n in items[first_late:]:
                    item(kind, n)
                pe.wait_ge(out_taken, i)
                pe.wait_ge(hidden_ready, (i + 1) * FC)
                for t in range(PT):
                    for c in range(FC):
                        k = widths[c]
                        pe.matmul(fbank[:, t * P:(t + 1) * P], hidden[0:k, c, t * P:(t + 1) * P], w2[0:k, c, :],
                                  start=(c == 0), stop=False)
                    last = pe.matmul(fbank[:, t * P:(t + 1) * P], core.ones_row[:], b2[:], start=False, stop=True)
                last.then_inc(out_up, 1)

            pair(0, False)
            with pe.Fori(1, PAIRS) as i:
                pair(i, True)
            tail.pe(pe, PAIRS - 1)

        @block.scalar
        def _(act):
            act.wait_ge(weights_in, 16 * loads)

            def pair(i, has_tail):
                def take(kind, n):
                    w = index[kind, n]
                    act.wait_ge(up, i * W + w + 1)
                    return work[w % 2], down[w % 2]

                for t in range(PT):
                    for part, kind in enumerate("qk"):
                        bank, sign = take(kind, t)
                        act.activation(raw[:, t, part, :], bank[:], ACT.Identity).then_inc(sign, 1)
                    bank, sign = take("v", t)
                    if t == 0:
                        act.wait_ge(o_up, i * units)
                    act.activation(values[:, t, :], bank[:], ACT.Identity).then_inc(sign, 1)
                act.wait_ge(sized, i + 1)
                act.activation(size[:], size[:], ACT.Sqrt).then_inc(rooted, 1)
                for t in range(PT):
                    for part, kind in enumerate(("turn_q", "turn_k")):
                        bank, sign = take(kind, t)
                        act.activation(qk_t[:, part, :, t * P:(t + 1) * P],
                                       bank[:].rearrange("p (c k) -> p c k", c=CH), ACT.Identity).then_inc(sign, 1)
                for u in range(units):
                    n = i * units + u
                    j, h = divmod(u, HEADS)
                    act.wait_ge(peaked, n + 1)
                    if not (isinstance(i, int) and u < 2):
                        act.wait_ge(probs_turned, n - 1)
                    for t, at in enumerate((slice(0, P), slice(P, SPAN))):
                        last = act.activation(probs[:, u % 2, at], work[u % 2][:, at], ACT.Exp,
                                              bias=peak[:, u % 2, t:t + 1], accum_out=total[:, 2 * j + t, h:h + 1])
                    last.then_inc(probs_done, 1)
                    if u == 3 and has_tail:
                        tail.act(act, i - 1)
                for t in range(PT):
                    bank, sign = take("turn_o", t)
                    act.activation(mixed_t[:, t].rearrange("p c k -> p (c k)"), bank[:], ACT.Identity).then_inc(sign, 1)
                bank, sign = take("turn_x", 0)
                by_seq = bank[:].rearrange("p (j t) -> p j t", j=2)
                act.activation(shifted[0:HALF], by_seq[0:HALF], ACT.Identity)
                act.activation(shifted[HALF:C, :, 1:SEQ], by_seq[HALF:C, :, 0:SEQ - 1], ACT.Identity)
                act.drain()
                act.sem_inc(sign, 1)
                bank, sign = take("turn_z", 0)
                act.activation(z_t[:], bank[:], ACT.Identity, bias=cols[:, 1:2], scale=cols[:, 0:1]).then_inc(sign, 1)
                for c in range(FC):
                    k = widths[c]
                    bank, sign = take("up_g", c)
                    if not (isinstance(i, int) and c < 2):
                        act.wait_ge(hidden_ready, i * FC + c - 1 if c >= 1 else i * FC)
                    act.activation(bent[0:k, c % 2, :], bank[0:k, :], ACT.Gelu,
                                   bias=cols[0:k, 2 + FC + c:3 + FC + c]).then_inc(sign, 1)

            pair(0, False)
            with act.Fori(1, PAIRS) as i:
                pair(i, True)
            tail.act(act, PAIRS - 1)

        @block.gpsimd
        def _(pool):
            pool.wait_ge(tables_ready, 1)
            with pool.Fori(0, PAIRS) as i:
                for t in range(PT):
                    for part, kind in enumerate("qk"):
                        n = 2 * t + part
                        w = index[kind, t]
                        pool.wait_ge(down[w % 2], i * (W // 2) + w // 2 + 1)
                        if n >= 2:
                            pool.wait_ge(part_asked, i * 2 * PT + n - 1)
                        pool.tensor_tensor(squares[:, n % 2, :], raw[:, t, part, :], raw[:, t, part, :],
                                           ALU.mult).then_inc(squared, 1)
                for t in range(PT):
                    for part in range(2):
                        n = 2 * t + part
                        if n >= 2:
                            pool.wait_ge(rotated, i * 2 * PT + n - 1)
                        else:
                            pool.wait_ge(part_asked, (i + 1) * 2 * PT)
                        rows = raw[:, t, part, :].rearrange("p (h s d) -> p h s d", s=2, d=HD // 2)[:, :, ::-1, :]
                        sines = tables[:, part, t % 2, 1, :].rearrange("p (s d) -> p s d", s=2).unsqueeze(1)
                        pool.tensor_tensor(
                            turned_part[:, n % 2, :].rearrange("p (h s d) -> p h s d", s=2, d=HD // 2), rows,
                            sines.broadcast_to([P, HEADS, 2, HD // 2]), ALU.mult).then_inc(part_ready, 1)
                norm.power(pool, i)
                tail.pool(pool, i)

        @block.vector
        def _(dve):
            dve.wait_ge(weights_in, 16 * loads)
            dve.memset(shifted[:], 0.0)
            for part in range(2):
                for t in range(2):
                    dve.tensor_tensor(tables[:, part, t], tables[:, part, t], scales[:, part], ALU.mult)
            dve.drain()
            dve.sem_inc(tables_ready, 1)

            with dve.Fori(0, PAIRS) as i:
                source = core.normed_t[:, bass.ds(i * PN, PN)].rearrange("p (j t) -> p j t", j=2)
                dve.wait_ge(up, i * W)
                dve.tensor_copy(shifted[0:HALF], source[0:HALF])
                dve.tensor_copy(shifted[HALF:C, :, 1:SEQ], source[HALF:C, :, 0:SEQ - 1])
                dve.drain()
                dve.sem_inc(shifted_ready, 1)
                for t in range(PT):
                    for part in range(2):
                        n = 2 * t + part
                        dve.wait_ge(squared, i * 2 * PT + n + 1)
                        dve.tensor_reduce(size[:, t, part, :],
                                          squares[:, n % 2, :].rearrange("p (h d) -> p h d", d=HD),
                                          AX.X, ALU.add).then_inc(part_asked, 1)
                dve.drain()
                dve.tensor_scalar(size[:], size[:], 1e-24, None, ALU.max)
                dve.drain()
                dve.sem_inc(sized, 1)
                dve.wait_ge(rooted, i + 1)
                dve.reciprocal(size[:], size[:])
                for t in range(PT):
                    for part in range(2):
                        n = 2 * t + part
                        rows = raw[:, t, part, :]
                        by_head = rows.rearrange("p (h d) -> p h d", d=HD)
                        dve.wait_ge(part_ready, i * 2 * PT + n + 1)
                        dve.tensor_tensor(by_head, by_head, tables[:, part, t % 2, 0, :].unsqueeze(1).broadcast_to(
                            [P, HEADS, HD]), ALU.mult)
                        dve.drain()
                        dve.tensor_tensor(rows, rows, turned_part[:, n % 2, :], ALU.add)
                        dve.drain()
                        dve.tensor_tensor(by_head, by_head, size[:, t, part, :].unsqueeze(2).broadcast_to(
                            [P, HEADS, HD]), ALU.mult).then_inc(rotated, 1)

                def peak_of(u):
                    dve.wait_ge(scores_up, i * units + u + 1)
                    for t, at in enumerate((slice(0, P), slice(P, SPAN))):
                        dve.tensor_reduce(peak[:, u % 2, t:t + 1], work[u % 2][:, at], AX.X, ALU.max, negate=True)
                    dve.drain()
                    dve.sem_inc(peaked, 1)

                peak_of(0)
                for u in range(units):
                    j, h = divmod(u, HEADS)
                    if u + 1 < units:
                        peak_of(u + 1)
                    dve.wait_ge(probs_turned, i * units + u + 1)
                    if u >= 2:
                        dve.wait_ge(o_up, i * units + u - 1)
                    dve.tensor_copy(probs_t[:, u % 2, :], pbank[u % 2][:, 0:SPAN]).then_inc(probs_t_done, 1)
                    if h == HEADS - 1:
                        dve.wait_ge(probs_done, i * units + u + 1)
                        dve.reciprocal(total[:, 2 * j:2 * j + 2, :], total[:, 2 * j:2 * j + 2, :])
                        dve.drain()
                        dve.wait_ge(o_up, i * units + u + 1)
                        for t in range(2):
                            dve.tensor_tensor(mixed[:, 2 * j + t, :].rearrange("p (h d) -> p h d", d=HD),
                                              obank[t][:].rearrange("p (h d) -> p h d", d=HD),
                                              total[:, 2 * j + t, :].unsqueeze(2).broadcast_to([P, HEADS, HD]),
                                              ALU.mult).then_inc(mixed_ready, 1)
                w = index["wo", 0]
                dve.wait_ge(up, i * W + w + 1)
                dve.tensor_tensor(core.branch[:].rearrange("p t c -> p (t c)"), work[w % 2][:],
                                  core.normed[:, bass.ds(i * PT, PT), :].rearrange("p t c -> p (t c)"), ALU.add)
                dve.drain()
                dve.sem_inc(x1_ready, 1)
                dve.sem_inc(down[w % 2], 1)
                w = index["rows", 0]
                dve.wait_ge(up, i * W + w + 1)
                norm.find_moments(dve, lambda r: work[w % 2][:, r * P:(r + 1) * P])
                norm.apply(dve, i, lambda r: z[:, r, :], lambda r: work[w % 2][:, r * P:(r + 1) * P])
                dve.drain()
                dve.sem_inc(z_ready, 1)
                dve.sem_inc(down[w % 2], 1)
                for c in range(FC):
                    k = widths[c]
                    w = index["up_a", c]
                    dve.wait_ge(up, i * W + w + 1)
                    wg = index["up_g", c]
                    dve.wait_ge(down[wg % 2], i * (W // 2) + wg // 2 + 1)
                    dve.scalar_tensor_tensor(hidden[0:k, c, :], work[w % 2][0:k, :], cols[0:k, 2 + c:3 + c],
                                             bent[0:k, c % 2, :], ALU.add, ALU.mult)
                    dve.drain()
                    dve.sem_inc(down[w % 2], 1)
                    dve.sem_inc(hidden_ready, 1)
                dve.wait_ge(out_up, i + 1)
                flat = core.branch[:].rearrange("p t c -> p (t c)")
                dve.tensor_tensor(flat, fbank[:], flat, ALU.add)
                dve.drain()
                dve.sem_inc(out_taken, 1)
                tail.dve(dve, i)


def wave_block(core, tail):
    nc, dram = core.nc, core.dram
    name = "wave"
    HEADS = 16
    HD = C // HEADS
    TWO_PI = 2.0 * np.pi
    PI1 = 6.28125
    PI2 = float(np.float32(np.round((TWO_PI - PI1) * 2 ** 22) / 2 ** 22))
    PI3 = float(TWO_PI - PI1 - PI2)
    ROUNDER = 1.5 * 2.0 ** 23
    kernel_rows = nc.dram_tensor("wave_kernel_rows", (HEADS, P + SEQ), F32, kind="Internal").ap()
    with ExitStack() as ctx:
        sb = lambda n, shape, dtype=F32: core.sb(f"{name}_{n}", shape, dtype, ctx=ctx)
        sem = lambda n: core.sem(f"{name}_{n}")
        w, wout, bout = sb("w", [P, 4, C]), sb("wout", [P, C]), sb("bout", [1, C])
        cols, params, time = sb("cols", [P, 4]), sb("params", [HEADS, 4]), sb("time", [HEADS, SEQ])
        coupling, coupling_wide = sb("coupling", [HEADS, HEADS]), sb("coupling_wide", [HEADS, HEADS, HD])
        spread, same = sb("spread", [HEADS, P]), sb("same", [P, P])
        coupler = sb("coupler", [P, P])
        stat = sb("stat", [HEADS, 4])
        phase, turns = sb("phase", [HEADS, SEQ]), sb("turns", [HEADS, SEQ])
        fade, padded = sb("fade", [HEADS, SEQ]), sb("padded", [HEADS, P + SEQ])
        toeplitz = sb("toeplitz", [P, HEADS, SEQ])
        field, waves = sb("field", [P, TILES, C]), sb("waves", [P, TILES, C])
        query = sb("query", [P, SEQS, SEQ])
        ex, pos = sb("ex", [P, 2, PN]), sb("pos", [P, 2, PN])
        gate, deposit = sb("gate", [P, PN]), sb("deposit", [P, PT, P])
        staged, wave_t, mixed = sb("staged", [P, PT, C]), sb("wave_t", [P, PN]), sb("mixed", [P, 2, SEQ])
        weights_in, params_in = sem("weights_in"), sem("params_in")
        exp_asked, exp_done = sem("exp_asked"), sem("exp_done")
        kernel_ready, kernel_out, toeplitz_in = sem("kernel_ready"), sem("kernel_out"), sem("toeplitz_in")
        wide_ready, coupler_up, coupler_ready = sem("wide_ready"), sem("coupler_up"), sem("coupler_ready")
        up, bent, taken = sem("up"), sem("bent"), sem("taken")
        deposit_ready, field_up, field_down = sem("deposit_ready"), sem("field_up"), sem("field_down")
        wave_up, wave_down = sem("wave_up"), [sem("wave_down_even"), sem("wave_down_odd")]
        staged_ready, turned, wave_t_ready = sem("staged_ready"), sem("turned"), sem("wave_t_ready")
        coupled, mixed_ready, out_up, out_taken = sem("coupled"), sem("mixed_ready"), sem("out_up"), sem("out_taken")
        loads = 6
        block = ctx.enter_context(nc.Block())

        by_seq = waves[:].rearrange("p (b h) c -> p h b c", h=2)

        def take_waves(eng, odd):
            for h in range(odd, HEADS, 2):
                eng.wait_ge(wave_up, h + 1)
                bank = core.bank[5 + h % 2][:, 0:2 * P].rearrange("p (t b d) -> p t b d", t=2, d=HD)
                out = by_seq[:, :, :, h * HD:(h + 1) * HD]
                (eng.activation(out, bank, ACT.Identity) if odd else eng.tensor_copy(out, bank)).then_inc(
                    wave_down[h % 2], 1)

        @block.sync
        def _(sp):
            sp.dma_start(params[:], dram["wave_params"]).then_inc(params_in, 16)
            sp.dma_start(time[:], dram["wave_time"]).then_inc(params_in, 16)
            sp.dma_start(coupling[:], dram["wave_coupling"]).then_inc(params_in, 16)
            for to, what in ((w, "w"), (cols, "cols"), (spread, "spread"), (same, "same"), (wout, "wout"),
                             (bout, "bout")):
                sp.dma_start(to[:], dram[f"wave_{what}"]).then_inc(weights_in, 16)
            sp.wait_ge(kernel_ready, 1)
            sp.dma_start(kernel_rows, padded[:]).then_inc(kernel_out, 16)
            sp.wait_ge(kernel_out, 16)
            shifted = bass.AP(tensor=kernel_rows.tensor, offset=1, ap=[[1, P], [P + SEQ, HEADS], [1, SEQ]])
            sp.dma_start(toeplitz[:], shifted).then_inc(toeplitz_in, 16)

        @block.scalar
        def _(act):
            act.wait_ge(params_in, 48)
            act.activation(stat[:, 0:1], params[:, 1:2], ACT.Abs)
            act.drain()
            act.activation(stat[:, 0:1], stat[:, 0:1], ACT.Exp, scale=-1.0)
            act.drain()
            act.activation(stat[:, 0:1], stat[:, 0:1], ACT.Ln, bias=1.0).then_inc(exp_done, 1)
            act.wait_ge(exp_asked, 1)
            act.activation(fade[:], time[:], ACT.Exp, scale=stat[:, 1:2])
            act.activation(coupling[:], coupling[:], ACT.Exp)
            act.activation(turns[:], phase[:], ACT.Sin, scale=0.5)
            act.drain()
            act.sem_inc(exp_done, 1)
            act.wait_ge(weights_in, 16 * loads)
            with act.Fori(0, PAIRS) as i:
                for part in range(2):
                    act.wait_ge(up, i * 4 + part + 1)
                    act.wait_ge(taken, i * 4)
                    act.activation(ex[:, part, :], core.bank[part][:], ACT.Exp, bias=cols[:, part:part + 1])
                act.drain()
                act.sem_inc(bent, 1)
                act.wait_ge(up, i * 4 + 4)
                act.activation(gate[:], core.bank[3][:], ACT.Sigmoid, bias=cols[:, 3:4])
                act.drain()
                act.sem_inc(bent, 1)
                act.wait_ge(field_up, i + 1)
                act.activation(field[:, bass.ds(i * PT, PT), :].rearrange("p t c -> p (t c)"), core.bank[4][:],
                               ACT.Identity).then_inc(field_down, 1)
            take_waves(act, 1)

            def pair(i, has_tail):
                act.wait_ge(turned, i + 1)
                act.activation(wave_t[:], core.bank[0][:], ACT.Identity).then_inc(wave_t_ready, 1)
                if has_tail:
                    tail.act(act, i - 1)

            pair(0, False)
            with act.Fori(1, PAIRS) as i:
                pair(i, True)
            tail.act(act, PAIRS - 1)

        @block.tensor
        def _(pe):
            pe.wait_ge(weights_in, 16 * loads)
            pe.wait_ge(wide_ready, 1)
            pe.matmul(core.bank[6][:, 0:P], coupling_wide[:].rearrange("i j d -> i (j d)"), spread[:],
                      start=True, stop=True).then_inc(coupler_up, 1)
            with pe.Fori(0, PAIRS) as i:
                pe.wait_ge(taken, i * 4)
                pe.wait_ge(bent, i * 2)
                for part in range(4):
                    pe.matmul(core.bank[part][:], w[:, part, :], core.normed_t[:, bass.ds(i * PN, PN)],
                              start=True, stop=True).then_inc(up, 1)
                pe.wait_ge(deposit_ready, i + 1)
                pe.wait_ge(field_down, i)
                for t in range(PT):
                    last = pe.transpose(core.bank[4][:, t * P:(t + 1) * P], deposit[:, t, :], core.ident[:])
                last.then_inc(field_up, 1)
            pe.wait_ge(toeplitz_in, 16)
            pe.wait_ge(field_down, PAIRS)
            pe.wait_ge(coupler_ready, 1)
            halves = field[:].rearrange("p (b h) c -> p h b c", h=2)
            for h in range(HEADS):
                bank = core.bank[5 + h % 2]
                if h >= 2:
                    pe.wait_ge(wave_down[h % 2], h // 2)
                cells = [halves[:, s, :, h * HD:(h + 1) * HD] for s in range(2)]
                near, far = toeplitz[:, h, 0:P], toeplitz[:, h, P:SEQ]
                pe.matmul(bank[:, 0:P], near, cells[0], start=True, stop=True)
                pe.matmul(bank[:, P:2 * P], far, cells[0], start=True, stop=False)
                pe.matmul(bank[:, P:2 * P], near, cells[1], start=False, stop=True).then_inc(wave_up, 1)

            def pair(i, has_tail):
                pe.wait_ge(staged_ready, i + 1)
                pe.wait_ge(wave_t_ready, i)
                for t in range(PT):
                    last = pe.transpose(core.bank[0][:, t * P:(t + 1) * P], staged[:, t, :], core.ident[:])
                last.then_inc(turned, 1)
                if has_tail:
                    tail.pe(pe, i - 1)
                pe.wait_ge(wave_t_ready, i + 1)
                pe.wait_ge(mixed_ready, i)
                pe.matmul(core.bank[1][:], coupler[:], wave_t[:], start=True, stop=True).then_inc(coupled, 1)
                pe.wait_ge(mixed_ready, i + 1)
                pe.wait_ge(out_taken, i)
                flat = mixed[:].rearrange("p j t -> p (j t)")
                for t in range(PT):
                    pe.matmul(core.bank[2][:, t * P:(t + 1) * P], flat[:, t * P:(t + 1) * P], wout[:],
                              start=True, stop=False)
                    last = pe.matmul(core.bank[2][:, t * P:(t + 1) * P], core.ones_row[:], bout[:],
                                     start=False, stop=True)
                last.then_inc(out_up, 1)

            pair(0, False)
            with pe.Fori(1, PAIRS) as i:
                pair(i, True)
            tail.pe(pe, PAIRS - 1)

        @block.gpsimd
        def _(pool):
            pool.wait_ge(wave_down[0], HEADS // 2)
            pool.wait_ge(wave_down[1], HEADS // 2)
            with pool.Fori(0, PAIRS) as i:
                pool.wait_ge(turned, i)
                pool.tensor_copy(staged[:], waves[:, bass.ds(i * PT, PT), :]).then_inc(staged_ready, 1)
                tail.pool(pool, i)

        @block.vector
        def _(dve):
            dve.wait_ge(params_in, 48)
            dve.wait_ge(exp_done, 1)
            dve.tensor_scalar(stat[:, 1:2], params[:, 1:2], 0.0, None, ALU.max)
            dve.drain()
            dve.tensor_tensor(stat[:, 1:2], stat[:, 1:2], stat[:, 0:1], ALU.add)
            dve.tensor_scalar(phase[:], time[:], params[:, 0:1], params[:, 2:3], ALU.mult, ALU.add)
            dve.drain()
            dve.tensor_scalar(stat[:, 1:2], stat[:, 1:2], -1.0, None, ALU.mult)
            dve.tensor_scalar(turns[:], phase[:], float(1.0 / TWO_PI), ROUNDER, ALU.mult, ALU.add)
            dve.drain()
            dve.tensor_scalar(turns[:], turns[:], ROUNDER, None, ALU.subtract)
            dve.drain()
            for part in (PI1, PI2, PI3):
                dve.scalar_tensor_tensor(phase[:], turns[:], -part, phase[:], ALU.mult, ALU.add)
                dve.drain()
            dve.tensor_reduce(stat[:, 2:3], coupling[:], AX.X, ALU.max)
            dve.drain()
            dve.tensor_scalar(coupling[:], coupling[:], stat[:, 2:3], None, ALU.subtract)
            dve.drain()
            dve.sem_inc(exp_asked, 1)
            dve.wait_ge(exp_done, 2)
            dve.tensor_tensor(turns[:], turns[:], turns[:], ALU.mult)
            dve.memset(padded[:], 0.0)
            dve.tensor_reduce(stat[:, 2:3], coupling[:], AX.X, ALU.add)
            dve.drain()
            dve.tensor_scalar(turns[:], turns[:], -2.0, 1.0, ALU.mult, ALU.add)
            dve.reciprocal(stat[:, 3:4], stat[:, 2:3])
            dve.drain()
            dve.tensor_tensor(fade[:], fade[:], turns[:], ALU.mult)
            dve.tensor_scalar(coupling[:], coupling[:], stat[:, 3:4], None, ALU.mult)
            dve.drain()
            dve.tensor_reduce(stat[:, 2:3], fade[:], AX.X, ALU.add, apply_absolute_value=True)
            dve.tensor_copy(coupling_wide[:], coupling[:].unsqueeze(2).broadcast_to([HEADS, HEADS, HD])).then_inc(
                wide_ready, 1)
            dve.drain()
            dve.tensor_scalar(stat[:, 2:3], stat[:, 2:3], 1e-8, None, ALU.max)
            dve.drain()
            dve.reciprocal(stat[:, 3:4], stat[:, 2:3])
            dve.drain()
            dve.tensor_scalar(padded[:, P:], fade[:], stat[:, 3:4], None, ALU.mult).then_inc(kernel_ready, 1)
            dve.wait_ge(weights_in, 16 * loads)
            dve.wait_ge(coupler_up, 1)
            dve.tensor_tensor(coupler[:], core.bank[6][:, 0:P], same[:], ALU.mult).then_inc(coupler_ready, 1)
            with dve.Fori(0, PAIRS) as i:
                dve.wait_ge(bent, i * 2 + 1)
                for part in range(2):
                    dve.tensor_scalar(pos[:, part, :], core.bank[part][:], cols[:, part:part + 1], 0.0,
                                      ALU.add, ALU.max)
                dve.drain()
                for part in range(2):
                    dve.scalar_tensor_tensor(pos[:, part, :], ex[:, part, :], 1.0, pos[:, part, :], ALU.min, ALU.add)
                dve.drain()
                dve.wait_ge(up, i * 4 + 3)
                dve.wait_ge(field_up, i)
                latest_first = lambda ap: ap.rearrange("p (t k) -> p t k", k=P)[:, :, ::-1]
                dve.scalar_tensor_tensor(deposit[:], latest_first(core.bank[2][:]), cols[:, 2:3],
                                         latest_first(pos[:, 1, :]), ALU.add, ALU.mult)
                dve.drain()
                ends = deposit[:].rearrange("p (j h) k -> p j h k", h=2)[:, :, 1, 0:2]
                dve.tensor_tensor(ends[:, :, 1], ends[:, :, 1], ends[:, :, 0], ALU.add)
                dve.drain()
                dve.memset(ends[:, :, 0:1], 0.0)
                dve.drain()
                dve.sem_inc(deposit_ready, 1)
                dve.wait_ge(bent, i * 2 + 2)
                dve.tensor_tensor(query[:, bass.ds(i * 2, 2), :], pos[:, 0, :].rearrange("p (j t) -> p j t", j=2),
                                  gate[:].rearrange("p (j t) -> p j t", j=2), ALU.mult)
                dve.drain()
                dve.sem_inc(taken, 4)
            take_waves(dve, 0)
            with dve.Fori(0, PAIRS) as i:
                dve.wait_ge(coupled, i + 1)
                dve.wait_ge(out_up, i)
                coupled_rows = core.bank[1][:].rearrange("p (j t) -> p j t", j=2)
                dve.tensor_tensor(mixed[:, :, 0:SEQ - 1], coupled_rows[:, :, 0:SEQ - 1],
                                  query[:, bass.ds(i * 2, 2), 0:SEQ - 1], ALU.mult)
                dve.tensor_tensor(mixed[:, :, SEQ - 1], coupled_rows[:, :, SEQ - 2],
                                  query[:, bass.ds(i * 2, 2), SEQ - 1], ALU.mult)
                dve.drain()
                dve.sem_inc(mixed_ready, 1)
                dve.wait_ge(out_up, i + 1)
                dve.tensor_copy(core.branch[:].rearrange("p t c -> p (t c)"), core.bank[2][:])
                dve.drain()
                dve.sem_inc(out_taken, 1)
                tail.dve(dve, i)


def rwkv_block(core, tail, x_dram):
    nc, dram = core.nc, core.dram
    name = "rwkv"
    HD = 8
    PH = 2
    PC = PH * HD
    GROUPS = C // PC
    ST = PH * HD * HD
    DECAY = float(np.exp(-0.5))
    g_rows = nc.dram_tensor("rwkv_g_rows", (PAIRS, P, PN), F32, kind="Internal").ap()
    decays = core.x[:].rearrange("p t c -> p (t c)").rearrange("p (c t) -> p c t", c=PC)
    rates = core.normed_t[:].rearrange("p (c t) -> p c t", c=PC)
    with ExitStack() as ctx:
        sb = lambda n, shape, dtype=F32, c=ctx: core.sb(f"{name}_{n}", shape, dtype, ctx=c)
        sem = lambda n: core.sem(f"{name}_{n}")
        recv, keys, values, removal = (sb(n, [P, PC, SEQ]) for n in ("recv", "keys", "values", "removal"))
        arrays_in = sem("arrays_in")
        arrays = (recv, decays, keys, values, removal, rates)

        with ExitStack() as inner:
            isb = lambda n, shape, dtype=F32: core.sb(f"{name}_{n}", shape, dtype, ctx=inner)
            pre = Norm(core, "rwkv_pre", PT, core.eps, core.norm_buffers("rwkv_pre", PT, inner))
            attn = TurnedNorm(core, "rwkv_attn", inner, core.bank[3])
            rows, pre_rows = isb("rows", [P, PT, C]), isb("pre_rows", [P, 2, C])
            cols = isb("cols", [P, 12])
            wide = isb("wide", [P, 5, C])
            low = isb("low", [P, 2, C // 2])
            high = isb("high", [C // 2, 2, C])
            padded = isb("padded", [P, 2, SEQ + 1])
            delta, mix = isb("delta", [P, 2, SEQ]), isb("mix", [P, 6, 2, SEQ])
            bent_low, bent_g = isb("bent_low", [C // 2, 2, PN]), isb("bent_g", [P, PN])
            k_raw, g_out, lift = isb("k_raw", [P, PN]), isb("g_out", [P, PN]), isb("lift", [P, PN])
            sent = [isb(f"sent_{n}", [P, 2, SEQ]) for n in ("r", "d", "k", "v", "kk", "a")]
            r_t, d_t, k_t, v_t, kk_t, a_t = (s[:].rearrange("p j t -> p (j t)") for s in sent)
            weights_in = sem("weights_in")
            padded_ready, mix_ready, up = sem("padded_ready"), sem("mix_ready"), sem("up")
            down = [sem(f"down_{b}") for b in range(3)]
            low_ready = [sem("low_w_ready"), sem("low_a_ready"), sem("low_g_ready")]
            a_ready, act_ready, dve_ready, g_ready = sem("a_ready"), sem("act_ready"), sem("dve_ready"), sem("g_ready")
            g_stored = sem("g_stored")
            items = ["w1", "a1", "g1", "k", "a2", "w2", "r", "v", "g2"]
            NB = 3
            W = len(items)
            index = {kind: w for w, kind in enumerate(items)}
            block = inner.enter_context(nc.Block())

            @block.sync
            def _(sp):
                for to, what in ((cols, "cols"), (wide, "wide"), (low, "low"), (high, "high")):
                    sp.dma_start(to[:], dram[f"rwkv_{what}"]).then_inc(weights_in, 16)
                sp.dma_start(pre_rows[:].rearrange("p a c -> p (a c)"),
                             dram["rwkv_pre_rows"].partition_broadcast(P)).then_inc(weights_in, 16)
                for i in range(PAIRS):
                    sp.wait_ge(act_ready, i + 1)
                    sp.wait_ge(dve_ready, i + 1)
                    for array, buffer in zip(arrays, sent):
                        for j in range(2):
                            b = 2 * i + j
                            sp.dma_start(array[b * GROUPS:(b + 1) * GROUPS, :, :],
                                         buffer[:, j, :]).then_inc(arrays_in, 16)
                    sp.wait_ge(g_ready, i + 1)
                    sp.dma_start(g_rows[i], g_out[:]).then_inc(g_stored, 16)
                sp.wait_ge(g_stored, 16 * PAIRS)
                sp.wait_ge(arrays_in, 16 * 12 * PAIRS)

            @block.tensor
            def _(pe):
                pe.wait_ge(weights_in, 16 * 5)

                def pair(i):
                    attn.pe(pe, i)
                    pe.wait_ge(mix_ready, i + 1)
                    for w, kind in enumerate(items):
                        bank = core.bank[w % NB]
                        if not (isinstance(i, int) and w < NB):
                            pe.wait_ge(down[w % NB], i * (W // NB) + w // NB)
                        mixed = lambda n: mix[:, n].rearrange("p j t -> p (j t)")
                        if kind in ("w1", "a1"):
                            n = int(kind == "a1")
                            last = pe.matmul(bank[0:C // 2, :], low[:, n, :], mixed(4 if n else 1), start=True, stop=True)
                        elif kind in ("w2", "a2"):
                            n = int(kind == "a2")
                            pe.wait_ge(low_ready[n], i + 1)
                            last = pe.matmul(bank[:], high[:, n, :], bent_low[:, n, :], start=True, stop=True)
                        elif kind == "g2":
                            pe.wait_ge(low_ready[2], i + 1)
                            last = pe.matmul(bank[:], wide[:, 4, :], bent_g[:], start=True, stop=True)
                        else:
                            part = ("r", "k", "v", "g1").index(kind)
                            last = pe.matmul(bank[:], wide[:, part, :], mixed((0, 2, 3, 5)[part]), start=True, stop=True)
                        last.then_inc(up, 1)

                pair(0)
                with pe.Fori(1, PAIRS) as i:
                    pair(i)

            @block.scalar
            def _(act):
                act.wait_ge(weights_in, 16 * 5)
                with act.Fori(0, PAIRS) as i:
                    def take(kind, out, func, signal=None, rows=P, **more):
                        w = index[kind]
                        act.wait_ge(up, i * W + w + 1)
                        act.activation(out, core.bank[w % NB][0:rows, :], func, **more).then_inc(down[w % NB], 1)
                        if signal is not None:
                            act.drain()
                            act.sem_inc(signal, 1)

                    act.wait_ge(mix_ready, i)
                    attn.act(act, i, padded[:, :, 1:], cols[:, 0:1], cols[:, 1:2])
                    act.drain()
                    act.sem_inc(padded_ready, 1)
                    take("w1", bent_low[:, 0, :], ACT.Tanh, low_ready[0], rows=C // 2)
                    take("a1", bent_low[:, 1, :], ACT.Identity, low_ready[1], rows=C // 2)
                    take("g1", bent_g[:], ACT.Sigmoid, low_ready[2])
                    act.wait_ge(dve_ready, i)
                    take("k", k_raw[:], ACT.Identity)
                    act.wait_ge(arrays_in, i * 16 * 12)
                    take("a2", a_t, ACT.Sigmoid, a_ready, bias=cols[:, 9:10])
                    take("w2", d_t, ACT.Sigmoid, bias=cols[:, 8:9])
                    take("r", r_t, ACT.Identity)
                    take("v", v_t, ACT.Identity)
                    act.drain()
                    act.activation(d_t, d_t, ACT.Exp, scale=-DECAY)
                    act.drain()
                    act.sem_inc(act_ready, 1)
                    act.wait_ge(g_stored, i * 16)
                    take("g2", g_out[:], ACT.Identity, g_ready)

            @block.gpsimd
            def _(pool):
                with pool.Fori(0, PAIRS) as i:
                    pre.power(pool, i)
                    attn.pool(pool, i)

            @block.vector
            def _(dve):
                dve.wait_ge(weights_in, 16 * 5)
                dve.memset(padded[:], 0.0)
                dve.drain()
                with dve.Fori(0, PAIRS) as i:
                    x1 = core.normed[:, bass.ds(i * PT, PT), :]
                    pre.find_moments(dve, lambda r: core.normed[:, i * PT + r, :])
                    pre.apply(dve, i, lambda r: rows[:, r, :], lambda r: core.normed[:, i * PT + r, :])
                    dve.drain()
                    dve.tensor_tensor(rows[:], rows[:], pre_rows[:, 0, :].unsqueeze(1).broadcast_to([P, PT, C]),
                                      ALU.mult)
                    dve.drain()
                    dve.tensor_tensor(x1, rows[:], pre_rows[:, 1, :].unsqueeze(1).broadcast_to([P, PT, C]), ALU.add)
                    dve.drain()
                    attn.dve(dve, i, lambda r: core.normed[:, i * PT + r, :])
                    dve.wait_ge(padded_ready, i + 1)
                    dve.wait_ge(up, i * W)
                    dve.tensor_tensor(delta[:], padded[:, :, 0:SEQ], padded[:, :, 1:], ALU.subtract)
                    dve.drain()
                    for n in range(6):
                        dve.scalar_tensor_tensor(mix[:, n], delta[:], cols[:, 2 + n:3 + n], padded[:, :, 1:],
                                                 ALU.mult, ALU.add)
                    dve.drain()
                    dve.sem_inc(mix_ready, 1)
                    wk = index["k"]
                    dve.wait_ge(down[wk % NB], i * (W // NB) + wk // NB + 1)
                    dve.wait_ge(arrays_in, i * 16 * 12)
                    dve.tensor_scalar(kk_t, k_raw[:], cols[:, 10:11], None, ALU.mult)
                    dve.wait_ge(a_ready, i + 1)
                    dve.tensor_scalar(lift[:], a_t, 1.0, cols[:, 11:12], ALU.subtract, ALU.mult)
                    dve.drain()
                    dve.scalar_tensor_tensor(k_t, lift[:], 1.0, k_raw[:], ALU.add, ALU.mult)
                    dve.drain()
                    dve.sem_inc(dve_ready, 1)

        with ExitStack() as inner:
            isb = lambda n, shape, dtype=F32: core.sb(f"{name}_{n}", shape, dtype, ctx=inner)
            CK = 16
            CHUNKS = SEQ // CK
            outer = isb("outer", [P, 2, CK, ST])
            states = isb("states", [P, 2, CK, ST])
            recalled = isb("recalled", [P, CK, ST])
            removed, decayed, added = (isb(n, [P, ST]) for n in ("removed", "decayed", "added"))
            sa, outputs = isb("sa", [P, PC]), isb("outputs", [P, CK, PC])
            stat, mean = isb("stat", [P, PH, SEQ]), isb("mean", [P, PH, SEQ])
            part_cols = isb("part_cols", [P, 3, PC])
            cols_in = sem("cols_in")
            squared, root_asked, rooted = sem("squared"), sem("root_asked"), sem("rooted")
            outer_ready, states_ready = sem("outer_ready"), sem("states_ready")
            recalled_ready, recalled_used = sem("recalled_ready"), sem("recalled_used")
            scan_done, bonus_ready, out_ready, x_back, out_sent = (sem(n) for n in (
                "scan_done", "bonus_ready", "out_ready", "x_back", "out_sent"))
            bonus_asked, centred = sem("bonus_asked"), sem("centred")
            square = states[:].rearrange("p a k s -> p (a k s)")
            block = inner.enter_context(nc.Block())

            def by_token(array, h):
                return array[:, h * HD:(h + 1) * HD, :].rearrange("p c t -> p t c")

            def rows_of(chunk, buffer, h):
                return buffer[:, :, h * HD * HD:(h + 1) * HD * HD].rearrange("p k (i j) -> p k i j", j=HD)

            full = [P, CK, HD, HD]

            @block.gpsimd
            def _(pool):
                flat = removal[:].rearrange("p c t -> p (c t)")
                pool.tensor_tensor(square, flat, flat, ALU.mult).then_inc(squared, 1)

                def outer_of(chunk, slot):
                    at = bass.ds(chunk * CK, CK)
                    for h in range(PH):
                        v = values[:, h * HD:(h + 1) * HD, at].rearrange("p c t -> p t c").unsqueeze(3)
                        k = keys[:, h * HD:(h + 1) * HD, at].rearrange("p c t -> p t c").unsqueeze(2)
                        last = pool.tensor_tensor(rows_of(chunk, outer[:, slot], h), v.broadcast_to(full),
                                                  k.broadcast_to(full), ALU.mult)
                    last.then_inc(outer_ready, 1)

                def recall(chunk, slot):
                    at = bass.ds(chunk * CK, CK)
                    pool.wait_ge(states_ready, chunk + 1)
                    pool.wait_ge(recalled_used, chunk)
                    for h in range(PH):
                        r = recv[:, h * HD:(h + 1) * HD, at].rearrange("p c t -> p t c").unsqueeze(2)
                        last = pool.tensor_tensor(rows_of(chunk, recalled, h), rows_of(chunk, states[:, slot], h),
                                                  r.broadcast_to(full), ALU.mult)
                    last.then_inc(recalled_ready, 1)

                outer_of(0, 0)
                outer_of(1, 1)
                with pool.Fori(0, CHUNKS // 2 - 1) as m:
                    for slot in range(2):
                        recall(m * 2 + slot, slot)
                        outer_of(m * 2 + slot + 2, slot)
                for slot in range(2):
                    recall(CHUNKS - 2 + slot, slot)
                pool.wait_ge(scan_done, 1)
                pool.wait_ge(cols_in, 16)
                pool.tensor_tensor(recv[:], recv[:], keys[:], ALU.mult)
                pool.drain()
                pool.tensor_tensor(recv[:], recv[:], part_cols[:, 0, :].unsqueeze(2).broadcast_to([P, PC, SEQ]),
                                   ALU.mult).then_inc(bonus_asked, 1)

            @block.scalar
            def _(act):
                act.wait_ge(root_asked, 1)
                act.activation(stat[:], stat[:], ACT.Sqrt).then_inc(rooted, 1)
                act.wait_ge(centred, 1)
                act.activation(square, removal[:].rearrange("p c t -> p (c t)"), ACT.Square).then_inc(squared, 1)
                act.wait_ge(root_asked, 2)
                act.activation(stat[:], stat[:], ACT.Sqrt).then_inc(rooted, 1)

            def by_head(array):
                return array.rearrange("p (h c) t -> p h c t", h=PH)

            def over_tokens(small):
                return small[:].unsqueeze(2).broadcast_to([P, PH, HD, SEQ])

            @block.vector
            def _(dve):
                def sum_channels(out, array):
                    dve.tensor_reduce(out[:], by_head(array).rearrange("p h c t -> p h t c"), AX.X, ALU.add)

                squares = square.rearrange("p (c t) -> p c t", c=PC)
                dve.wait_ge(squared, 1)
                sum_channels(stat, squares)
                dve.drain()
                dve.tensor_scalar(stat[:], stat[:], 1e-24, None, ALU.max)
                dve.drain()
                dve.sem_inc(root_asked, 1)
                dve.wait_ge(rooted, 1)
                dve.reciprocal(mean[:], stat[:])
                dve.drain()
                dve.tensor_scalar(stat[:], mean[:], -1.0, None, ALU.mult)
                dve.drain()
                dve.tensor_tensor(by_head(removal[:]), by_head(removal[:]), over_tokens(stat), ALU.mult)
                dve.drain()
                dve.scalar_tensor_tensor(rates.rearrange("p c t -> p (c t)"), removal[:].rearrange("p c t -> p (c t)"),
                                         -1.0, rates.rearrange("p c t -> p (c t)"), ALU.mult, ALU.mult)
                dve.memset(states[:, 1, CK - 1, :], 0.0)
                dve.drain()

                def row(array, t):
                    at = array[:, :, bass.ds(t, 1)].rearrange("p (h j) o -> p h (o j)", h=PH)
                    return at.unsqueeze(2).broadcast_to([P, PH, HD, HD])

                def square_of(flat):
                    return flat.rearrange("p (h i j) -> p h i j", h=PH, j=HD)

                def chunk(c, slot):
                    dve.wait_ge(outer_ready, c + 1)
                    if not (isinstance(c, int) and c < 2):
                        dve.wait_ge(recalled_ready, c - 1)
                    for k in range(CK):
                        t = c * CK + k
                        old = states[:, slot, k - 1, :] if k else states[:, 1 - slot, CK - 1, :]
                        dve.tensor_tensor(square_of(removed[:]), square_of(old), row(removal, t), ALU.mult)
                        dve.tensor_tensor(square_of(decayed[:]), square_of(old), row(decays, t), ALU.mult)
                        dve.drain()
                        dve.tensor_reduce(sa[:], removed[:].rearrange("p (c j) -> p c j", j=HD), AX.X, ALU.add)
                        dve.tensor_tensor(decayed[:], decayed[:], outer[:, slot, k, :], ALU.add)
                        dve.drain()
                        dve.tensor_tensor(square_of(added[:]),
                                          sa[:].rearrange("p (h i) -> p h i", h=PH).unsqueeze(3).broadcast_to(
                                              [P, PH, HD, HD]), row(rates, t), ALU.mult)
                        dve.drain()
                        last = dve.tensor_tensor(states[:, slot, k, :], decayed[:], added[:], ALU.add)
                        if k < CK - 1:
                            dve.drain()
                    last.then_inc(states_ready, 1)
                    dve.drain()

                def collect(c):
                    dve.wait_ge(recalled_ready, c + 1)
                    dve.tensor_reduce(outputs[:], recalled[:].rearrange("p k (c j) -> p k c j", j=HD), AX.X,
                                      ALU.add).then_inc(recalled_used, 1)
                    dve.drain()
                    dve.tensor_copy(removal[:, :, bass.ds(c * CK, CK)].rearrange("p c t -> p t c"), outputs[:])
                    dve.drain()

                chunk(0, 0)
                chunk(1, 1)
                collect(0)
                with dve.Fori(1, CHUNKS // 2) as m:
                    for slot in range(2):
                        chunk(m * 2 + slot, slot)
                        collect(m * 2 + slot - 1)
                collect(CHUNKS - 1)
                dve.drain()
                dve.sem_inc(scan_done, 1)
                out = removal[:]
                sum_channels(mean, out)
                dve.drain()
                dve.tensor_scalar(mean[:], mean[:], 1.0 / HD, None, ALU.mult)
                dve.drain()
                dve.tensor_tensor(by_head(out), by_head(out), over_tokens(mean), ALU.subtract)
                dve.drain()
                dve.sem_inc(centred, 1)
                dve.wait_ge(squared, 2)
                sum_channels(stat, squares)
                dve.drain()
                dve.tensor_scalar(stat[:], stat[:], 1.0 / HD, 0.00064, ALU.mult, ALU.add)
                dve.drain()
                dve.sem_inc(root_asked, 1)
                dve.wait_ge(bonus_asked, 1)
                sum_channels(mean, recv[:])
                dve.drain()
                dve.tensor_tensor(by_head(values[:]), by_head(values[:]), over_tokens(mean), ALU.mult)
                dve.wait_ge(rooted, 2)
                dve.drain()
                dve.reciprocal(mean[:], stat[:])
                dve.drain()
                dve.tensor_tensor(by_head(out), by_head(out), over_tokens(mean), ALU.mult)
                dve.wait_ge(cols_in, 16)
                dve.drain()
                for c in range(PC):
                    dve.tensor_scalar(removal[:, c, :], removal[:, c, :], part_cols[:, 1, c:c + 1],
                                      part_cols[:, 2, c:c + 1], ALU.mult, ALU.add)
                dve.drain()
                dve.tensor_tensor(out, out, values[:], ALU.add).then_inc(out_ready, 1)

            @block.sync
            def _(sp):
                sp.dma_start(part_cols[:], dram["rwkv_part_cols"]).then_inc(cols_in, 16)
                sp.wait_ge(scan_done, 1)
                sp.dma_start(core.x[:], x_dram.rearrange("b (h p) c -> p (b h) c", p=P)).then_inc(x_back, 16)
                sp.wait_ge(out_ready, 1)
                for b in range(SEQS):
                    sp.dma_start(core.normed_t[:, b * SEQ:(b + 1) * SEQ],
                                 removal[b * GROUPS:(b + 1) * GROUPS, :, :]).then_inc(out_sent, 16)
                sp.wait_ge(out_sent, 16 * SEQS)
                sp.wait_ge(x_back, 16)

    HC = 4
    with ExitStack() as inner:
        isb = lambda n, shape, dtype=F32: core.sb(f"{name}_{n}", shape, dtype, ctx=inner)
        ffn = TurnedNorm(core, "rwkv_ffn", inner, core.bank[1])
        cols, wo = isb("out_cols", [P, 3]), isb("wo", [P, C])
        w1, w2 = isb("w1", [P, HC * P]), isb("w2", [P, HC, C])
        g_in, gated = isb("g_in", [P, PN]), isb("gated", [P, PN])
        padded, delta, mix = isb("padded2", [P, 2, SEQ + 1]), isb("delta2", [P, 2, SEQ]), isb("mix2", [P, 2, SEQ])
        relu, hidden = isb("relu", [P, HC, PN]), isb("hidden", [P, HC, PN])
        weights_in, g_loaded, gated_ready = sem2(core, "weights_in"), sem2(core, "g_loaded"), sem2(core, "gated_ready")
        wo_up, wo_taken = sem2(core, "wo_up"), sem2(core, "wo_taken")
        padded_ready, mix_ready = sem2(core, "padded_ready"), sem2(core, "mix_ready")
        hidden_up, relu_done, hidden_done = sem2(core, "hidden_up"), sem2(core, "relu_done"), sem2(core, "hidden_done")
        out_up, out_taken = sem2(core, "out_up"), sem2(core, "out_taken")
        block = inner.enter_context(nc.Block())

        @block.sync
        def _(sp):
            for to, what in ((cols, "out_cols"), (wo, "wo"), (w1, "w1"), (w2, "w2")):
                sp.dma_start(to[:], dram[f"rwkv_{what}"]).then_inc(weights_in, 16)
            with sp.Fori(0, PAIRS) as i:
                sp.wait_ge(gated_ready, i)
                sp.dma_start(g_in[:], g_rows[bass.ds(i, 1)].rearrange("a p n -> (a p) n")).then_inc(g_loaded, 16)

        @block.tensor
        def _(pe):
            pe.wait_ge(weights_in, 64)

            def pair(i, has_tail):
                pe.wait_ge(gated_ready, i + 1)
                pe.wait_ge(wo_taken, i)
                for t in range(PT):
                    last = pe.matmul(core.bank[0][:, t * P:(t + 1) * P], gated[:, t * P:(t + 1) * P], wo[:],
                                     start=True, stop=True)
                last.then_inc(wo_up, 1)
                if has_tail:
                    tail.pe(pe, i - 1)
                ffn.pe(pe, i)
                pe.wait_ge(mix_ready, i + 1)
                pe.wait_ge(relu_done, i * HC)
                for f in range(HC):
                    pe.matmul(core.bank[2 + f][:], w1[:, f * P:(f + 1) * P], mix[:].rearrange("p j t -> p (j t)"),
                              start=True, stop=True).then_inc(hidden_up, 1)
                pe.wait_ge(hidden_done, (i + 1) * HC)
                pe.wait_ge(out_taken, i)
                for t in range(PT):
                    for f in range(HC):
                        last = pe.matmul(core.bank[6][:, t * P:(t + 1) * P], hidden[:, f, t * P:(t + 1) * P],
                                         w2[:, f, :], start=(f == 0), stop=(f == HC - 1))
                last.then_inc(out_up, 1)

            pair(0, False)
            with pe.Fori(1, PAIRS) as i:
                pair(i, True)
            tail.pe(pe, PAIRS - 1)

        @block.scalar
        def _(act):
            act.wait_ge(weights_in, 64)

            def pair(i, has_tail):
                if has_tail:
                    tail.act(act, i - 1)
                act.wait_ge(mix_ready, i)
                ffn.act(act, i, padded[:, :, 1:], cols[:, 0:1], cols[:, 1:2])
                act.drain()
                act.sem_inc(padded_ready, 1)
                act.wait_ge(hidden_done, i * HC)
                for f in range(HC):
                    act.wait_ge(hidden_up, i * HC + f + 1)
                    act.activation(relu[:, f, :], core.bank[2 + f][:], ACT.Relu).then_inc(relu_done, 1)

            pair(0, False)
            with act.Fori(1, PAIRS) as i:
                pair(i, True)
            tail.act(act, PAIRS - 1)

        @block.gpsimd
        def _(pool):
            with pool.Fori(0, PAIRS) as i:
                ffn.pool(pool, i)
                pool.wait_ge(out_up, i)
                for f in range(HC):
                    pool.wait_ge(relu_done, i * HC + f + 1)
                    pool.tensor_tensor(hidden[:, f, :], relu[:, f, :], relu[:, f, :], ALU.mult).then_inc(hidden_done, 1)
                tail.pool(pool, i)

        @block.vector
        def _(dve):
            dve.wait_ge(weights_in, 64)
            dve.memset(padded[:], 0.0)
            dve.drain()
            with dve.Fori(0, PAIRS) as i:
                dve.wait_ge(g_loaded, (i + 1) * 16)
                dve.wait_ge(wo_up, i)
                dve.tensor_tensor(gated[:], g_in[:], core.normed_t[:, bass.ds(i * PN, PN)],
                                  ALU.mult).then_inc(gated_ready, 1)
                dve.wait_ge(wo_up, i + 1)
                flat = core.branch[:].rearrange("p t c -> p (t c)")
                dve.tensor_tensor(flat, core.bank[0][:], core.normed[:, bass.ds(i * PT, PT), :].rearrange(
                    "p t c -> p (t c)"), ALU.add)
                dve.drain()
                dve.sem_inc(wo_taken, 1)
                ffn.dve(dve, i, lambda r: core.branch[:, r, :])
                dve.wait_ge(padded_ready, i + 1)
                dve.tensor_tensor(delta[:], padded[:, :, 0:SEQ], padded[:, :, 1:], ALU.subtract)
                dve.drain()
                dve.wait_ge(hidden_up, i * HC)
                dve.scalar_tensor_tensor(mix[:], delta[:], cols[:, 2:3], padded[:, :, 1:], ALU.mult,
                                         ALU.add).then_inc(mix_ready, 1)
                dve.wait_ge(out_up, i + 1)
                dve.tensor_tensor(flat, core.bank[6][:], flat, ALU.add)
                dve.drain()
                dve.sem_inc(out_taken, 1)
                tail.dve(dve, i)


def sem2(core, name):
    return core.sem(f"rwkv_out_{name}")


def build(nc, dram, out, blocks=("rwkv", "moe0", "wave", "local", "ssm", "moe2", "mamba", "attn3")):
    with ExitStack() as ctx:
        core = Core(nc, ctx, dram)
        capacity = -(-TILES * P * 2 * 5 // (EXPERTS * 4))
        prologue(core, dram["x"])
        core.end_of_block()
        if "rwkv" in blocks:
            rwkv_block(core, Tail(core, "rwkv", keep_rows=False, turned=True), dram["x"])
            core.end_of_block()
        if "moe0" in blocks:
            moe_block(core, "moe0", Tail(core, "moe0", keep_rows=False, turned=True), shared=True, bias=True,
                      normalised=True, chunks=4)
            core.end_of_block()
        if "wave" in blocks:
            wave_block(core, Tail(core, "wave", keep_rows=True, turned=True))
            core.end_of_block()
        if "local" in blocks:
            local_layer(core, 0, Carry(core, "local0", keep_rows=False, turned=True))
            core.end_of_block()
            local_layer(core, 1, Tail(core, "local1", keep_rows=False, turned=True))
            core.end_of_block()
        if "ssm" in blocks:
            ssm_block(core, "ssm", Tail(core, "ssm", keep_rows=False, turned=True), 16, False)
            core.end_of_block()
        if "moe2" in blocks:
            moe_block(core, "moe2", Tail(core, "moe2", keep_rows=True, turned=False), shared=False, bias=True,
                      normalised=False, chunks=4)
            core.end_of_block()
        if "mamba" in blocks:
            ssm_block(core, "mamba", Tail(core, "mamba", keep_rows=True, turned=False), 4, True)
            core.end_of_block()
        if "attn3" in blocks:
            attention_over_sequences(core)
            core.end_of_block()
            moe_block(core, "moe3", Tail(core, "moe3", keep_rows=False, turned=False, last=True), shared=False,
                      bias=False, normalised=True, chunks=2, capacity=capacity, base=core.normed)
            core.end_of_block()
        stored = core.sem("stored")
        with nc.Block() as block:
            @block.sync
            def _(sp):
                sp.dma_start(out.rearrange("b (h p) c -> p (b h) c", p=P), core.x[:]).then_inc(stored, 16)
                sp.wait_ge(stored, 16)


def arrange(inputs):
    a = {k: np.ascontiguousarray(v) for k, v in inputs.items()}
    t = np.arange(P)
    bf16 = mybir.dt.np(BF16)
    out = {
        "identity": np.eye(P, dtype=np.float32),
        "earlier": (t[:, None] < t[None, :]).astype(np.float32),
        "ones": np.ones((P, P), np.float32),
    }

    def moe(name, w1, w2, b1=None, b2=None):
        e, f, d = w1.shape
        out[f"{name}_w1"] = w1.transpose(2, 0, 1)
        out[f"{name}_w2"] = w2.reshape(e, d, f // P, P).transpose(3, 0, 2, 1)
        if b1 is not None:
            out[f"{name}_b1"] = b1.reshape(e, f // P, P).transpose(2, 0, 1).reshape(P, -1)
            out[f"{name}_b2"] = b2

    moe("moe0", np.concatenate([a["L0_ffn_shared_w1"][None], a["L0_ffn_spec_w1"]]),
        np.concatenate([a["L0_ffn_shared_w2"][None], a["L0_ffn_spec_w2"]]),
        np.concatenate([a["L0_ffn_shared_b1"][None], a["L0_ffn_spec_b1"]]),
        np.concatenate([a["L0_ffn_shared_b2"][None], a["L0_ffn_spec_b2"]]))
    out["moe0_router"] = a["L0_ffn_router_w"].T
    out["moe0_router_b"] = a["L0_ffn_router_b"][:, None]
    moe("moe2", a["L2_ffn_w1"].transpose(1, 0, 2), a["L2_ffn_w2"].transpose(1, 0, 2), a["L2_ffn_b1"], a["L2_ffn_b2"])
    out["moe2_router"] = a["L2_ffn_gate_w"].T
    moe("moe3", a["L3_ffn_moe_w1"].transpose(0, 2, 1), a["L3_ffn_moe_w2"].transpose(0, 2, 1))
    out["moe3_router"] = a["L3_ffn_router_weight"]

    def columns(*names):
        return np.stack([a[n].reshape(-1) for n in names], axis=1)

    out["attn_cols"] = columns("L3_ffn_ln1_weight", "L3_ffn_ln1_bias", "L3_ffn_ln2_weight", "L3_ffn_ln2_bias")
    out["attn_wqkv"] = a["L3_ffn_qkv_weight"].T
    out["attn_wproj"] = a["L3_ffn_proj_weight"].T

    def ssm(name, w_in, wx, wbc, wgate, wdt, w_out, taps, conv_b, heads, cols, head_cols):
        inner = 2 * C
        out[f"{name}_wx"], out[f"{name}_wdt"], out[f"{name}_wgate"] = w_in[:, wx], w_in[:, wdt], wgate
        out[f"{name}_wbc"] = wbc
        out[f"{name}_wout"] = w_out.reshape(inner // P, P, C).transpose(1, 0, 2)
        out[f"{name}_taps"] = np.concatenate([taps, conv_b[:, None]], axis=1).reshape(inner // P, P, 5).transpose(1, 0, 2)
        out[f"{name}_cols"], out[f"{name}_head_cols"] = cols, head_cols
        row = np.arange(96)
        mine = ((row % 32)[:, None] == np.arange(heads)[None, :])
        out[f"{name}_pick"] = np.broadcast_to(mine[:, :, None], (96, heads, P)).astype(bf16)
        out[f"{name}_unpick"] = (-mine.astype(np.float32)).astype(bf16)

    out["identity16"] = np.eye(P, dtype=bf16)
    out["future"] = np.where(t[:, None] <= t[None, :], 0.0, -BIG).astype(bf16)
    w_in, nw = a["L2_attn_W_in"], a["L2_attn_norm_w"]
    ssm("ssm", w_in, slice(0, 256), w_in[:, 256:2304].reshape(P, 16, P), a["L2_attn_W_gate"], slice(2304, 2320),
        a["L2_attn_W_out"], a["L2_attn_conv_w"], a["L2_attn_conv_b"], 16, nw.reshape(2, P).T,
        np.stack([a["L2_attn_delta_param"]] * 2, axis=1))
    w_in, ns = a["L3_attn_w_in"], a["L3_attn_norm_scale"]
    ssm("mamba", w_in, slice(256, 512), w_in[:, 516:644].reshape(P, 2, 64), w_in[:, 0:256], slice(512, 516),
        a["L3_attn_w_out"], a["L3_attn_conv_weight"].T, a["L3_attn_conv_bias"], 4, np.stack([ns, ns], axis=1),
        np.stack([a["L3_attn_dt_bias"], a["L3_attn_A_log"]], axis=1))

    hd, f32 = 64, np.float32
    half = np.arange(0, hd, 2, dtype=f32)
    pos = np.arange(SEQ, dtype=f32)
    freqs = pos[:, None] * (f32(1.0) / f32(10000.0) ** (half / f32(hd)))[None, :]
    freqs = np.concatenate([freqs, freqs], axis=1)
    base = (half + f32(0.4 * hd)) / f32(1.4 * hd)
    scale = base[None, :] ** ((pos - SEQ // 2) / f32(32.0))[:, None]
    scale = np.concatenate([scale, scale], axis=1)
    sign = np.where(np.arange(hd) < hd // 2, f32(-1.0), f32(1.0))
    tabs = np.stack([np.stack([np.cos(freqs) * scale * f32(8.0), np.sin(freqs) * sign * scale * f32(8.0)]),
                     np.stack([np.cos(freqs) / scale, np.sin(freqs) * sign / scale])])
    out["rotary"] = tabs.reshape(2, 2, 2, P, hd).transpose(3, 0, 2, 1, 4).astype(f32)
    blocks = []
    for q0, k0 in ((0, 0), (P, 0), (P, P)):
        gap = (t[:, None] + q0) - (t[None, :] + k0)
        blocks.append(np.where((gap >= 0) & (gap <= 64), 0.0, -BIG))
    out["window"] = np.concatenate(blocks, axis=1).astype(bf16)
    hid = a["L1_ffn_w2"].shape[1]
    fc = -(-hid // P)

    def padded(v):
        return np.concatenate([v, np.zeros((*v.shape[:-1], fc * P - hid), v.dtype)], axis=-1)

    for l in range(2):
        w1, b1 = a["L1_ffn_w1"][l], a["L1_ffn_b1"][l]
        out[f"local{l}_wqkv"] = a["L1_ffn_wqkv"][l]
        out[f"local{l}_wo"] = a["L1_ffn_wo"][l].reshape(4, P, C).transpose(1, 0, 2)
        both = np.stack([padded(w1[:, :hid]), padded(w1[:, hid:])])
        out[f"local{l}_w1"] = both.reshape(2, C, fc, P).transpose(1, 2, 0, 3)
        out[f"local{l}_w2"] = padded(a["L1_ffn_w2"][l].T).reshape(C, fc, P).transpose(2, 1, 0)
        out[f"local{l}_cols"] = np.concatenate(
            [a["L1_ffn_ln_g"][l][:, None], a["L1_ffn_ln_b"][l][:, None], padded(b1[:hid]).reshape(fc, P).T,
             padded(b1[hid:]).reshape(fc, P).T], axis=1)
        out[f"local{l}_b2"] = a["L1_ffn_b2"][l][None]
        own = np.stack([a["L1_ffn_q_scale"][l], a["L1_ffn_k_scale"][l]])
        other = np.concatenate([own[:, hd // 2:], own[:, :hd // 2]], axis=1)
        out[f"local{l}_scales"] = np.stack([own, other], axis=1).reshape(-1)

    out["wave_params"] = np.stack([a["L1_attn_wave_frequency"], a["L1_attn_wave_damping"],
                                   a["L1_attn_wave_phase"], a["L1_attn_wave_phase"]], axis=1)
    out["wave_time"] = np.broadcast_to(pos[None], (16, SEQ))
    out["wave_coupling"] = a["L1_attn_field_coupling"]
    out["wave_w"] = a["L1_attn_Wqkvg"].reshape(4, C, C).transpose(2, 0, 1)
    out["wave_cols"] = a["L1_attn_bqkvg"].reshape(4, C).T
    out["wave_wout"], out["wave_bout"] = a["L1_attn_Wout"].T, a["L1_attn_bout"][None]
    head, channel = np.arange(P) // 8, np.arange(P) % 8
    out["wave_spread"] = (np.arange(16)[:, None] == head[None, :]).astype(f32)
    out["wave_same"] = (channel[:, None] == channel[None, :]).astype(f32)

    L = lambda n: a["L0_attn_" + n]
    out["rwkv_pre_rows"] = np.concatenate([L("ln_pre_w"), L("ln_pre_b")])
    out["rwkv_cols"] = columns(*("L0_attn_" + n for n in (
        "ln_attn_w", "ln_attn_b", "x_r", "x_w", "x_k", "x_v", "x_a", "x_g", "w0", "a0", "k_k", "k_a")))
    out["rwkv_wide"] = np.stack([L("W_r"), L("W_k"), L("W_v"), L("g1"), L("g2")], axis=1)
    out["rwkv_low"] = np.stack([L("w1"), L("a1")], axis=1)
    out["rwkv_high"] = np.stack([L("w2"), L("a2")], axis=1)
    per_part = np.stack([L("r_k").reshape(8, 16), L("gn_w").reshape(8, 16), L("gn_b").reshape(8, 16)], axis=1)
    out["rwkv_part_cols"] = np.broadcast_to(per_part[None], (SEQS, 8, 3, 16)).reshape(P, 3, 16)
    out["rwkv_out_cols"] = columns("L0_attn_ln_ffn_w", "L0_attn_ln_ffn_b", "L0_attn_ffn_x_k")
    out["rwkv_wo"], out["rwkv_w1"] = L("W_o"), L("W_ffn1")
    out["rwkv_w2"] = L("W_ffn2").reshape(4, P, C).transpose(1, 0, 2)
    out = {k: np.ascontiguousarray(v) for k, v in out.items()}
    out["x"] = a["L0_attn_x"]
    return out


def kernel(**inputs):
    import concourse.bacc as bacc
    from concourse.bass_utils import run_bass_kernel_spmd

    nc = bacc.Bacc("TRN2", target_bir_lowering=False, num_devices=1)
    arrays, dram = {}, {}
    for name, array in arrange(inputs).items():
        arrays[f"in_{name}_dram"] = array
        dram[name] = nc.dram_tensor(f"in_{name}_dram", array.shape, mybir.dt.from_np(array.dtype),
                                    kind="ExternalInput").ap()
    out = nc.dram_tensor("out_dram", (SEQS, SEQ, C), F32, kind="ExternalOutput").ap()
    build(nc, dram, out)
    got = run_bass_kernel_spmd(nc, [arrays], core_ids=[0])
    return got.results[0]["out_dram"]
```

```python
from contextlib import ExitStack

import numpy as np
import concourse.bass as bass
from concourse import mybir

F32 = mybir.dt.float32
BF16 = mybir.dt.bfloat16
ALU = mybir.AluOpType
ACT = mybir.ActivationFunctionType
AX = mybir.AxisListType

SEQS, SEQ, C = 16, 256, 128
P = 128
TILES = SEQS * SEQ // P
PAIRS = SEQS // 2
PT = 4
PN = PT * P
EPS = 1e-5
BIG = 1e30


class Core:

    def __init__(self, nc, ctx, dram):
        self.nc, self.ctx, self.dram = nc, ctx, dram
        self.semaphores = []
        self.x = self.sb("x", [P, TILES, C])
        self.normed = self.sb("normed", [P, TILES, C])
        self.normed_t = self.sb("normed_t", [C, TILES * P])
        self.ident = self.sb("ident", [P, P])
        self.minus_half = self.sb("minus_half", [P, 16])
        self.eps = self.sb("eps", [P, 16])
        self.ones_row = self.sb("ones_row", [1, P])
        self.branch = self.sb("branch", [P, PT, C])
        self.fresh = self.sb("fresh", [P, PT, C])
        self.branch_norm = self.norm_buffers("branch_norm", PT)
        self.x_norm = self.norm_buffers("x_norm", PT)
        self.bank = [ctx.enter_context(nc.psum_tensor(f"bank{i}", [P, 512], F32)) for i in range(8)]

    def norm_buffers(self, name, rows, ctx=None):
        return [self.sb(f"{name}_parts", [P, rows, 6], ctx=ctx), self.sb(f"{name}_moments", [P, rows, 2], ctx=ctx),
                self.sb(f"{name}_rstd", [P, rows], ctx=ctx), self.sb(f"{name}_shifted", [P, rows], ctx=ctx)]

    def sb(self, name, shape, dtype=F32, ctx=None):
        return (ctx or self.ctx).enter_context(self.nc.sbuf_tensor(name, shape, dtype))

    def sem(self, name):
        handle = self.nc.alloc_semaphore(name)
        self.semaphores.append(handle)
        return handle

    def end_of_block(self):
        self.nc.clear_and_free_semaphores(self.semaphores)
        self.nc.all_engine_barrier()
        self.semaphores = []


class Norm:

    def __init__(self, core, name, rows, eps, buffers):
        self.core, self.rows, self.eps = core, rows, eps
        self.parts, self.moments, self.rstd, self.shifted = buffers
        self.moments_ready = core.sem(f"{name}_moments_ready")
        self.rstd_ready = core.sem(f"{name}_rstd_ready")

    def find_moments(self, dve, row_of):
        for r in range(self.rows):
            dve.bn_stats(self.parts[:, r, :], row_of(r))
        dve.drain()
        for r in range(self.rows):
            last = dve.bn_aggr(self.moments[:, r, :], self.parts[:, r, :])
        last.then_inc(self.moments_ready, 1)
        dve.drain()

    def power(self, pool, turn):
        pool.wait_ge(self.moments_ready, turn + 1)
        pool.tensor_tensor(self.shifted[:], self.moments[:, :, 1], self.eps[:, 0:self.rows], ALU.add)
        pool.drain()
        pool.tensor_tensor(self.rstd[:], self.shifted[:], self.core.minus_half[:, 0:self.rows],
                           ALU.pow).then_inc(self.rstd_ready, 1)

    def apply(self, dve, turn, out_of, row_of):
        dve.wait_ge(self.rstd_ready, turn + 1)
        for r in range(self.rows):
            last = dve.tensor_scalar(out_of(r), row_of(r), self.moments[:, r, 0:1], self.rstd[:, r:r + 1],
                                     ALU.subtract, ALU.mult)
        return last


class Tail:

    def __init__(self, core, name, keep_rows, turned, last=False, bank=7):
        self.core, self.keep_rows, self.turned, self.last = core, keep_rows, turned, last
        self.turn_bank = core.bank[bank]
        self.of_branch = Norm(core, f"{name}_branch", PT, core.eps, core.branch_norm)
        self.of_x = Norm(core, f"{name}_x", PT, core.eps, core.x_norm)
        self.fresh_ready = core.sem(f"{name}_fresh_ready")
        self.fresh_turned = core.sem(f"{name}_fresh_turned")
        self.turned_stored = core.sem(f"{name}_turned_stored")
        self.fresh_kept = core.sem(f"{name}_fresh_kept")
        self.x_final = core.sem(f"{name}_x_final")

    def dve(self, dve, i):
        self.dve_branch(dve, i)
        self.dve_stream(dve, i)
        self.dve_fresh(dve, i)

    def dve_branch(self, dve, i):
        self.of_branch.find_moments(dve, lambda r: self.core.branch[:, r, :])

    def dve_stream(self, dve, i):
        core = self.core
        self.of_branch.apply(dve, i, lambda r: core.branch[:, r, :], lambda r: core.branch[:, r, :])
        dve.drain()
        x = core.x[:, bass.ds(i * PT, PT), :]
        last = dve.tensor_tensor(x, x, core.branch[:], ALU.add)
        if self.last:
            last.then_inc(self.x_final, 1)
            dve.drain()
            return
        dve.drain()
        self.of_x.find_moments(dve, lambda r: core.x[:, i * PT + r, :])

    def dve_fresh(self, dve, i):
        if self.last:
            return
        core = self.core
        if self.turned:
            dve.wait_ge(self.fresh_turned, i)
        if self.keep_rows:
            dve.wait_ge(self.fresh_kept, i)
        self.of_x.apply(dve, i, lambda r: core.fresh[:, r, :],
                        lambda r: core.x[:, i * PT + r, :]).then_inc(self.fresh_ready, 1)
        dve.drain()

    def pool(self, pool, i):
        self.of_branch.power(pool, i)
        if self.last:
            return
        self.of_x.power(pool, i)
        if self.keep_rows:
            pool.wait_ge(self.fresh_ready, i + 1)
            pool.tensor_copy(self.core.normed[:, bass.ds(i * PT, PT), :],
                             self.core.fresh[:]).then_inc(self.fresh_kept, 1)

    def pe(self, pe, i):
        pe.wait_ge(self.fresh_ready, i + 1)
        pe.wait_ge(self.turned_stored, i)
        for t in range(PT):
            last = pe.transpose(self.turn_bank[:, t * P:(t + 1) * P], self.core.fresh[:, t, :], self.core.ident[:])
        last.then_inc(self.fresh_turned, 1)

    def act(self, act, i):
        act.wait_ge(self.fresh_turned, i + 1)
        act.activation(self.core.normed_t[:, bass.ds(i * PN, PN)], self.turn_bank[:],
                       ACT.Identity).then_inc(self.turned_stored, 1)


def prologue(core, x_dram):
    nc, dram = core.nc, core.dram
    with ExitStack() as ctx:
        norm = Norm(core, "first", PT, core.eps, core.x_norm)
        x_loaded, consts = core.sem("x_loaded"), core.sem("consts_loaded")
        fresh_ready, fresh_turned = core.sem("first_ready"), core.sem("first_turned")
        stored, kept = core.sem("first_stored"), core.sem("first_kept")
        block = ctx.enter_context(nc.Block())

        @block.sync
        def _(sp):
            sp.dma_start(core.ident[:], dram["identity"]).then_inc(consts, 16)
            sp.dma_start(core.x[:], x_dram.rearrange("b (h p) c -> p (b h) c", p=P)).then_inc(x_loaded, 16)

        @block.gpsimd
        def _(pool):
            pool.memset(core.minus_half[:], -0.5)
            pool.memset(core.eps[:], EPS)
            pool.memset(core.ones_row[:], 1.0)
            pool.drain()
            with pool.Fori(0, PAIRS) as i:
                norm.power(pool, i)
                pool.wait_ge(fresh_ready, i + 1)
                pool.tensor_copy(core.normed[:, bass.ds(i * PT, PT), :], core.fresh[:]).then_inc(kept, 1)

        @block.vector
        def _(dve):
            dve.wait_ge(x_loaded, 16)
            with dve.Fori(0, PAIRS) as i:
                norm.find_moments(dve, lambda r: core.x[:, i * PT + r, :])
                dve.wait_ge(fresh_turned, i)
                dve.wait_ge(kept, i)
                norm.apply(dve, i, lambda r: core.fresh[:, r, :],
                           lambda r: core.x[:, i * PT + r, :]).then_inc(fresh_ready, 1)
                dve.drain()

        @block.tensor
        def _(pe):
            pe.wait_ge(consts, 16)
            with pe.Fori(0, PAIRS) as i:
                pe.wait_ge(fresh_ready, i + 1)
                pe.wait_ge(stored, i)
                for t in range(PT):
                    last = pe.transpose(core.bank[7][:, t * P:(t + 1) * P], core.fresh[:, t, :], core.ident[:])
                last.then_inc(fresh_turned, 1)

        @block.scalar
        def _(act):
            with act.Fori(0, PAIRS) as i:
                act.wait_ge(fresh_turned, i + 1)
                act.activation(core.normed_t[:, bass.ds(i * PN, PN)], core.bank[7][:],
                               ACT.Identity).then_inc(stored, 1)


EXPERTS = 8


def top_two(core, name, ctx, logits, weights, normalised, act_exp):
    shape = [P, TILES, EXPERTS]
    work = core.sb(f"{name}_gate_work", shape, ctx=ctx)
    rest = core.sb(f"{name}_gate_rest", shape, ctx=ctx)
    picked = core.sb(f"{name}_gate_picked", shape, ctx=ctx)
    order = core.sb(f"{name}_gate_order", [P, EXPERTS], ctx=ctx)
    best = core.sb(f"{name}_gate_best", [P, TILES], ctx=ctx)
    first = core.sb(f"{name}_gate_first", [P, TILES], ctx=ctx)

    def wide(small):
        return small[:].unsqueeze(2).broadcast_to(shape)

    ranks = order[:].unsqueeze(1).broadcast_to(shape)

    def run(dve):
        for e in range(EXPERTS):
            dve.memset(order[:, e:e + 1], float(EXPERTS - e))
        dve.drain()
        for k in range(2):
            source = logits if k == 0 else rest
            dve.tensor_reduce(best[:], source[:], AX.X, ALU.max)
            dve.drain()
            dve.tensor_tensor(work[:], source[:], wide(best), ALU.is_equal)
            if k == 0:
                dve.tensor_tensor(weights[:], logits[:], wide(best), ALU.subtract)
            dve.drain()
            dve.tensor_tensor(work[:], work[:], ranks, ALU.mult)
            dve.drain()
            dve.tensor_reduce(first[:], work[:], AX.X, ALU.max)
            dve.drain()
            dve.tensor_tensor(work[:], ranks, wide(first), ALU.is_equal)
            dve.drain()
            if k == 0:
                dve.tensor_copy(picked[:], work[:])
                dve.scalar_tensor_tensor(rest[:], work[:], -BIG, logits[:], ALU.mult, ALU.add)
            else:
                dve.tensor_tensor(picked[:], picked[:], work[:], ALU.add)
            dve.drain()
        act_exp(dve)
        if normalised:
            dve.tensor_tensor(weights[:], weights[:], picked[:], ALU.mult)
            dve.drain()
        dve.tensor_reduce(best[:], weights[:], AX.X, ALU.add)
        dve.drain()
        dve.reciprocal(first[:], best[:])
        dve.drain()
        if not normalised:
            dve.tensor_tensor(weights[:], weights[:], picked[:], ALU.mult)
            dve.drain()
        dve.tensor_tensor(weights[:], weights[:], wide(first), ALU.mult)
        dve.drain()

    return run, picked


def moe_block(core, name, tail, shared, bias, normalised, chunks, capacity=None, source_t=None, base=None):
    nc, dram = core.nc, core.dram
    heads = EXPERTS + (1 if shared else 0)
    first_routed = heads - EXPERTS
    hidden = chunks * P
    source_t = source_t or core.normed_t
    with ExitStack() as ctx:
        w1 = core.sb(f"{name}_w1", [P, heads, hidden], ctx=ctx)
        w2 = core.sb(f"{name}_w2", [P, heads, chunks, C], ctx=ctx)
        router = core.sb(f"{name}_router", [P, EXPERTS], ctx=ctx)
        logits = core.sb(f"{name}_logits", [P, TILES, EXPERTS], ctx=ctx)
        weights = core.sb(f"{name}_weights", [P, TILES, EXPERTS], ctx=ctx)
        logit_rows = core.sb(f"{name}_logit_rows", [EXPERTS, 2, PN], ctx=ctx)
        hid = core.sb(f"{name}_hidden", [P, 2, chunks, PN], ctx=ctx)
        if bias:
            b1 = core.sb(f"{name}_b1", [P, heads * chunks], ctx=ctx)
            b2 = core.sb(f"{name}_b2", [heads, C], ctx=ctx)
            pair_weights = core.sb(f"{name}_pair_weights", [P, PT, heads], ctx=ctx)
            weight_rows = core.sb(f"{name}_weight_rows", [heads, PN], ctx=ctx)
        if shared:
            router_b = core.sb(f"{name}_router_b", [EXPERTS, 1], ctx=ctx)
        if capacity:
            earlier = core.sb(f"{name}_earlier", [P, P], ctx=ctx)
            ones = core.sb(f"{name}_ones", [P, P], ctx=ctx)
            counts = core.sb(f"{name}_counts", [P, TILES, EXPERTS], ctx=ctx)
            before = core.sb(f"{name}_before", [P, TILES, EXPERTS], ctx=ctx)
            fits = core.sb(f"{name}_fits", [P, TILES, EXPERTS], ctx=ctx)
            picks_ready, ranks_ready = core.sem(f"{name}_picks_ready"), core.sem(f"{name}_ranks_ready")
            ranks_taken = core.sem(f"{name}_ranks_taken")
        weights_in = core.sem(f"{name}_weights_in")
        logit_rows_up, logit_rows_down = core.sem(f"{name}_logit_rows_up"), core.sem(f"{name}_logit_rows_down")
        logits_up, logits_down = core.sem(f"{name}_logits_up"), core.sem(f"{name}_logits_down")
        exp_asked, exp_done = core.sem(f"{name}_exp_asked"), core.sem(f"{name}_exp_done")
        hidden_up, hidden_done = core.sem(f"{name}_hidden_up"), core.sem(f"{name}_hidden_done")
        out_up, out_taken = core.sem(f"{name}_out_up"), core.sem(f"{name}_out_taken")
        if bias:
            pair_staged, pair_turned = core.sem(f"{name}_pair_staged"), core.sem(f"{name}_pair_turned")
            rows_staged = core.sem(f"{name}_rows_staged")
            bias_up, bias_taken = core.sem(f"{name}_bias_up"), core.sem(f"{name}_bias_taken")
        hbank, obank, small = core.bank[0:4], core.bank[4:6], core.bank[6]
        rbank = [small, hbank[3]]
        loads = 3 + (2 if bias else 0) + (1 if shared else 0) + (2 if capacity else 0)
        per_pair = heads * chunks

        def act_exp(dve):
            dve.sem_inc(exp_asked, 1)
            dve.wait_ge(exp_done, 1)

        gate, picked = top_two(core, name, ctx, logits, weights, normalised, act_exp)
        block = ctx.enter_context(nc.Block())

        def slot_turn(i, e):
            back = 1 if heads % 2 and e == 0 else 2
            if isinstance(i, int) and i * heads + e < back:
                return None
            return i * heads + e - back + 1

        @block.sync
        def _(sp):
            sp.dma_start(router[:], dram[f"{name}_router"]).then_inc(weights_in, 16)
            sp.dma_start(w1[:], dram[f"{name}_w1"]).then_inc(weights_in, 16)
            sp.dma_start(w2[:], dram[f"{name}_w2"]).then_inc(weights_in, 16)
            if bias:
                sp.dma_start(b1[:], dram[f"{name}_b1"]).then_inc(weights_in, 16)
                sp.dma_start(b2[:], dram[f"{name}_b2"]).then_inc(weights_in, 16)
            if shared:
                sp.dma_start(router_b[:], dram[f"{name}_router_b"]).then_inc(weights_in, 16)
            if capacity:
                sp.dma_start(earlier[:], dram["earlier"]).then_inc(weights_in, 16)
                sp.dma_start(ones[:], dram["ones"]).then_inc(weights_in, 16)

        @block.tensor
        def _(pe):
            pe.wait_ge(weights_in, 16 * loads)
            with pe.Fori(0, PAIRS // 2) as m:
                for k in range(2):
                    pe.wait_ge(logit_rows_down, m * 2)
                    pe.matmul(rbank[k][0:EXPERTS, :], router[:], source_t[:, bass.ds(m * (2 * PN) + k * PN, PN)],
                              start=True, stop=True).then_inc(logit_rows_up, 1)
                for k in range(2):
                    pe.wait_ge(logit_rows_down, m * 2 + k + 1)
                    pe.wait_ge(logits_down, m * 2)
                    for t in range(PT):
                        last = pe.matmul(obank[k][:, t * EXPERTS:(t + 1) * EXPERTS],
                                         logit_rows[:, k, t * P:(t + 1) * P],
                                         core.ident[0:EXPERTS, 0:EXPERTS], start=True, stop=True)
                    last.then_inc(logits_up, 1)
            if capacity:
                pe.wait_ge(picks_ready, 1)
                flat = picked[:].rearrange("p t e -> p (t e)")
                pe.matmul(hbank[0][:, 0:TILES * EXPERTS], earlier[:], flat, start=True, stop=True)
                pe.matmul(hbank[1][:, 0:TILES * EXPERTS], ones[:], flat, start=True,
                          stop=True).then_inc(ranks_ready, 1)
                pe.wait_ge(ranks_taken, 1)
            pe.wait_ge(logits_down, PAIRS)

            def pair(i, has_tail):
                def up(e):
                    for f in range(chunks):
                        n = e * chunks + f
                        if not (isinstance(i, int) and n < 4):
                            pe.wait_ge(hidden_done, i * per_pair + n - 3)
                        pe.matmul(hbank[n % 4][:], w1[:, e, f * P:(f + 1) * P], source_t[:, bass.ds(i * PN, PN)],
                                  start=True, stop=True).then_inc(hidden_up, 1)

                def down(e):
                    pe.wait_ge(hidden_done, i * per_pair + (e + 1) * chunks)
                    if (turn := slot_turn(i, e)) is not None:
                        pe.wait_ge(out_taken, turn)
                    for t in range(PT):
                        for f in range(chunks):
                            last = pe.matmul(obank[e % 2][:, t * P:(t + 1) * P], hid[:, e % 2, f, t * P:(t + 1) * P],
                                             w2[:, e, f, :], start=(f == 0), stop=(f == chunks - 1))
                    last.then_inc(out_up, 1)

                up(0)
                for e in range(1, heads + 1):
                    if e < heads:
                        up(e)
                    if e == 2 and bias:
                        pe.wait_ge(rows_staged, i + 1)
                        for t in range(PT):
                            last = pe.matmul(small[:, t * P:(t + 1) * P], weight_rows[:, t * P:(t + 1) * P], b2[:],
                                             start=True, stop=True)
                        last.then_inc(bias_up, 1)
                    down(e - 1)
                    if e == 1 and bias:
                        pe.wait_ge(pair_staged, i + 1)
                        pe.wait_ge(bias_taken, i)
                        for t in range(PT):
                            last = pe.transpose(small[0:heads, t * P:(t + 1) * P], pair_weights[:, t, :],
                                                core.ident[:])
                        last.then_inc(pair_turned, 1)
                    if e == 3 and has_tail and tail.turned:
                        tail.pe(pe, i - 1)

            pair(0, False)
            with pe.Fori(1, PAIRS) as i:
                pair(i, True)
            if tail.turned:
                tail.pe(pe, PAIRS - 1)

        @block.scalar
        def _(act):
            act.wait_ge(weights_in, 16 * loads)
            with act.Fori(0, PAIRS // 2) as m:
                for k in range(2):
                    act.wait_ge(logit_rows_up, m * 2 + k + 1)
                    act.wait_ge(logits_up, m * 2)
                    act.activation(logit_rows[:, k, :], rbank[k][0:EXPERTS, :], ACT.Identity,
                                   bias=router_b[:, 0:1] if shared else 0.0).then_inc(logit_rows_down, 1)
            act.wait_ge(exp_asked, 1)
            act.activation(weights[:], weights[:], ACT.Exp).then_inc(exp_done, 1)

            def pair(i, has_tail):
                for e in range(heads):
                    if (turn := slot_turn(i, e)) is not None:
                        act.wait_ge(out_up, turn)
                    for f in range(chunks):
                        n = e * chunks + f
                        act.wait_ge(hidden_up, i * per_pair + n + 1)
                        act.activation(hid[:, e % 2, f, :], hbank[n % 4][:], ACT.Gelu_apprx_tanh,
                                       bias=b1[:, n:n + 1] if bias else 0.0).then_inc(hidden_done, 1)
                    if e == 1 and bias:
                        act.wait_ge(pair_turned, i + 1)
                        act.wait_ge(bias_up, i)
                        act.activation(weight_rows[:], small[0:heads, :], ACT.Identity).then_inc(rows_staged, 1)
                    if e == 3 and has_tail and tail.turned:
                        tail.act(act, i - 1)

            pair(0, False)
            with act.Fori(1, PAIRS) as i:
                pair(i, True)
            if tail.turned:
                tail.act(act, PAIRS - 1)

        @block.gpsimd
        def _(pool):
            with pool.Fori(0, PAIRS) as i:
                tail.pool(pool, i)

        @block.vector
        def _(dve):
            with dve.Fori(0, PAIRS // 2) as m:
                for k in range(2):
                    dve.wait_ge(logits_up, m * 2 + k + 1)
                    dve.tensor_copy(logits[:, bass.ds(m * (2 * PT) + k * PT, PT), :],
                                    obank[k][:, 0:PT * EXPERTS].rearrange("p (t e) -> p t e", e=EXPERTS)
                                    ).then_inc(logits_down, 1)
            dve.drain()
            gate(dve)
            if capacity:
                dve.sem_inc(picks_ready, 1)
                dve.wait_ge(weights_in, 16 * loads)
                dve.wait_ge(ranks_ready, 1)
                dve.tensor_copy(counts[:].rearrange("p t e -> p (t e)"), hbank[1][:, 0:TILES * EXPERTS])
                dve.memset(before[:], 0.0)
                dve.drain()
                for e in range(EXPERTS):
                    dve.tensor_tensor_scan(before[:, 1:TILES, e], ones[:, 0:TILES - 1], counts[:, 0:TILES - 1, e], 0.0,
                                           ALU.mult, ALU.add)
                dve.drain()
                dve.tensor_tensor(before[:], before[:],
                                  hbank[0][:, 0:TILES * EXPERTS].rearrange("p (t e) -> p t e", e=EXPERTS),
                                  ALU.add).then_inc(ranks_taken, 1)
                dve.drain()
                dve.tensor_scalar(fits[:], before[:], float(capacity), None, ALU.is_lt)
                dve.drain()
                dve.tensor_tensor(weights[:], weights[:], fits[:], ALU.mult)
                dve.drain()
            if bias and shared:
                dve.memset(pair_weights[:], 1.0)
                dve.drain()

            def stage(i):
                if not (isinstance(i, int) and i == 0):
                    dve.wait_ge(pair_turned, i)
                dve.tensor_copy(pair_weights[:, :, first_routed:heads],
                                weights[:, bass.ds(i * PT, PT), :]).then_inc(pair_staged, 1)

            def pair(i, has_next):
                if bias:
                    dve.wait_ge(bias_up, i + 1)
                    dve.tensor_copy(core.branch[:].rearrange("p t c -> p (t c)"), small[:]).then_inc(bias_taken, 1)
                else:
                    dve.tensor_copy(core.branch[:], base[:, bass.ds(i * PT, PT), :])
                dve.drain()
                for e in range(heads):
                    dve.wait_ge(out_up, i * heads + e + 1)
                    if e < first_routed:
                        last = dve.tensor_tensor(core.branch[:].rearrange("p t c -> p (t c)"), obank[e % 2][:],
                                                 core.branch[:].rearrange("p t c -> p (t c)"), ALU.add)
                    else:
                        for t in range(PT):
                            last = dve.scalar_tensor_tensor(
                                core.branch[:, t, :], obank[e % 2][:, t * P:(t + 1) * P],
                                weights[:, i * PT + t, e - first_routed:e - first_routed + 1],
                                core.branch[:, t, :], ALU.mult, ALU.add)
                    last.then_inc(out_taken, 1)
                    dve.drain()
                if bias and has_next:
                    stage(i + 1)
                tail.dve(dve, i)

            if bias:
                stage(0)
            with dve.Fori(0, PAIRS - 1) as i:
                pair(i, True)
            pair(PAIRS - 1, False)


class TurnedNorm:

    def __init__(self, core, name, ctx, bank, eps=None):
        self.core, self.bank = core, bank
        self.norm = Norm(core, name, PT, core.eps if eps is None else eps, core.norm_buffers(name, PT, ctx))
        self.rows = core.sb(f"{name}_rows", [P, PT, C], ctx=ctx)
        self.rows_ready, self.turned = core.sem(f"{name}_rows_ready"), core.sem(f"{name}_turned")
        self.taken = core.sem(f"{name}_taken")

    def dve(self, dve, i, row_of):
        self.norm.find_moments(dve, row_of)
        self.dve_rows(dve, i, row_of)

    def dve_rows(self, dve, i, row_of):
        dve.wait_ge(self.turned, i)
        self.norm.apply(dve, i, lambda r: self.rows[:, r, :], row_of).then_inc(self.rows_ready, 1)

    def pool(self, pool, i):
        self.norm.power(pool, i)

    def pe(self, pe, i):
        pe.wait_ge(self.rows_ready, i + 1)
        pe.wait_ge(self.taken, i)
        for t in range(PT):
            last = pe.transpose(self.bank[:, t * P:(t + 1) * P], self.rows[:, t, :], self.core.ident[:])
        last.then_inc(self.turned, 1)

    def act(self, act, i, out, scale, shift):
        act.wait_ge(self.turned, i + 1)
        return act.activation(out, self.bank[:], ACT.Identity, bias=shift, scale=scale).then_inc(self.taken, 1)


def attention_over_sequences(core):
    nc, dram = core.nc, core.dram
    HEADS, GROUPS, HD = 16, 4, 8
    PER = HEADS // GROUPS
    GW = (PER + 2) * HD
    LAGS = SEQS
    SCALE = float(1.0 / np.sqrt(HD).astype(np.float32))
    with ExitStack() as ctx:
        qkv = core.sb("attn_qkv", [P, TILES, GROUPS * GW], ctx=ctx)
        scores = core.sb("attn_scores", [P, TILES * HEADS, LAGS], ctx=ctx)
        mixed = core.sb("attn_mixed", [P, TILES, C], ctx=ctx)
        products = core.sb("attn_products", [P, 2, TILES * PER * HD], ctx=ctx)
        own = core.sb("attn_own_product", [P, TILES * PER * HD], ctx=ctx)
        top = core.sb("attn_top", [P, TILES * HEADS], ctx=ctx)
        share = core.sb("attn_share", [P, TILES * HEADS], ctx=ctx)
        cols = core.sb("attn_cols", [P, 4], ctx=ctx)
        wqkv = core.sb("attn_wqkv", [P, GROUPS * GW], ctx=ctx)
        wproj = core.sb("attn_wproj", [P, C], ctx=ctx)
        xt = core.sb("attn_xt", [P, PN], ctx=ctx)
        weights_in = core.sem("attn_weights_in")

        with ExitStack() as inner:
            ln1 = TurnedNorm(core, "attn_ln1", inner, core.bank[0])
            xt_ready, qkv_up, qkv_down = core.sem("attn_xt_ready"), core.sem("attn_qkv_up"), core.sem("attn_qkv_down")
            block = inner.enter_context(nc.Block())

            @block.sync
            def _(sp):
                sp.dma_start(cols[:], dram["attn_cols"]).then_inc(weights_in, 16)
                sp.dma_start(wqkv[:], dram["attn_wqkv"]).then_inc(weights_in, 16)
                sp.dma_start(wproj[:], dram["attn_wproj"]).then_inc(weights_in, 16)

            @block.vector
            def _(dve):
                def normalise(i):
                    ln1.dve(dve, i, lambda r: core.normed[:, i * PT + r, :])

                def pair(i, has_next):
                    if has_next:
                        normalise(i + 1)
                    dve.wait_ge(qkv_up, i + 1)
                    for h in range(2):
                        last = dve.tensor_copy(qkv[:, bass.ds(i * PT + 2 * h, 2), :],
                                               core.bank[1 + h][:, 0:2 * GROUPS * GW].rearrange(
                                                   "p (t c) -> p t c", t=2))
                    last.then_inc(qkv_down, 1)

                normalise(0)
                with dve.Fori(0, PAIRS - 1) as i:
                    pair(i, True)
                pair(PAIRS - 1, False)

            @block.gpsimd
            def _(pool):
                with pool.Fori(0, PAIRS) as i:
                    ln1.pool(pool, i)

            @block.tensor
            def _(pe):
                pe.wait_ge(weights_in, 48)

                def pair(i, has_next):
                    pe.wait_ge(xt_ready, i + 1)
                    pe.wait_ge(qkv_down, i)
                    for t in range(PT):
                        last = pe.matmul(core.bank[1 + t // 2][:, (t % 2) * GROUPS * GW:(t % 2 + 1) * GROUPS * GW],
                                         xt[:, t * P:(t + 1) * P], wqkv[:], start=True, stop=True)
                    last.then_inc(qkv_up, 1)
                    if has_next:
                        ln1.pe(pe, i + 1)

                ln1.pe(pe, 0)
                with pe.Fori(0, PAIRS - 1) as i:
                    pair(i, True)
                pair(PAIRS - 1, False)

            @block.scalar
            def _(act):
                act.wait_ge(weights_in, 48)
                with act.Fori(0, PAIRS) as i:
                    act.wait_ge(qkv_up, i)
                    ln1.act(act, i, xt[:], cols[:, 0:1], cols[:, 1:2])
                    act.drain()
                    act.sem_inc(xt_ready, 1)

        with ExitStack() as inner:
            product_ready, product_used = core.sem("attn_product_ready"), core.sem("attn_product_used")
            share_ready = core.sem("attn_share_ready")
            exp_asked, exp_done = core.sem("attn_exp_asked"), core.sem("attn_exp_done")
            block = inner.enter_context(nc.Block())
            steps = [(lag, g) for lag in range(LAGS) for g in range(GROUPS)]
            by_group = qkv[:].rearrange("p t (g c) -> p t g c", g=GROUPS)
            by_head = scores[:].rearrange("p (t h) l -> p t h l", h=HEADS)

            by_dve = [n % 3 == 2 for n in range(len(steps))]
            numbers = [n - sum(by_dve[:n]) for n in range(len(steps))]
            POOL_STEPS = len(steps) - sum(by_dve)

            def product(n, count):
                buffer = own[:] if by_dve[n] else products[:, numbers[n] % 2, :]
                return buffer[:, 0:count * PER * HD].rearrange("p (t q d) -> p t q d", q=PER, d=HD)

            def score_product(eng, n, lag, g):
                count = TILES - 2 * lag
                queries = by_group[:, 2 * lag:, g, 0:PER * HD].rearrange("p t (q d) -> p t q d", d=HD)
                keys = by_group[:, 0:count, g, PER * HD:(PER + 1) * HD].unsqueeze(2)
                return eng.tensor_tensor(product(n, count), queries, keys.broadcast_to([P, count, PER, HD]), ALU.mult)

            def value_product(eng, n, lag, g):
                count = TILES - 2 * lag
                share_of = by_head[:, 2 * lag:, g * PER:(g + 1) * PER, lag].unsqueeze(3)
                values = by_group[:, 0:count, g, (PER + 1) * HD:].unsqueeze(2)
                return eng.tensor_tensor(product(n, count), share_of.broadcast_to([P, count, PER, HD]),
                                         values.broadcast_to([P, count, PER, HD]), ALU.mult)

            @block.gpsimd
            def _(pool):
                for n, (lag, g) in enumerate(steps):
                    if by_dve[n]:
                        continue
                    if numbers[n] >= 2:
                        pool.wait_ge(product_used, numbers[n] - 1)
                    score_product(pool, n, lag, g).then_inc(product_ready, 1)
                pool.wait_ge(share_ready, 1)
                for n, (lag, g) in enumerate(steps):
                    if by_dve[n]:
                        continue
                    pool.wait_ge(product_used, POOL_STEPS + numbers[n] - 1)
                    value_product(pool, n, lag, g).then_inc(product_ready, 1)

            @block.scalar
            def _(act):
                act.wait_ge(exp_asked, 1)
                act.activation(scores[:], scores[:], ACT.Exp).then_inc(exp_done, 1)

            @block.vector
            def _(dve):
                dve.memset(scores[:], -BIG)
                dve.drain()
                for n, (lag, g) in enumerate(steps):
                    count = TILES - 2 * lag
                    if by_dve[n]:
                        score_product(dve, n, lag, g)
                        dve.drain()
                    else:
                        dve.wait_ge(product_ready, numbers[n] + 1)
                    last = dve.tensor_reduce(by_head[:, 2 * lag:, g * PER:(g + 1) * PER, lag], product(n, count),
                                             AX.X, ALU.add)
                    if by_dve[n]:
                        dve.drain()
                    else:
                        last.then_inc(product_used, 1)
                dve.drain()
                dve.tensor_reduce(top[:], scores[:], AX.X, ALU.max)
                dve.drain()
                dve.tensor_tensor(scores[:], scores[:],
                                  top[:].unsqueeze(2).broadcast_to([P, TILES * HEADS, LAGS]), ALU.subtract)
                dve.drain()
                dve.tensor_scalar(scores[:], scores[:], SCALE, None, ALU.mult)
                dve.drain()
                dve.sem_inc(exp_asked, 1)
                dve.wait_ge(exp_done, 1)
                dve.tensor_reduce(top[:], scores[:], AX.X, ALU.add)
                dve.drain()
                dve.reciprocal(share[:], top[:])
                dve.sem_inc(share_ready, 1)
                for n, (lag, g) in enumerate(steps):
                    count = TILES - 2 * lag
                    if by_dve[n]:
                        value_product(dve, n, lag, g)
                        dve.drain()
                    else:
                        dve.wait_ge(product_ready, POOL_STEPS + numbers[n] + 1)
                    mix = mixed[:, 2 * lag:, g * PER * HD:(g + 1) * PER * HD].rearrange("p t (q d) -> p t q d", d=HD)
                    if lag == 0:
                        last = dve.tensor_copy(mix, product(n, count))
                    else:
                        last = dve.tensor_tensor(mix, mix, product(n, count), ALU.add)
                    if not by_dve[n]:
                        last.then_inc(product_used, 1)
                    if by_dve[n] or g == GROUPS - 1:
                        dve.drain()

        with ExitStack() as inner:
            ln2 = TurnedNorm(core, "attn_ln2", inner, core.bank[0])
            scaled = core.sb("attn_scaled", [P, PT, C], ctx=inner)
            scaled_ready, scaled_turned = core.sem("attn_scaled_ready"), core.sem("attn_scaled_turned")
            mix_t_ready = core.sem("attn_mix_t_ready")
            proj_up, proj_down = core.sem("attn_proj_up"), core.sem("attn_proj_down")
            block = inner.enter_context(nc.Block())

            @block.vector
            def _(dve):
                share_rows = share[:].rearrange("p (t h) -> p t h", h=HEADS)

                def scale(i):
                    dve.wait_ge(scaled_turned, i)
                    for t in range(PT):
                        last = dve.tensor_tensor(scaled[:, t, :].rearrange("p (h d) -> p h d", d=HD),
                                                 mixed[:, i * PT + t, :].rearrange("p (h d) -> p h d", d=HD),
                                                 share_rows[:, i * PT + t, :].unsqueeze(2).broadcast_to([P, HEADS, HD]),
                                                 ALU.mult)
                    last.then_inc(scaled_ready, 1)

                def pair(i, has_next):
                    dve.wait_ge(proj_up, i + 1)
                    h1 = core.normed[:, bass.ds(i * PT, PT), :]
                    dve.tensor_tensor(h1, core.bank[1][:].rearrange("p (t c) -> p t c", c=C), h1,
                                      ALU.add).then_inc(proj_down, 1)
                    dve.drain()
                    rows = lambda r: core.normed[:, i * PT + r, :]
                    ln2.norm.find_moments(dve, rows)
                    if has_next:
                        scale(i + 1)
                    ln2.dve_rows(dve, i, rows)

                scale(0)
                with dve.Fori(0, PAIRS - 1) as i:
                    pair(i, True)
                pair(PAIRS - 1, False)

            @block.gpsimd
            def _(pool):
                with pool.Fori(0, PAIRS) as i:
                    ln2.pool(pool, i)

            @block.tensor
            def _(pe):
                def turn(i):
                    pe.wait_ge(scaled_ready, i + 1)
                    pe.wait_ge(mix_t_ready, i)
                    for t in range(PT):
                        last = pe.transpose(core.bank[2][:, t * P:(t + 1) * P], scaled[:, t, :], core.ident[:])
                    last.then_inc(scaled_turned, 1)

                def pair(i, has_next):
                    pe.wait_ge(mix_t_ready, i + 1)
                    pe.wait_ge(proj_down, i)
                    for t in range(PT):
                        last = pe.matmul(core.bank[1][:, t * P:(t + 1) * P], xt[:, t * P:(t + 1) * P], wproj[:],
                                         start=True, stop=True)
                    last.then_inc(proj_up, 1)
                    if has_next:
                        turn(i + 1)
                    ln2.pe(pe, i)

                turn(0)
                with pe.Fori(0, PAIRS - 1) as i:
                    pair(i, True)
                pair(PAIRS - 1, False)

            @block.scalar
            def _(act):
                def store(i):
                    act.wait_ge(scaled_turned, i + 1)
                    act.wait_ge(proj_up, i)
                    act.activation(xt[:], core.bank[2][:], ACT.Identity).then_inc(mix_t_ready, 1)

                def pair(i, has_next):
                    if has_next:
                        store(i + 1)
                    ln2.act(act, i, core.normed_t[:, bass.ds(i * PN, PN)], cols[:, 2:3], cols[:, 3:4])

                store(0)
                with act.Fori(0, PAIRS - 1) as i:
                    pair(i, True)
                pair(PAIRS - 1, False)


class Rms(Norm):

    def power(self, pool, turn):
        core, n = self.core, self.rows
        pool.wait_ge(self.moments_ready, turn + 1)
        pool.tensor_tensor(self.rstd[:], self.moments[:, :, 0], self.moments[:, :, 0], ALU.mult)
        pool.tensor_tensor(self.shifted[:], self.moments[:, :, 1], self.eps[:, 0:n], ALU.add)
        pool.drain()
        pool.tensor_tensor(self.shifted[:], self.shifted[:], self.rstd[:], ALU.add)
        pool.drain()
        pool.tensor_tensor(self.rstd[:], self.shifted[:], core.minus_half[:, 0:n], ALU.pow).then_inc(self.rstd_ready, 1)

    def scale(self, dve, turn, out_of, row_of):
        dve.wait_ge(self.rstd_ready, turn + 1)
        for r in range(self.rows):
            last = dve.tensor_scalar(out_of(r), row_of(r), self.rstd[:, r:r + 1], None, ALU.mult)
        return last


def ssm_block(core, name, tail, heads, mamba):
    nc, dram = core.nc, core.dram
    INNER, STATE, TAPS = 2 * C, 64, 4
    HD = INNER // heads
    CH = INNER // P
    EACH = heads // CH
    bc_items = 2 if mamba else 2 * heads * STATE // P
    units = 2 * heads
    SPAN = 3 * P
    items = ([("turn_in", 0)] if mamba else []) + [("x", c) for c in range(CH)] + [("dt", 0)]
    bc_order = list(range(bc_items)) if mamba else [*range(bc_items // 2, bc_items), *range(bc_items // 2)]
    items += [("bc", b) for b in bc_order] + [("gate", g) for g in range(2)]
    items += ([("turn_dt", 0)] if mamba else []) + [("turn_x", c) for c in range(CH)]
    late_items = [("turn_y", 1), ("out", 0)]
    LATE_AT = 6
    first_items = items + [("turn_y", 0)]
    items = items[:LATE_AT] + late_items + items[LATE_AT:] + [("turn_y", 0)]
    W = len(items)
    assert W % 2 == 0
    tail_at = (0, 2, 4, 6) if mamba else (1, 4, 7, 10)
    with ExitStack() as ctx:
        sb = lambda n, shape, dtype=F32: core.sb(f"{name}_{n}", shape, dtype, ctx=ctx)
        sem = lambda n: core.sem(f"{name}_{n}")
        wx, wdt = sb("wx", [P, INNER]), sb("wdt", [P, heads])
        wbc, wgate = sb("wbc", [P, bc_items, P if not mamba else STATE]), sb("wgate", [P, INNER])
        wout, taps, cols = sb("wout", [P, CH, C]), sb("taps", [P, CH, TAPS + 1]), sb("cols", [P, CH])
        head_cols = sb("head_cols", [heads, 2])
        pick, unpick = sb("pick", [96, heads, P], BF16), sb("unpick", [96, heads], BF16)
        ident16, future = sb("ident16", [P, P], BF16), sb("future", [P, P], BF16)
        padded = sb("padded", [P, CH, 2, SEQ + TAPS - 1])
        conv = sb("conv", [P, CH, 2, SEQ])
        if mamba:
            x_rows = sb("x_rows", [P, PT, INNER])
            bc = sb("bc", [P, bc_items, PN])
        else:
            x_wide = sb("x_wide", [P, PT, CH, EACH * (P + HD)])
            b_rows, c_rows = sb("b_rows", [P, bc_items // 2, PN]), sb("c_rows", [P, 2, bc_items // 2, PN])
            squares, sums, shares = sb("squares", [P, CH, 2, SEQ]), sb("sums", [P, PT]), sb("shares", [P, PT])
            ones_col = sb("ones_col", [P, 1])
            summed = sem("summed")
        gate = sb("gate", [P, PT, INNER])
        raw, bent, delta, logs, cum = (sb(n, [heads, PN]) for n in ("raw", "bent", "delta", "logs", "cum"))
        ones_dt = sb("ones_dt", [heads, SEQ])
        part16, parts = sb("part16", [heads, PN], BF16), sb("parts", [96, PN], BF16)
        decay, mixer = sb("decay", [P, 2, SPAN]), sb("mixer", [P, 2, SPAN])
        if mamba:
            gated, gated_t = sb("gated", [P, PT, INNER]), sb("gated_t", [P, PT, CH, P])
        else:
            gated_t = sb("gated_t", [P, CH, PN])
        if mamba:
            dt_rows, scores = sb("dt_rows", [P, PT, heads]), sb("scores", [P, SPAN])
            scaled, in_t = sb("scaled", [P, PT, C]), sb("in_t", [P, PN])
            rms_eps = sb("rms_eps", [P, 16])
            rms = Rms(core, f"{name}_rms", PT, rms_eps, core.norm_buffers(f"{name}_rms", PT, ctx))
            scaled_ready = sem("scaled_ready")
            in_rows = in_t
        else:
            magnitude = sb("magnitude", [heads, PN])
            in_rows, staged = sb("in_rows", [P, PN]), sem("staged")
            rms_eps = sb("rms_eps", [P, 16])
            rms = Rms(core, f"{name}_rms", PT, rms_eps, core.norm_buffers(f"{name}_rms", PT, ctx))
        weights_in, ready = sem("weights_in"), sem("ready")
        up = sem("work_up")
        down = [sem("work_down_even"), sem("work_down_odd")]
        padded_ready, conv_ready, x_bent = sem("padded_ready"), sem("conv_ready"), sem("x_bent")
        raw_ready, soft_ready, parts_ready = sem("raw_ready"), sem("soft_ready"), sem("parts_ready")
        delta_ready = sem("delta_ready")
        decay_up, decay_done = sem("decay_up"), sem("decay_done")
        scores_up, scores_taken = sem("scores_up"), sem("scores_taken")
        mixer_done, y_up, y_taken = sem("mixer_done"), sem("y_up"), sem("y_taken")
        out_stored = sem("out_stored")
        gated_ready, folded, squared = sem("gated_ready"), sem("folded"), sem("squared")
        dbank, gbank, ybank, work = core.bank[0:2], core.bank[2:4], core.bank[4], core.bank[5:7]
        loads = 12
        block = ctx.enter_context(nc.Block())

        def place(i, kind, n):
            if (kind, n) in late_items:
                w, i = late_items.index((kind, n)), i + 1
                if not (isinstance(i, int) and i == PAIRS):
                    w += LATE_AT
            elif isinstance(i, int) and i == 0:
                w = first_items.index((kind, n))
                return w, w % 2, w // 2
            else:
                w = items.index((kind, n))
            return i * W - len(late_items) + w, w % 2, i * (W // 2) - 1 + w // 2

        def wait_up(eng, i, kind, n):
            eng.wait_ge(up, place(i, kind, n)[0] + 1)

        @block.sync
        def _(sp):
            for to, what in ((wx, "wx"), (wdt, "wdt"), (wbc, "wbc"), (wgate, "wgate"), (wout, "wout"), (taps, "taps"),
                             (cols, "cols"), (head_cols, "head_cols"), (pick, "pick"), (unpick, "unpick"),):
                sp.dma_start(to[:], dram[f"{name}_{what}"]).then_inc(weights_in, 16)
            sp.dma_start(ident16[:], dram["identity16"]).then_inc(weights_in, 16)
            sp.dma_start(future[:], dram["future"]).then_inc(weights_in, 16)

        @block.gpsimd
        def _(pool):
            pool.memset(rms_eps[:], 1e-6 if mamba else 1.1920928955078125e-07)
            pool.memset(ones_dt[:], 1.0)
            pool.memset(parts[:], 0.0)
            pool.memset(padded[:], 0.0)
            if not mamba:
                pool.memset(x_wide[:], 0.0)
                pool.memset(shares[:], 1.0 / INNER)
                pool.memset(ones_col[:], 1.0)
            pool.drain()
            pool.sem_inc(ready, 1)
            if mamba:
                rms.power(pool, 0)
                with pool.Fori(1, PAIRS) as i:
                    rms.power(pool, i)
                    tail.pool(pool, i - 1)
                tail.pool(pool, PAIRS - 1)
                return
            with pool.Fori(0, PAIRS) as i:
                pool.wait_ge(summed, i + 1)
                pool.tensor_tensor(rms.shifted[:], sums[:], shares[:], ALU.mult)
                pool.drain()
                pool.tensor_tensor(rms.shifted[:], rms.shifted[:], rms.eps[:, 0:PT], ALU.add)
                pool.drain()
                pool.tensor_tensor(rms.rstd[:], rms.shifted[:], core.minus_half[:, 0:PT], ALU.pow).then_inc(
                    rms.rstd_ready, 1)
                tail.pool(pool, i)

        @block.tensor
        def _(pe):
            pe.wait_ge(weights_in, 16 * loads)
            pe.wait_ge(folded, 1)

            source = in_rows[:]

            def run_item(i, kind, n):
                _, side, before = place(i, kind, n)
                if not (isinstance(before, int) and before < 1):
                    pe.wait_ge(down[side], before)
                bank = work[side]
                if kind == "turn_in":
                    pe.wait_ge(scaled_ready, i + 1)
                    for t in range(PT):
                        last = pe.transpose(bank[:, t * P:(t + 1) * P], scaled[:, t, :], core.ident[:])
                elif kind == "x":
                    if mamba and n == 0:
                        pe.wait_ge(down[place(i, "turn_in", 0)[1]], place(i, "turn_in", 0)[2] + 1)
                    last = pe.matmul(bank[:], wx[:, n * P:(n + 1) * P], source, start=True, stop=True)
                elif kind == "dt":
                    last = pe.matmul(bank[0:heads, :], wdt[:], source, start=True, stop=True)
                elif kind == "bc":
                    rows = STATE if mamba else P
                    last = pe.matmul(bank[0:rows, :], wbc[:, n, :], source, start=True, stop=True)
                elif kind == "gate" and not mamba:
                    last = pe.matmul(bank[:], wgate[:, n * P:(n + 1) * P], source, start=True, stop=True)
                elif kind == "gate":
                    for t in range(2):
                        tile = 2 * n + t
                        last = pe.matmul(bank[:, t * INNER:(t + 1) * INNER], in_rows[:, tile * P:(tile + 1) * P],
                                         wgate[:], start=True, stop=True)
                elif kind == "turn_x":
                    pe.wait_ge(x_bent, i * CH + n + 1)
                    flat = conv[:, n].rearrange("p j t -> p (j t)")
                    for t in range(PT):
                        last = pe.transpose(bank[:, t * P:(t + 1) * P], flat[:, t * P:(t + 1) * P], core.ident[:])
                elif kind == "turn_dt":
                    pe.wait_ge(delta_ready, i + 1)
                    for t in range(PT):
                        last = pe.matmul(bank[:, t * heads:(t + 1) * heads], delta[:, t * P:(t + 1) * P],
                                         core.ident[0:heads, 0:heads], start=True, stop=True)
                elif kind == "turn_y" and not mamba:
                    pe.wait_ge(squared, i * 2 + n + 1)
                    for t in range(2):
                        for c in range(CH):
                            last = pe.matmul(bank[:, t:t + 1], squares[:, c, n, t * P:(t + 1) * P], ones_col[:],
                                             start=(c == 0), stop=(c == CH - 1))
                elif kind == "turn_y":
                    pe.wait_ge(gated_ready, i * 2 + n + 1)
                    for t in range(2):
                        for c in range(CH):
                            last = pe.transpose(bank[:, (t * CH + c) * P:(t * CH + c + 1) * P],
                                                gated[:, 2 * n + t, c * P:(c + 1) * P], core.ident[:])
                else:
                    _, side, before = place(i, "turn_y", 1)
                    pe.wait_ge(down[side], before + 1)
                    for t in range(PT):
                        for c in range(CH):
                            rows = gated_t[:, t, c, :] if mamba else gated_t[:, c, t * P:(t + 1) * P]
                            last = pe.matmul(bank[:, t * P:(t + 1) * P], rows, wout[:, c, :],
                                             start=(c == 0), stop=(c == CH - 1))
                last.then_inc(up, 1)

            def late_of(i):
                for kind, n in late_items:
                    run_item(i, kind, n)

            def pair(i, has_late):
                def item(kind, n):
                    run_item(i, kind, n)

                def unit(u):
                    j, h = divmod(u, heads)
                    n = i * units + u
                    s = [j * SEQ, j * SEQ + P]
                    bank = dbank[u % 2]
                    if not (isinstance(i, int) and u < 2):
                        pe.wait_ge(decay_done, n - 1)
                    for col, rows, width in ((0, s[0], SEQ), (SEQ, s[1], P)):
                        pe.matmul(bank[:, col:col + width], pick[:, h, :], parts[:, rows:rows + width],
                                  start=True, stop=False)
                        pe.matmul(bank[:, col:col + width], parts[:, rows:rows + P],
                                  unpick[:, h:h + 1].broadcast_to([96, width]), start=False, stop=False)
                        last = pe.matmul(bank[:, col:col + P], ident16[:], future[:], start=False, stop=True)
                    last.then_inc(decay_up, 1)
                    if mamba and h:
                        return
                    if mamba:
                        b, c = bc[0:STATE, 0, :], bc[0:STATE, 1, :]
                        turn_no = i * 2 + j
                        skip = isinstance(i, int) and j < 1
                        need = turn_no
                        gb = gbank[0]
                    else:
                        b, c = b_rows[:, h // 2, :], c_rows[:, h % 2, h // 2, :]
                        skip = isinstance(i, int) and u < 2
                        need = n - 1
                        gb = gbank[u % 2]
                    if not skip:
                        pe.wait_ge(scores_taken, need)
                    pe.matmul(gb[:, 0:SEQ], b[:, s[0]:s[0] + P], c[:, s[0]:s[0] + SEQ], start=True, stop=True)
                    pe.matmul(gb[:, SEQ:SPAN], b[:, s[1]:s[1] + P], c[:, s[1]:s[1] + P], start=True,
                              stop=True).then_inc(scores_up, 1)

                def mix(u):
                    j, h = divmod(u, heads)
                    pe.wait_ge(mixer_done, i * units + u + 1)
                    if h == 0 and not (isinstance(i, int) and j == 0):
                        pe.wait_ge(y_taken, i * 2 + j)
                    m = mixer[:, u % 2, :]
                    if not mamba:
                        c, k = divmod(h, EACH)
                        x = [x_wide[:, 2 * j + t, c, k * P:(k + 1) * P] for t in range(2)]
                        pe.matmul(ybank[:, c * SEQ:(c + 1) * SEQ], x[0], m[:, 0:SEQ], start=(k == 0), stop=False)
                        pe.matmul(ybank[:, c * SEQ + P:(c + 1) * SEQ], x[1], m[:, SEQ:SPAN], start=False,
                                  stop=(k == EACH - 1)).then_inc(y_up, 1)
                        return
                    at = [slice(t * INNER + h * HD, t * INNER + (h + 1) * HD) for t in range(2)]
                    x = [x_rows[:, 2 * j + t, h * HD:(h + 1) * HD] for t in range(2)]
                    pe.matmul(ybank[:, at[0]], m[:, 0:P], x[0], start=True, stop=True)
                    pe.matmul(ybank[:, at[1]], m[:, P:SEQ], x[0], start=True, stop=False)
                    pe.matmul(ybank[:, at[1]], m[:, SEQ:SPAN], x[1], start=False, stop=True).then_inc(y_up, 1)

                if not mamba:
                    pe.wait_ge(staged, i + 1)
                for w, (kind, n) in enumerate(first_items[:-1]):
                    if w == LATE_AT and has_late:
                        late_of(i - 1)
                    item(kind, n)
                pe.wait_ge(parts_ready, i + 1)
                for kind, n in first_items[-3:-1]:
                    _, side, before = place(i, kind, n)
                    pe.wait_ge(down[side], before + 1)
                unit(0)
                for u in range(units):
                    if u + 1 < units:
                        unit(u + 1)
                    if u == heads + (0 if mamba else 3):
                        item("turn_y", 0)
                    mix(u)
                    if u == tail_at[3] and has_late and tail.turned:
                        tail.pe(pe, i - 1)

            pair(0, False)
            with pe.Fori(1, PAIRS) as i:
                pair(i, True)
            late_of(PAIRS - 1)
            if tail.turned:
                tail.pe(pe, PAIRS - 1)

        @block.scalar
        def _(act):
            act.wait_ge(weights_in, 16 * loads)
            act.wait_ge(ready, 1)
            if not mamba:
                act.wait_ge(folded, 1)
            if mamba:
                act.activation(head_cols[:, 1:2], head_cols[:, 1:2], ACT.Exp).then_inc(soft_ready, 1)

            def pair(i, has_late):
                def take(kind, n):
                    if has_late and (kind, n) == first_items[LATE_AT]:
                        late_of(i - 1)
                    _, side, _ = place(i, kind, n)
                    wait_up(act, i, kind, n)
                    return work[side], down[side]

                if mamba:
                    bank, sign = take("turn_in", 0)
                    act.activation(in_t[:], bank[:], ACT.Identity, scale=cols[:, 0:1]).then_inc(sign, 1)
                for c in range(CH):
                    bank, sign = take("x", c)
                    act.wait_ge(conv_ready, i * CH)
                    ins = act.activation(padded[:, c, :, TAPS - 1:], bank[:].rearrange("p (j t) -> p j t", j=2),
                                         ACT.Identity)
                    ins.then_inc(sign, 1)
                act.drain()
                act.sem_inc(padded_ready, 1)
                bank, sign = take("dt", 0)
                act.wait_ge(parts_ready, i)
                act.activation(raw[:], bank[0:heads, :], ACT.Identity).then_inc(sign, 1)
                act.drain()
                act.activation(bent[:], raw[:], ACT.Abs, bias=head_cols[:, 0:1])
                if not mamba:
                    act.activation(magnitude[:], raw[:], ACT.Abs)
                act.drain()
                act.activation(bent[:], bent[:], ACT.Exp, scale=-1.0)
                act.drain()
                act.activation(bent[:], bent[:], ACT.Ln, bias=1.0)
                act.drain()
                act.sem_inc(raw_ready, 1)
                for b in bc_order:
                    if not mamba and b < bc_items // 2 and b % 2:
                        continue
                    bank, sign = take("bc", b)
                    rows = STATE if mamba else P
                    if b == bc_order[0]:
                        act.wait_ge(scores_up, i * (2 if mamba else units))
                    if mamba:
                        act.activation(bc[0:rows, b, :], bank[0:rows, :], ACT.Identity).then_inc(sign, 1)
                    elif b < bc_items // 2:
                        act.activation(b_rows[:, b, :], bank[:], ACT.Identity).then_inc(sign, 1)
                    else:
                        for half in range(2):
                            low = slice(half * STATE, (half + 1) * STATE)
                            act.activation(c_rows[low, half, b - bc_items // 2, :], bank[low, :], ACT.Identity)
                        act.drain()
                        act.sem_inc(sign, 1)
                for g in range(2):
                    bank, sign = take("gate", g)
                    act.wait_ge(y_taken, 2 * i)
                    act.activation(gate[:].rearrange("p t c -> p (t c)")[:, g * PN:(g + 1) * PN], bank[:],
                                   ACT.Silu if mamba else ACT.Sigmoid).then_inc(sign, 1)
                for c in range(CH):
                    act.wait_ge(conv_ready, i * CH + c + 1)
                    flat = conv[:, c].rearrange("p j t -> p (j t)")
                    act.activation(flat, flat, ACT.Silu).then_inc(x_bent, 1)
                for u in range(units):
                    n = i * units + u
                    act.wait_ge(decay_up, n + 1)
                    if not (isinstance(i, int) and u < 2):
                        act.wait_ge(mixer_done, n - 1)
                    act.activation(decay[:, u % 2, :], dbank[u % 2][:, 0:SPAN], ACT.Exp).then_inc(decay_done, 1)
                    if u == heads + 1 and not mamba:
                        square(i, 0)
                    if u == heads + (1 if mamba else 4):
                        turned_y(i, 0)
                    if u == tail_at[3] and has_late and tail.turned:
                        tail.act(act, i - 1)
                if not mamba:
                    square(i, 1)

            def late_of(i):
                turned_y(i, 1)
                if not mamba:
                    act.drain()
                    act.sem_inc(summed, 1)
                _, side, _ = place(i, "out", 0)
                wait_up(act, i, "out", 0)
                act.activation(core.branch[:].rearrange("p t c -> p (t c)"), work[side][:], ACT.Identity)
                act.drain()
                act.sem_inc(down[side], 1)
                act.sem_inc(out_stored, 1)

            def square(i, j):
                act.wait_ge(gated_ready, i * 2 + j + 1)
                act.activation(squares[:, :, j, :], gated_t[:, :, j * SEQ:(j + 1) * SEQ], ACT.Square).then_inc(squared, 1)

            def turned_y(i, j):
                _, w, _ = place(i, "turn_y", j)
                wait_up(act, i, "turn_y", j)
                if not mamba:
                    act.activation(sums[:, 2 * j:2 * j + 2], work[w][:, 0:2], ACT.Identity).then_inc(down[w], 1)
                    return
                act.activation(gated_t[:, 2 * j:2 * j + 2].rearrange("p t c k -> p (t c k)"), work[w][:],
                               ACT.Identity).then_inc(down[w], 1)

            pair(0, False)
            with act.Fori(1, PAIRS) as i:
                pair(i, True)
            late_of(PAIRS - 1)
            if tail.turned:
                tail.act(act, PAIRS - 1)

        @block.vector
        def _(dve):
            if not mamba:
                dve.memset(c_rows[:], 0.0)
            dve.wait_ge(weights_in, 16 * loads)
            dve.wait_ge(ready, 1)
            if mamba:
                dve.wait_ge(soft_ready, 1)
                dve.tensor_scalar(head_cols[:, 1:2], head_cols[:, 1:2], -1.0, None, ALU.mult)
            else:
                for c in range(CH):
                    dve.tensor_scalar(wout[:, c, :], wout[:, c, :], cols[:, c:c + 1], None, ALU.mult)
            dve.drain()
            dve.sem_inc(folded, 1)

            def used(i):
                if not (isinstance(i, int) and i == 0):
                    wait_up(dve, i - 1, "turn_x", CH - 1)

            def take_gated(i, j):
                dve.wait_ge(y_up, i * units + (j + 1) * heads)
                if mamba:
                    dve.tensor_tensor(gated[:, 2 * j:2 * j + 2, :].rearrange("p t c -> p (t c)"), ybank[:],
                                      gate[:, 2 * j:2 * j + 2, :].rearrange("p t c -> p (t c)"),
                                      ALU.mult).then_inc(gated_ready, 1)
                else:
                    at = slice(j * SEQ, (j + 1) * SEQ)
                    dve.tensor_tensor(gated_t[:, :, at], ybank[:].rearrange("p (c t) -> p c t", c=CH),
                                      gate[:].rearrange("p a b -> p (a b)").rearrange(
                                          "p (c t) -> p c t", c=CH)[:, :, at], ALU.mult).then_inc(gated_ready, 1)
                dve.drain()
                dve.sem_inc(y_taken, 1)

            def take_out(i):
                dve.wait_ge(out_stored, i + 1)
                if mamba:
                    dve.tensor_tensor(core.branch[:], core.branch[:], core.normed[:, bass.ds(i * PT, PT), :], ALU.add)
                else:
                    rms.scale(dve, i, lambda r: core.branch[:, r, :], lambda r: core.branch[:, r, :])
                dve.drain()

            def pair(i, has_late):
                if mamba:
                    rms.find_moments(dve, lambda r: core.normed[:, i * PT + r, :])
                    used(i)
                    rms.scale(dve, i, lambda r: scaled[:, r, :],
                              lambda r: core.normed[:, i * PT + r, :]).then_inc(scaled_ready, 1)
                else:
                    used(i)
                    dve.tensor_copy(in_rows[:], core.normed_t[:, bass.ds(i * PN, PN)]).then_inc(staged, 1)
                if has_late:
                    take_gated(i - 1, 1)
                dve.wait_ge(padded_ready, i + 1)
                for k in range(TAPS):
                    for c in range(CH):
                        tap = taps[:, c, k:k + 1]
                        shifted = padded[:, c, :, k:k + SEQ]
                        if k == 0:
                            ins = dve.tensor_scalar(conv[:, c], shifted, tap, taps[:, c, TAPS:TAPS + 1],
                                                    ALU.mult, ALU.add)
                        else:
                            ins = dve.scalar_tensor_tensor(conv[:, c], shifted, tap, conv[:, c], ALU.mult, ALU.add)
                        if k == TAPS - 1:
                            ins.then_inc(conv_ready, 1)
                    dve.drain()
                dve.wait_ge(raw_ready, i + 1)
                dve.wait_ge(y_up, i * units)
                dve.tensor_scalar(delta[:], raw[:], head_cols[:, 0:1], 0.0, ALU.add, ALU.max)
                dve.drain()
                dve.tensor_tensor(delta[:], delta[:], bent[:], ALU.add).then_inc(delta_ready, 1)
                dve.drain()
                if mamba:
                    dve.tensor_scalar(logs[:], delta[:], head_cols[:, 1:2], None, ALU.mult)
                else:
                    dve.scalar_tensor_tensor(logs[:], delta[:], -1.0, magnitude[:], ALU.mult, ALU.mult)
                dve.drain()
                for j in range(2):
                    at = slice(j * SEQ, (j + 1) * SEQ)
                    dve.tensor_tensor_scan(cum[:, at], ones_dt[:], logs[:, at], 0.0, ALU.mult, ALU.add)
                dve.drain()
                for part in range(3):
                    dve.tensor_copy(part16[:], cum[:])
                    dve.drain()
                    dve.tensor_copy(parts[32 * part:32 * part + heads, :], part16[:])
                    if part < 2:
                        dve.tensor_tensor(cum[:], cum[:], part16[:], ALU.subtract)
                    dve.drain()
                dve.sem_inc(parts_ready, 1)
                if mamba:
                    _, w, _ = place(i, "turn_dt", 0)
                    wait_up(dve, i, "turn_dt", 0)
                    dve.tensor_copy(dt_rows[:].rearrange("p t h -> p (t h)"),
                                    work[w][:, 0:PT * heads]).then_inc(down[w], 1)
                    dve.drain()
                if not mamba:
                    dve.wait_ge(scores_up, i * units)
                    for b in range(1, bc_items // 2, 2):
                        _, w, _ = place(i, "bc", b)
                        wait_up(dve, i, "bc", b)
                        dve.tensor_copy(b_rows[:, b, :], work[w][:]).then_inc(down[w], 1)
                for c in range(CH):
                    _, w, _ = place(i, "turn_x", c)
                    wait_up(dve, i, "turn_x", c)
                    bank = work[w][:].rearrange("p (t k) -> p t k", t=PT)
                    if mamba:
                        out = x_rows[:, :, c * P:(c + 1) * P]
                    if mamba:
                        for t in range(PT):
                            each = heads // CH
                            ins = dve.tensor_tensor(out[:, t].rearrange("p (h d) -> p h d", d=HD),
                                                    bank[:, t].rearrange("p (h d) -> p h d", d=HD),
                                                    dt_rows[:, t, c * each:(c + 1) * each].unsqueeze(2).broadcast_to(
                                                        [P, each, HD]), ALU.mult)
                    else:
                        out = x_wide[:, :, c].rearrange("p t (h k) -> p t h k", k=P + HD)[:, :, :, 0:HD]
                        ins = dve.tensor_copy(out, bank.rearrange("p t (h d) -> p t h d", d=HD))
                    ins.then_inc(down[w], 1)
                for u in range(units):
                    j, h = divmod(u, heads)
                    n = i * units + u
                    if not mamba:
                        dve.wait_ge(scores_up, n + 1)
                        scored = gbank[u % 2][:, 0:SPAN]
                    elif h == 0:
                        dve.wait_ge(scores_up, i * 2 + j + 1)
                        dve.tensor_copy(scores[:], gbank[0][:, 0:SPAN]).then_inc(scores_taken, 1)
                        dve.drain()
                    if mamba:
                        scored = scores[:]
                    dve.wait_ge(decay_done, n + 1)
                    if u >= 2:
                        dve.wait_ge(y_up, n - 1)
                    ins = dve.tensor_tensor(mixer[:, u % 2, :], decay[:, u % 2, :], scored, ALU.mult)
                    ins.then_inc(mixer_done, 1)
                    if not mamba:
                        dve.drain()
                        dve.sem_inc(scores_taken, 1)
                    if u == heads - 1:
                        take_gated(i, 0)
                    if has_late:
                        if u == tail_at[0]:
                            take_out(i - 1)
                            tail.dve_branch(dve, i - 1)
                        elif u == tail_at[1]:
                            tail.dve_stream(dve, i - 1)
                        elif u == tail_at[2]:
                            tail.dve_fresh(dve, i - 1)

            pair(0, False)
            with dve.Fori(1, PAIRS) as i:
                pair(i, True)
            take_gated(PAIRS - 1, 1)
            take_out(PAIRS - 1)
            tail.dve(dve, PAIRS - 1)

class Carry(Tail):

    def dve_branch(self, dve, i):
        core = self.core
        dve.tensor_copy(core.normed[:, bass.ds(i * PT, PT), :], core.branch[:])
        dve.wait_ge(self.fresh_turned, i)
        dve.tensor_copy(core.fresh[:], core.branch[:]).then_inc(self.fresh_ready, 1)
        dve.drain()

    def dve_stream(self, dve, i):
        pass

    def dve_fresh(self, dve, i):
        pass

    def pool(self, pool, i):
        pass


def local_layer(core, layer, tail):
    nc, dram = core.nc, core.dram
    name = f"local{layer}"
    HEADS, HD = 8, 64
    INNER = HEADS * HD
    CH = INNER // P
    HID = int(C * 4 * 2 / 3)
    FC = -(-HID // P)
    HALF = C // 2
    SPAN = 3 * P
    UNITS = 2 * HEADS

    frame_slots = {0: (("v", 1, 0), ("q", 2, 0)), 1: (("v", 1, 1), ("k", 2, 0)), 2: (("q", 2, 1), ("turn_q", 1, 0)),
                   3: (("k", 2, 1), ("turn_k", 1, 0)), 4: (("turn_q", 1, 1),), 5: (("turn_k", 1, 1),)}
    first_items = [(kind, s, t) for s in range(2) for t in range(2) for kind in "qk"]
    first_items += [("v", 0, t) for t in range(2)] + [(kind, 0, t) for t in range(2) for kind in ("turn_q", "turn_k")]
    FRAME = sum(len(x) for x in frame_slots.values())

    def frame_base(s):
        full = len(first_items) + FRAME * s
        return full - len("qkqk") if isinstance(s, int) and s == SEQS - 1 else full

    def frame_items(i, h, j):
        s = 2 * i + j
        live = lambda ahead: not isinstance(i, int) or s + ahead < SEQS
        n, out = frame_base(s), []
        for slot, row in frame_slots.items():
            for kind, ahead, t in row:
                if live(ahead):
                    if slot == h:
                        out.append((kind, s + ahead, (j + ahead) % 2, t, n))
                    n = n + 1
        return out

    def item_number(i, j, kind, t):
        for h in range(HEADS):
            for k, _, _, tile, n in frame_items(i, h, j):
                if (k, tile) == (kind, t):
                    return n

    def values_up(i, j):
        if isinstance(i, int) and i == 0 and j == 0:
            return len(first_items) - 4
        return item_number(*((i, 0) if j else (i - 1, 1)), "v", 1) + 1

    late_items = [("turn_o", t) for t in range(PT)] + [("wo", 0), ("turn_x", 0), ("rows", 0), ("turn_z", 0)]
    late_items += [(kind, c) for kind in ("up_g", "up_a") for c in range(FC)] + [("out", 0)]
    LATE = len(late_items)
    late_index = {item: w for w, item in enumerate(late_items)}
    late_before = {0: ("turn_o", 0), 1: ("turn_o", 2), 2: ("wo", 0), 3: ("turn_x", 0), 4: ("rows", 0),
                   6: ("turn_z", 0), 7: ("up_g", 0), 8: ("up_g", 2), 9: ("up_a", 0),
                   10: ("up_a", 1), 11: ("up_a", 2), 12: ("out", 0)}
    late_after = {0: ("turn_o", 1), 1: ("turn_o", 3), 7: ("up_g", 1)}
    assert FC == 3

    with ExitStack() as ctx:
        sb = lambda n, shape, dtype=F32: core.sb(f"{name}_{n}", shape, dtype, ctx=ctx)
        sem = lambda n: core.sem(f"{name}_{n}")
        wqkv, wo = sb("wqkv", [P, 3 * INNER]), sb("wo", [P, CH, C])
        w1, w2 = sb("w1", [P, FC, 2, P]), sb("w2", [P, FC, C])
        cols, b2 = sb("cols", [P, 2 + 2 * FC]), sb("b2", [1, C])
        tables, scales = sb("tables", [P, 2, 2, 2, HD]), sb("scales", [P, 2, 2, HD])
        ident16, masks = sb("ident16", [P, P], BF16), sb("masks", [P, SPAN], BF16)
        shifted = sb("shifted", [P, 2, SEQ])
        late_shifted = sb("late_shifted", [P, 2, SEQ])
        raw = sb("raw", [P, PT, 2, INNER])
        squares, turned_part = sb("squares", [P, 2, INNER]), sb("turned_part", [P, 2, INNER])
        size, half_powers = sb("size", [P, 2, 2, 2, HEADS]), sb("half_powers", [P, 4 * HEADS])
        q_t, k_t = sb("q_t", [P, 2, CH, PN]), sb("k_t", [P, CH, PN])
        values = sb("values", [P, PT, INNER])
        peak, total = sb("peak", [P, 2, 2]), sb("total", [P, PT, HEADS])
        probs, probs_t = sb("probs", [P, 2, SPAN]), sb("probs_t", [P, 2, SPAN])
        mixed, mixed_t = sb("mixed", [P, PT, INNER]), sb("mixed_t", [P, PT, CH, P])
        z, z_t = sb("z", [P, PT, C]), sb("z_t", [P, PN])
        bent, hidden = sb("bent", [P, FC, PN]), sb("hidden", [P, FC, PN])
        norm = Norm(core, f"{name}_norm", PT, core.eps, core.norm_buffers(f"{name}_norm", PT, ctx))
        weights_in, tables_ready = sem("weights_in"), sem("tables_ready")
        a_up, a_down, c_up, c_down = sem("a_up"), sem("a_down"), sem("c_up"), sem("c_down")
        shifted_ready, squared, part_asked = sem("shifted_ready"), sem("squared"), sem("part_asked")
        sized, scaled, part_ready, rotated = sem("sized"), sem("scaled"), sem("part_ready"), sem("rotated")
        bent_ready = sem("bent_ready")
        scores_up, peaked, probs_done = sem("scores_up"), sem("peaked"), sem("probs_done")
        probs_turned, probs_t_done = sem("probs_turned"), sem("probs_t_done")
        o_up, mixed_ready = sem("o_up"), sem("mixed_ready")
        sbank, pbank, obank = core.bank[0:2], [core.bank[2], core.bank[5]], core.bank[3:5]
        abank, cbank = core.bank[6], tail.turn_bank
        widths = [min(P, HID - c * P) for c in range(FC)]
        x1 = core.branch
        loads = 10
        block = ctx.enter_context(nc.Block())

        def wait_from(eng, semaphore, count):
            if not (isinstance(count, int) and count < 1):
                eng.wait_ge(semaphore, count)

        def ahead(i, u):
            return (i, u) if u < UNITS else (i + 1, u - UNITS)

        def run(eng, slot):
            for u in range(UNITS):
                slot(0, u, False, True)
            with eng.Fori(1, PAIRS - 1) as i:
                for u in range(UNITS):
                    slot(i, u, True, True)
            for u in range(UNITS):
                slot(PAIRS - 1, u, True, False)

        @block.sync
        def _(sp):
            for to, what in ((wqkv, "wqkv"), (wo, "wo"), (w1, "w1"), (w2, "w2"), (cols, "cols"), (b2, "b2")):
                sp.dma_start(to[:], dram[f"{name}_{what}"]).then_inc(weights_in, 16)
            sp.dma_start(tables[:], dram["rotary"]).then_inc(weights_in, 16)
            sp.dma_start(scales[:].rearrange("p a b d -> p (a b d)"),
                         dram[f"{name}_scales"].partition_broadcast(P)).then_inc(weights_in, 16)
            sp.dma_start(ident16[:], dram["identity16"]).then_inc(weights_in, 16)
            sp.dma_start(masks[:], dram["window"]).then_inc(weights_in, 16)

        @block.tensor
        def _(pe):
            pe.wait_ge(weights_in, 16 * loads)

            def item(kind, s, j, t, n):
                wait_from(pe, a_down, n)
                if kind in ("q", "k", "v"):
                    part = "qkv".index(kind)
                    pe.wait_ge(shifted_ready, s + 1)
                    pe.matmul(abank[:], shifted[:, j, t * P:(t + 1) * P], wqkv[:, part * INNER:(part + 1) * INNER],
                              start=True, stop=True).then_inc(a_up, 1)
                else:
                    part = int(kind == "turn_k")
                    pe.wait_ge(rotated, s * 4 + 2 * t + part + 1)
                    for c in range(CH):
                        last = pe.transpose(abank[:, c * P:(c + 1) * P], raw[:, 2 * j + t, part, c * P:(c + 1) * P],
                                            core.ident[:])
                    last.then_inc(a_up, 1)

            def late_item(kind, c, i):
                w = late_index[kind, c]
                if w == 0:
                    wait_from(pe, tail.turned_stored, i)
                wait_from(pe, c_down, i * LATE + w)
                bank, tiles = cbank, [slice(t * P, (t + 1) * P) for t in range(PT)]
                if kind == "turn_o":
                    pe.wait_ge(mixed_ready, i * PT + c + 1)
                    for k in range(CH):
                        last = pe.transpose(bank[:, tiles[k]], mixed[:, c, k * P:(k + 1) * P], core.ident[:])
                elif kind == "wo":
                    for t in range(PT):
                        for k in range(CH):
                            last = pe.matmul(bank[:, tiles[t]], mixed_t[:, t, k, :], wo[:, k, :],
                                             start=(k == 0), stop=(k == CH - 1))
                elif kind in ("turn_x", "turn_z"):
                    source = x1 if kind == "turn_x" else z
                    for t in range(PT):
                        last = pe.transpose(bank[:, tiles[t]], source[:, t, :], core.ident[:])
                elif kind == "rows":
                    flat = late_shifted[:].rearrange("p j t -> p (j t)")
                    for t in range(PT):
                        last = pe.transpose(bank[:, tiles[t]], flat[:, tiles[t]], core.ident[:])
                elif kind in ("up_g", "up_a"):
                    last = pe.matmul(bank[0:widths[c], :], w1[:, c, int(kind == "up_g"), 0:widths[c]], z_t[:],
                                     start=True, stop=True)
                else:
                    for t in range(PT):
                        for k in range(FC):
                            pe.matmul(bank[:, tiles[t]], hidden[0:widths[k], k, tiles[t]], w2[0:widths[k], k, :],
                                      start=(k == 0), stop=False)
                        last = pe.matmul(bank[:, tiles[t]], core.ones_row[:], b2[:], start=False, stop=True)
                last.then_inc(c_up, 1)

            def late(u, table, i):
                if u in table:
                    late_item(*table[u], i)

            def scores(i, u):
                j, h = divmod(u, HEADS)
                n = i * UNITS + u
                q, k = (rows[:, h // 2, j * SEQ:(j + 1) * SEQ] for rows in (q_t[:, h % 2], k_t))
                bank = sbank[u % 2]
                wait_from(pe, probs_done, n - 1)
                if h == 0:
                    pe.wait_ge(a_down, frame_base(2 * i + j))
                pe.matmul(bank[:, 0:P], q[:, 0:P], k[:, 0:P], start=True, stop=False)
                pe.matmul(bank[:, 0:P], ident16[:], masks[:, 0:P], start=False, stop=True)
                pe.matmul(bank[:, P:SPAN], q[:, P:SEQ], k[:], start=True, stop=False)
                pe.matmul(bank[:, P:SPAN], ident16[:], masks[:, P:SPAN], start=False, stop=True).then_inc(
                    scores_up, 1)

            def turn(i, u):
                n = i * UNITS + u
                pe.wait_ge(probs_done, n + 1)
                wait_from(pe, probs_t_done, n - 1)
                for b in range(3):
                    last = pe.transpose(pbank[u % 2][:, b * P:(b + 1) * P], probs[:, u % 2, b * P:(b + 1) * P],
                                        core.ident[:])
                last.then_inc(probs_turned, 1)

            def mix(i, u):
                j, h = divmod(u, HEADS)
                pe.wait_ge(probs_t_done, i * UNITS + u + 1)
                if h == 0:
                    wait_from(pe, mixed_ready, i * PT + 2 * j)
                    pe.wait_ge(a_down, values_up(i, j))
                p = probs_t[:, u % 2, :]
                at = slice(h * HD, (h + 1) * HD)
                v = [values[:, 2 * j + t, at] for t in range(2)]
                pe.matmul(obank[0][:, at], p[:, 0:P], v[0], start=True, stop=True)
                pe.matmul(obank[1][:, at], p[:, P:2 * P], v[0], start=True, stop=False)
                pe.matmul(obank[1][:, at], p[:, 2 * P:SPAN], v[1], start=False, stop=True).then_inc(o_up, 1)

            def slot(i, u, has_late, has_next):
                j, h = divmod(u, HEADS)
                if has_next or u + 2 < UNITS:
                    scores(*ahead(i, u + 2))
                items = frame_items(i, h, j)
                for args in items[:1]:
                    item(*args)
                if has_late:
                    late(u, late_before, i - 1)
                if has_next or u + 1 < UNITS:
                    turn(*ahead(i, u + 1))
                for args in items[1:]:
                    item(*args)
                mix(i, u)
                if has_late:
                    late(u, late_after, i - 1)
                    if u == 15:
                        tail.pe(pe, i - 1)

            for n, (kind, s, t) in enumerate(first_items):
                item(kind, s, s % 2, t, n)
            scores(0, 0)
            scores(0, 1)
            turn(0, 0)
            run(pe, slot)
            for u in range(UNITS):
                late(u, late_before, PAIRS - 1)
                late(u, late_after, PAIRS - 1)
            tail.pe(pe, PAIRS - 1)

        @block.scalar
        def _(act):
            act.wait_ge(weights_in, 16 * loads)
            act.wait_ge(tables_ready, 1)

            def take(kind, s, j, t, n):
                if kind == "v" and t == 0:
                    wait_from(act, o_up, (s - 1) * HEADS)
                act.wait_ge(a_up, n + 1)
                if kind == "v":
                    to, rows = values[:, 2 * j + t, :], abank[:]
                elif kind in ("q", "k"):
                    to, rows = raw[:, 2 * j + t, int(kind == "k"), :], abank[:]
                else:
                    at = j * SEQ + t * P
                    to, rows = k_t[:, :, at:at + P], abank[:].rearrange("p (c k) -> p c k", c=CH)
                    if kind == "turn_q":
                        for half in range(2):
                            low = slice(half * HD, (half + 1) * HD)
                            act.activation(q_t[low, half, :, at:at + P], rows[low], ACT.Identity)
                        act.drain()
                        act.sem_inc(a_down, 1)
                        return
                act.activation(to, rows, ACT.Identity).then_inc(a_down, 1)

            def probabilities(i, u):
                n = i * UNITS + u
                j, h = divmod(u, HEADS)
                act.wait_ge(peaked, n + 1)
                wait_from(act, probs_turned, n - 1)
                for t, at in enumerate((slice(0, P), slice(P, SPAN))):
                    last = act.activation(probs[:, u % 2, at], sbank[u % 2][:, at], ACT.Exp,
                                          bias=peak[:, u % 2, t:t + 1], accum_out=total[:, 2 * j + t, h:h + 1])
                last.then_inc(probs_done, 1)

            def late_item(kind, c, i):
                if kind in ("wo", "rows", "up_a", "out"):
                    return
                act.wait_ge(c_up, i * LATE + late_index[kind, c] + 1)
                if kind == "turn_o":
                    last = act.activation(mixed_t[:, c].rearrange("p c k -> p (c k)"), cbank[:], ACT.Identity)
                elif kind == "turn_x":
                    by_seq = cbank[:].rearrange("p (j t) -> p j t", j=2)
                    act.activation(late_shifted[0:HALF], by_seq[0:HALF], ACT.Identity)
                    act.activation(late_shifted[HALF:C, :, 1:SEQ], by_seq[HALF:C, :, 0:SEQ - 1], ACT.Identity)
                    act.drain()
                    act.sem_inc(c_down, 1)
                    return
                elif kind == "turn_z":
                    last = act.activation(z_t[:], cbank[:], ACT.Identity, bias=cols[:, 1:2], scale=cols[:, 0:1])
                else:
                    k = widths[c]
                    last = act.activation(bent[0:k, c, :], cbank[0:k, :], ACT.Identity,
                                          bias=cols[0:k, 2 + FC + c:3 + FC + c])
                last.then_inc(c_down, 1)
                if (kind, c) == ("up_g", FC - 1):
                    act.drain()
                    act.activation(bent[:, 0:FC - 1], bent[:, 0:FC - 1], ACT.Gelu)
                    act.activation(bent[0:k, c], bent[0:k, c], ACT.Gelu)
                    act.drain()
                    act.sem_inc(bent_ready, 1)

            def late(u, table, i):
                if u in table:
                    late_item(*table[u], i)

            def slot(i, u, has_late, has_next):
                j, h = divmod(u, HEADS)
                if has_next or u + 1 < UNITS:
                    probabilities(*ahead(i, u + 1))
                items = frame_items(i, h, j)
                for args in items[:1]:
                    take(*args)
                if has_late:
                    late(u, late_before, i - 1)
                for args in items[1:]:
                    take(*args)
                if has_late:
                    late(u, late_after, i - 1)
                    if u == 15:
                        tail.act(act, i - 1)

            for n, (kind, s, t) in enumerate(first_items):
                take(kind, s, s % 2, t, n)
            probabilities(0, 0)
            run(act, slot)
            for u in range(UNITS):
                late(u, late_before, PAIRS - 1)
                late(u, late_after, PAIRS - 1)
            tail.act(act, PAIRS - 1)

        @block.gpsimd
        def _(pool):
            pool.wait_ge(tables_ready, 1)
            pool.memset(half_powers[:], -0.5)
            pool.drain()

            def square(s, j, m, n):
                pool.wait_ge(a_down, n + 1)
                wait_from(pool, part_asked, s * 4 + m - 1)
                rows = raw[:, 2 * j + m // 2, m % 2, :]
                pool.tensor_tensor(squares[:, m % 2, :], rows, rows, ALU.mult).then_inc(squared, 1)

            def other_half(s, j, m):
                t, part = divmod(m, 2)
                wait_from(pool, rotated, s * 4 + m - 1)
                rows = raw[:, 2 * j + t, part, :].rearrange("p (h s d) -> p h s d", s=2, d=HD // 2)[:, :, ::-1, :]
                sines = tables[:, part, t, 1, :].rearrange("p (s d) -> p s d", s=2).unsqueeze(1)
                pool.tensor_tensor(
                    turned_part[:, m % 2, :].rearrange("p (h s d) -> p h s d", s=2, d=HD // 2), rows,
                    sines.broadcast_to([P, HEADS, 2, HD // 2]), ALU.mult).then_inc(part_ready, 1)

            def scale(s, j):
                pool.wait_ge(sized, s + 1)
                flat = size[:, j].rearrange("p t a h -> p (t a h)")
                pool.tensor_tensor(flat, flat, half_powers[:], ALU.pow).then_inc(scaled, 1)

            def pair(i, has_late, has_next):
                for j in range(2):
                    s = 2 * i + j
                    for m in range(5):
                        if m < 4 and (has_next or j == 0):
                            other_half(s + 1, 1 - j, m)
                        if m > 0 and has_next:
                            square(s + 2, j, m - 1, item_number(i, j, "qk"[(m - 1) % 2], (m - 1) // 2))
                    if has_late:
                        if j == 0:
                            norm.power(pool, i - 1)
                        else:
                            tail.pool(pool, i - 1)
                    if has_next:
                        scale(s + 2, j)

            for s in range(2):
                for m in range(4):
                    square(s, s, m, 4 * s + m)
            for s in range(2):
                scale(s, s)
            for m in range(4):
                other_half(0, 0, m)
            pair(0, False, True)
            with pool.Fori(1, PAIRS - 1) as i:
                pair(i, True, True)
            pair(PAIRS - 1, True, False)
            norm.power(pool, PAIRS - 1)
            tail.pool(pool, PAIRS - 1)

        @block.vector
        def _(dve):
            dve.wait_ge(weights_in, 16 * loads)
            dve.memset(shifted[:], 0.0)
            dve.memset(late_shifted[:], 0.0)
            dve.memset(q_t[:], 0.0)
            for part in range(2):
                for t in range(2):
                    dve.tensor_tensor(tables[:, part, t], tables[:, part, t], scales[:, part], ALU.mult)
            dve.drain()
            dve.sem_inc(tables_ready, 1)

            def shift(s, j):
                source = core.normed_t[:, bass.ds(s * SEQ, SEQ)]
                dve.tensor_copy(shifted[0:HALF, j, :], source[0:HALF])
                dve.tensor_copy(shifted[HALF:C, j, 1:SEQ], source[HALF:C, 0:SEQ - 1])
                dve.drain()
                dve.sem_inc(shifted_ready, 1)

            def sum_squares(s, j, m):
                dve.wait_ge(squared, s * 4 + m + 1)
                dve.tensor_reduce(size[:, j, m // 2, m % 2, :], squares[:, m % 2, :].rearrange("p (h d) -> p h d", d=HD),
                                  AX.X, ALU.add).then_inc(part_asked, 1)

            def ask_root(j):
                dve.drain()
                dve.tensor_scalar(size[:, j], size[:, j], 1e-24, None, ALU.max)
                dve.drain()
                dve.sem_inc(sized, 1)

            def rotate(s, j, m):
                t, part = divmod(m, 2)
                rows = raw[:, 2 * j + t, part, :]
                by_head = rows.rearrange("p (h d) -> p h d", d=HD)
                dve.wait_ge(part_ready, s * 4 + m + 1)
                if m == 0:
                    dve.wait_ge(scaled, s + 1)
                dve.tensor_tensor(by_head, by_head, tables[:, part, t, 0, :].unsqueeze(1).broadcast_to(
                    [P, HEADS, HD]), ALU.mult)
                dve.drain()
                dve.tensor_tensor(rows, rows, turned_part[:, m % 2, :], ALU.add)
                dve.drain()
                dve.tensor_tensor(by_head, by_head, size[:, j, t, part, :].unsqueeze(2).broadcast_to(
                    [P, HEADS, HD]), ALU.mult).then_inc(rotated, 1)

            def peak_of(i, u):
                dve.wait_ge(scores_up, i * UNITS + u + 1)
                for t, at in enumerate((slice(0, P), slice(P, SPAN))):
                    dve.tensor_reduce(peak[:, u % 2, t:t + 1], sbank[u % 2][:, at], AX.X, ALU.max, negate=True)
                dve.drain()
                dve.sem_inc(peaked, 1)

            def take_mixed(i, j):
                dve.reciprocal(total[:, 2 * j:2 * j + 2, :], total[:, 2 * j:2 * j + 2, :])
                dve.drain()
                dve.wait_ge(o_up, i * UNITS + (j + 1) * HEADS)
                if j == 0 and not (isinstance(i, int) and i == 0):
                    dve.wait_ge(c_up, (i - 1) * LATE + PT)
                for t in range(2):
                    dve.tensor_tensor(mixed[:, 2 * j + t, :].rearrange("p (h d) -> p h d", d=HD),
                                      obank[t][:].rearrange("p (h d) -> p h d", d=HD),
                                      total[:, 2 * j + t, :].unsqueeze(2).broadcast_to([P, HEADS, HD]),
                                      ALU.mult).then_inc(mixed_ready, 1)

            def late(u, i):
                took = lambda kind, c=0: dve.wait_ge(c_up, i * LATE + late_index[kind, c] + 1)
                flat = core.branch[:].rearrange("p t c -> p (t c)")
                if u == 2:
                    took("wo")
                    dve.tensor_tensor(flat, cbank[:], core.normed[:, bass.ds(i * PT, PT), :].rearrange(
                        "p t c -> p (t c)"), ALU.add)
                    dve.drain()
                    dve.sem_inc(c_down, 1)
                elif u == 4:
                    took("rows")
                    norm.find_moments(dve, lambda r: cbank[:, r * P:(r + 1) * P])
                elif u == 5:
                    norm.apply(dve, i, lambda r: z[:, r, :], lambda r: cbank[:, r * P:(r + 1) * P])
                    dve.drain()
                    dve.sem_inc(c_down, 1)
                elif u in (9, 10, 11):
                    dve.wait_ge(bent_ready, i + 1)
                    c = u - 9
                    k = widths[c]
                    took("up_a", c)
                    dve.scalar_tensor_tensor(hidden[0:k, c, :], cbank[0:k, :], cols[0:k, 2 + c:3 + c],
                                             bent[0:k, c, :], ALU.add, ALU.mult)
                    dve.drain()
                    dve.sem_inc(c_down, 1)
                elif u == 12:
                    took("out")
                    dve.tensor_tensor(flat, cbank[:], flat, ALU.add)
                    dve.drain()
                    dve.sem_inc(c_down, 1)
                    tail.dve_branch(dve, i)
                elif u == 13:
                    tail.dve_stream(dve, i)
                elif u == 14:
                    tail.dve_fresh(dve, i)

            def slot(i, u, has_late, has_next):
                j, h = divmod(u, HEADS)
                n = i * UNITS + u
                s = 2 * i + j
                if has_next or u + 1 < UNITS:
                    peak_of(*ahead(i, u + 1))
                if has_next and h == 0:
                    dve.wait_ge(a_up, values_up(i, j))
                    shift(s + 2, j)
                if u == HEADS:
                    take_mixed(i, 0)
                elif u == 0 and has_late:
                    take_mixed(i - 1, 1)
                dve.wait_ge(probs_turned, n + 1)
                wait_from(dve, o_up, n - 1)
                dve.tensor_copy(probs_t[:, u % 2, :], pbank[u % 2][:, 0:SPAN]).then_inc(probs_t_done, 1)
                if has_next or j == 0:
                    if h < 4:
                        rotate(s + 1, 1 - j, h)
                if has_next:
                    if 2 <= h < 6:
                        sum_squares(s + 2, j, h - 2)
                    if h == 5:
                        ask_root(j)
                if has_late:
                    late(u, i - 1)

            shift(0, 0)
            shift(1, 1)
            for s in range(2):
                for m in range(4):
                    sum_squares(s, s, m)
                ask_root(s)
            for m in range(4):
                rotate(0, 0, m)
            peak_of(0, 0)
            run(dve, slot)
            take_mixed(PAIRS - 1, 1)
            for u in range(UNITS):
                late(u, PAIRS - 1)

def wave_block(core, tail):
    nc, dram = core.nc, core.dram
    name = "wave"
    HEADS = 16
    HD = C // HEADS
    TWO_PI = 2.0 * np.pi
    PI1 = 6.28125
    PI2 = float(np.float32(np.round((TWO_PI - PI1) * 2 ** 22) / 2 ** 22))
    PI3 = float(TWO_PI - PI1 - PI2)
    ROUNDER = 1.5 * 2.0 ** 23
    kernel_rows = nc.dram_tensor("wave_kernel_rows", (HEADS, P + SEQ), F32, kind="Internal").ap()
    with ExitStack() as ctx:
        sb = lambda n, shape, dtype=F32: core.sb(f"{name}_{n}", shape, dtype, ctx=ctx)
        sem = lambda n: core.sem(f"{name}_{n}")
        w, wout, bout = sb("w", [P, 4, C]), sb("wout", [P, C]), sb("bout", [1, C])
        cols, params, time = sb("cols", [P, 4]), sb("params", [HEADS, 4]), sb("time", [HEADS, SEQ])
        coupling, coupling_wide = sb("coupling", [HEADS, HEADS]), sb("coupling_wide", [HEADS, HEADS, HD])
        spread, same = sb("spread", [HEADS, P]), sb("same", [P, P])
        coupler = sb("coupler", [P, P])
        stat = sb("stat", [HEADS, 4])
        phase, turns = sb("phase", [HEADS, SEQ]), sb("turns", [HEADS, SEQ])
        fade, padded = sb("fade", [HEADS, SEQ]), sb("padded", [HEADS, P + SEQ])
        toeplitz = sb("toeplitz", [P, HEADS, SEQ])
        field, waves = sb("field", [P, TILES, C]), sb("waves", [P, TILES, C])
        query = sb("query", [P, SEQS, SEQ])
        ex, pos = sb("ex", [P, 2, PN]), sb("pos", [P, 2, PN])
        gate, deposit = sb("gate", [P, PN]), sb("deposit", [P, PT, P])
        staged, wave_t, mixed = sb("staged", [P, PT, C]), sb("wave_t", [P, PN]), sb("mixed", [P, 2, SEQ])
        weights_in, params_in = sem("weights_in"), sem("params_in")
        exp_asked, exp_done = sem("exp_asked"), sem("exp_done")
        kernel_ready, kernel_out, toeplitz_in = sem("kernel_ready"), sem("kernel_out"), sem("toeplitz_in")
        wide_ready, coupler_up, coupler_ready = sem("wide_ready"), sem("coupler_up"), sem("coupler_ready")
        up, bent, taken = sem("up"), sem("bent"), sem("taken")
        deposit_ready, field_up, field_down = sem("deposit_ready"), sem("field_up"), sem("field_down")
        wave_up, wave_down = sem("wave_up"), [sem("wave_down_even"), sem("wave_down_odd")]
        staged_ready, turned, wave_t_ready = sem("staged_ready"), sem("turned"), sem("wave_t_ready")
        coupled, mixed_ready, out_up, out_taken = sem("coupled"), sem("mixed_ready"), sem("out_up"), sem("out_taken")
        loads = 6
        block = ctx.enter_context(nc.Block())

        by_seq = waves[:].rearrange("p (b h) c -> p h b c", h=2)

        def take_waves(eng, odd):
            for h in range(odd, HEADS, 2):
                eng.wait_ge(wave_up, h + 1)
                bank = core.bank[5 + h % 2][:, 0:2 * P].rearrange("p (t b d) -> p t b d", t=2, d=HD)
                out = by_seq[:, :, :, h * HD:(h + 1) * HD]
                (eng.activation(out, bank, ACT.Identity) if odd else eng.tensor_copy(out, bank)).then_inc(
                    wave_down[h % 2], 1)

        @block.sync
        def _(sp):
            sp.dma_start(params[:], dram["wave_params"]).then_inc(params_in, 16)
            sp.dma_start(time[:], dram["wave_time"]).then_inc(params_in, 16)
            sp.dma_start(coupling[:], dram["wave_coupling"]).then_inc(params_in, 16)
            for to, what in ((w, "w"), (cols, "cols"), (spread, "spread"), (same, "same"), (wout, "wout"),
                             (bout, "bout")):
                sp.dma_start(to[:], dram[f"wave_{what}"]).then_inc(weights_in, 16)
            sp.wait_ge(kernel_ready, 1)
            sp.dma_start(kernel_rows, padded[:]).then_inc(kernel_out, 16)
            sp.wait_ge(kernel_out, 16)
            shifted = bass.AP(tensor=kernel_rows.tensor, offset=1, ap=[[1, P], [P + SEQ, HEADS], [1, SEQ]])
            sp.dma_start(toeplitz[:], shifted).then_inc(toeplitz_in, 16)

        @block.scalar
        def _(act):
            act.wait_ge(params_in, 48)
            act.activation(stat[:, 0:1], params[:, 1:2], ACT.Abs)
            act.drain()
            act.activation(stat[:, 0:1], stat[:, 0:1], ACT.Exp, scale=-1.0)
            act.drain()
            act.activation(stat[:, 0:1], stat[:, 0:1], ACT.Ln, bias=1.0).then_inc(exp_done, 1)
            act.wait_ge(exp_asked, 1)
            act.activation(fade[:], time[:], ACT.Exp, scale=stat[:, 1:2])
            act.activation(coupling[:], coupling[:], ACT.Exp)
            act.activation(turns[:], phase[:], ACT.Sin, scale=0.5)
            act.drain()
            act.sem_inc(exp_done, 1)
            act.wait_ge(weights_in, 16 * loads)
            with act.Fori(0, PAIRS) as i:
                for part in range(2):
                    act.wait_ge(up, i * 4 + part + 1)
                    act.wait_ge(taken, i * 4)
                    act.activation(ex[:, part, :], core.bank[part][:], ACT.Exp, bias=cols[:, part:part + 1])
                act.drain()
                act.sem_inc(bent, 1)
                act.wait_ge(up, i * 4 + 4)
                act.activation(gate[:], core.bank[3][:], ACT.Sigmoid, bias=cols[:, 3:4])
                act.drain()
                act.sem_inc(bent, 1)
                act.wait_ge(field_up, i + 1)
                act.activation(field[:, bass.ds(i * PT, PT), :].rearrange("p t c -> p (t c)"), core.bank[4][:],
                               ACT.Identity).then_inc(field_down, 1)
            take_waves(act, 1)

            act.wait_ge(wave_down[0], HEADS // 2)
            act.drain()

            def stage(i):
                act.activation(staged[:], waves[:, bass.ds(i * PT, PT), :], ACT.Identity).then_inc(staged_ready, 1)

            def pair(i, has_tail, has_next):
                act.wait_ge(turned, i + 1)
                act.activation(wave_t[:], core.bank[0][:], ACT.Identity).then_inc(wave_t_ready, 1)
                if has_next:
                    stage(i + 1)
                if has_tail:
                    tail.act(act, i - 1)

            stage(0)
            pair(0, False, True)
            with act.Fori(1, PAIRS - 1) as i:
                pair(i, True, True)
            pair(PAIRS - 1, True, False)
            tail.act(act, PAIRS - 1)

        @block.tensor
        def _(pe):
            pe.wait_ge(weights_in, 16 * loads)
            pe.wait_ge(wide_ready, 1)
            pe.matmul(core.bank[6][:, 0:P], coupling_wide[:].rearrange("i j d -> i (j d)"), spread[:],
                      start=True, stop=True).then_inc(coupler_up, 1)
            with pe.Fori(0, PAIRS) as i:
                pe.wait_ge(taken, i * 4)
                pe.wait_ge(bent, i * 2)
                for part in range(4):
                    pe.matmul(core.bank[part][:], w[:, part, :], core.normed_t[:, bass.ds(i * PN, PN)],
                              start=True, stop=True).then_inc(up, 1)
                pe.wait_ge(deposit_ready, i + 1)
                pe.wait_ge(field_down, i)
                for t in range(PT):
                    last = pe.transpose(core.bank[4][:, t * P:(t + 1) * P], deposit[:, t, :], core.ident[:])
                last.then_inc(field_up, 1)
            pe.wait_ge(toeplitz_in, 16)
            pe.wait_ge(field_down, PAIRS)
            pe.wait_ge(coupler_ready, 1)
            halves = field[:].rearrange("p (b h) c -> p h b c", h=2)
            for h in range(HEADS):
                bank = core.bank[5 + h % 2]
                if h >= 2:
                    pe.wait_ge(wave_down[h % 2], h // 2)
                cells = [halves[:, s, :, h * HD:(h + 1) * HD] for s in range(2)]
                near, far = toeplitz[:, h, 0:P], toeplitz[:, h, P:SEQ]
                pe.matmul(bank[:, 0:P], near, cells[0], start=True, stop=True)
                pe.matmul(bank[:, P:2 * P], far, cells[0], start=True, stop=False)
                pe.matmul(bank[:, P:2 * P], near, cells[1], start=False, stop=True).then_inc(wave_up, 1)

            def pair(i, has_tail):
                pe.wait_ge(staged_ready, i + 1)
                pe.wait_ge(wave_t_ready, i)
                for t in range(PT):
                    last = pe.transpose(core.bank[0][:, t * P:(t + 1) * P], staged[:, t, :], core.ident[:])
                last.then_inc(turned, 1)
                pe.wait_ge(wave_t_ready, i + 1)
                pe.wait_ge(mixed_ready, i)
                pe.matmul(core.bank[1][:], coupler[:], wave_t[:], start=True, stop=True).then_inc(coupled, 1)
                pe.wait_ge(mixed_ready, i + 1)
                pe.wait_ge(out_taken, i)
                flat = mixed[:].rearrange("p j t -> p (j t)")
                for t in range(PT):
                    pe.matmul(core.bank[2][:, t * P:(t + 1) * P], flat[:, t * P:(t + 1) * P], wout[:],
                              start=True, stop=False)
                    last = pe.matmul(core.bank[2][:, t * P:(t + 1) * P], core.ones_row[:], bout[:],
                                     start=False, stop=True)
                last.then_inc(out_up, 1)
                if has_tail:
                    tail.pe(pe, i - 1)

            pair(0, False)
            with pe.Fori(1, PAIRS) as i:
                pair(i, True)
            tail.pe(pe, PAIRS - 1)

        @block.gpsimd
        def _(pool):
            with pool.Fori(0, PAIRS) as i:
                tail.pool(pool, i)

        @block.vector
        def _(dve):
            dve.wait_ge(params_in, 48)
            dve.wait_ge(exp_done, 1)
            dve.tensor_scalar(stat[:, 1:2], params[:, 1:2], 0.0, None, ALU.max)
            dve.drain()
            dve.tensor_tensor(stat[:, 1:2], stat[:, 1:2], stat[:, 0:1], ALU.add)
            dve.tensor_scalar(phase[:], time[:], params[:, 0:1], params[:, 2:3], ALU.mult, ALU.add)
            dve.drain()
            dve.tensor_scalar(stat[:, 1:2], stat[:, 1:2], -1.0, None, ALU.mult)
            dve.tensor_scalar(turns[:], phase[:], float(1.0 / TWO_PI), ROUNDER, ALU.mult, ALU.add)
            dve.drain()
            dve.tensor_scalar(turns[:], turns[:], ROUNDER, None, ALU.subtract)
            dve.drain()
            for part in (PI1, PI2, PI3):
                dve.scalar_tensor_tensor(phase[:], turns[:], -part, phase[:], ALU.mult, ALU.add)
                dve.drain()
            dve.tensor_reduce(stat[:, 2:3], coupling[:], AX.X, ALU.max)
            dve.drain()
            dve.tensor_scalar(coupling[:], coupling[:], stat[:, 2:3], None, ALU.subtract)
            dve.drain()
            dve.sem_inc(exp_asked, 1)
            dve.wait_ge(exp_done, 2)
            dve.tensor_tensor(turns[:], turns[:], turns[:], ALU.mult)
            dve.memset(padded[:], 0.0)
            dve.tensor_reduce(stat[:, 2:3], coupling[:], AX.X, ALU.add)
            dve.drain()
            dve.tensor_scalar(turns[:], turns[:], -2.0, 1.0, ALU.mult, ALU.add)
            dve.reciprocal(stat[:, 3:4], stat[:, 2:3])
            dve.drain()
            dve.tensor_tensor(fade[:], fade[:], turns[:], ALU.mult)
            dve.tensor_scalar(coupling[:], coupling[:], stat[:, 3:4], None, ALU.mult)
            dve.drain()
            dve.tensor_reduce(stat[:, 2:3], fade[:], AX.X, ALU.add, apply_absolute_value=True)
            dve.tensor_copy(coupling_wide[:], coupling[:].unsqueeze(2).broadcast_to([HEADS, HEADS, HD])).then_inc(
                wide_ready, 1)
            dve.drain()
            dve.tensor_scalar(stat[:, 2:3], stat[:, 2:3], 1e-8, None, ALU.max)
            dve.drain()
            dve.reciprocal(stat[:, 3:4], stat[:, 2:3])
            dve.drain()
            dve.tensor_scalar(padded[:, P:], fade[:], stat[:, 3:4], None, ALU.mult).then_inc(kernel_ready, 1)
            dve.wait_ge(weights_in, 16 * loads)
            dve.wait_ge(coupler_up, 1)
            dve.tensor_tensor(coupler[:], core.bank[6][:, 0:P], same[:], ALU.mult).then_inc(coupler_ready, 1)
            with dve.Fori(0, PAIRS) as i:
                dve.wait_ge(bent, i * 2 + 1)
                for part in range(2):
                    dve.tensor_scalar(pos[:, part, :], core.bank[part][:], cols[:, part:part + 1], 0.0,
                                      ALU.add, ALU.max)
                dve.drain()
                for part in range(2):
                    dve.scalar_tensor_tensor(pos[:, part, :], ex[:, part, :], 1.0, pos[:, part, :], ALU.min, ALU.add)
                dve.drain()
                dve.wait_ge(up, i * 4 + 3)
                dve.wait_ge(field_up, i)
                latest_first = lambda ap: ap.rearrange("p (t k) -> p t k", k=P)[:, :, ::-1]
                dve.scalar_tensor_tensor(deposit[:], latest_first(core.bank[2][:]), cols[:, 2:3],
                                         latest_first(pos[:, 1, :]), ALU.add, ALU.mult)
                dve.drain()
                ends = deposit[:].rearrange("p (j h) k -> p j h k", h=2)[:, :, 1, 0:2]
                dve.tensor_tensor(ends[:, :, 1], ends[:, :, 1], ends[:, :, 0], ALU.add)
                dve.drain()
                dve.memset(ends[:, :, 0:1], 0.0)
                dve.drain()
                dve.sem_inc(deposit_ready, 1)
                dve.wait_ge(bent, i * 2 + 2)
                dve.tensor_tensor(query[:, bass.ds(i * 2, 2), :], pos[:, 0, :].rearrange("p (j t) -> p j t", j=2),
                                  gate[:].rearrange("p (j t) -> p j t", j=2), ALU.mult)
                dve.drain()
                dve.sem_inc(taken, 4)
            take_waves(dve, 0)

            def pair(i, has_tail):
                dve.wait_ge(coupled, i + 1)
                dve.wait_ge(out_up, i)
                coupled_rows = core.bank[1][:].rearrange("p (j t) -> p j t", j=2)
                dve.tensor_tensor(mixed[:, :, 0:SEQ - 1], coupled_rows[:, :, 0:SEQ - 1],
                                  query[:, bass.ds(i * 2, 2), 0:SEQ - 1], ALU.mult)
                dve.tensor_tensor(mixed[:, :, SEQ - 1], coupled_rows[:, :, SEQ - 2],
                                  query[:, bass.ds(i * 2, 2), SEQ - 1], ALU.mult)
                dve.drain()
                dve.sem_inc(mixed_ready, 1)
                if has_tail:
                    tail.dve_stream(dve, i - 1)
                dve.wait_ge(out_up, i + 1)
                dve.tensor_copy(core.branch[:].rearrange("p t c -> p (t c)"), core.bank[2][:])
                dve.drain()
                dve.sem_inc(out_taken, 1)
                if has_tail:
                    tail.dve_fresh(dve, i - 1)
                tail.dve_branch(dve, i)

            pair(0, False)
            with dve.Fori(1, PAIRS) as i:
                pair(i, True)
            tail.dve_stream(dve, PAIRS - 1)
            tail.dve_fresh(dve, PAIRS - 1)


def rwkv_block(core, tail, x_dram):
    nc, dram = core.nc, core.dram
    name = "rwkv"
    HD = 8
    PH = 2
    PC = PH * HD
    GROUPS = C // PC
    ST = PH * HD * HD
    DECAY = float(np.exp(-0.5))
    g_rows = nc.dram_tensor("rwkv_g_rows", (PAIRS, P, PN), F32, kind="Internal").ap()
    decays = core.x[:].rearrange("p t c -> p (t c)").rearrange("p (c t) -> p c t", c=PC)
    rates = core.normed_t[:].rearrange("p (c t) -> p c t", c=PC)
    with ExitStack() as ctx:
        sb = lambda n, shape, dtype=F32, c=ctx: core.sb(f"{name}_{n}", shape, dtype, ctx=c)
        sem = lambda n: core.sem(f"{name}_{n}")
        recv, keys, values, removal = (sb(n, [P, PC, SEQ]) for n in ("recv", "keys", "values", "removal"))
        arrays_in = sem("arrays_in")
        arrays = (recv, decays, keys, values, removal, rates)

        with ExitStack() as inner:
            isb = lambda n, shape, dtype=F32: core.sb(f"{name}_{n}", shape, dtype, ctx=inner)
            pre = Norm(core, "rwkv_pre", PT, core.eps, core.norm_buffers("rwkv_pre", PT, inner))
            attn = TurnedNorm(core, "rwkv_attn", inner, core.bank[3])
            rows, pre_rows = isb("rows", [P, PT, C]), isb("pre_rows", [P, 2, C])
            cols = isb("cols", [P, 12])
            wide = isb("wide", [P, 5, C])
            low = isb("low", [P, 2, C // 2])
            high = isb("high", [C // 2, 2, C])
            padded = isb("padded", [P, 2, SEQ + 1])
            delta, mix = isb("delta", [P, 2, SEQ]), isb("mix", [P, 6, 2, SEQ])
            bent_low, bent_g = isb("bent_low", [C // 2, 2, PN]), isb("bent_g", [P, PN])
            k_raw, g_out, lift = isb("k_raw", [P, PN]), isb("g_out", [P, PN]), isb("lift", [P, PN])
            sent = [isb(f"sent_{n}", [P, 2, SEQ]) for n in ("r", "d", "k", "v", "kk", "a")]
            r_t, d_t, k_t, v_t, kk_t, a_t = (s[:].rearrange("p j t -> p (j t)") for s in sent)
            weights_in = sem("weights_in")
            padded_ready, mix_ready, up = sem("padded_ready"), sem("mix_ready"), sem("up")
            down = [sem(f"down_{b}") for b in range(3)]
            low_ready = [sem("low_w_ready"), sem("low_a_ready"), sem("low_g_ready")]
            a_ready, act_ready, dve_ready, g_ready = sem("a_ready"), sem("act_ready"), sem("dve_ready"), sem("g_ready")
            g_stored = sem("g_stored")
            items = ["w1", "a1", "g1", "k", "a2", "w2", "r", "v", "g2"]
            NB = 3
            W = len(items)
            index = {kind: w for w, kind in enumerate(items)}
            block = inner.enter_context(nc.Block())

            @block.sync
            def _(sp):
                for to, what in ((cols, "cols"), (wide, "wide"), (low, "low"), (high, "high")):
                    sp.dma_start(to[:], dram[f"rwkv_{what}"]).then_inc(weights_in, 16)
                sp.dma_start(pre_rows[:].rearrange("p a c -> p (a c)"),
                             dram["rwkv_pre_rows"].partition_broadcast(P)).then_inc(weights_in, 16)
                for i in range(PAIRS):
                    sp.wait_ge(act_ready, i + 1)
                    sp.wait_ge(dve_ready, i + 1)
                    for array, buffer in zip(arrays, sent):
                        for j in range(2):
                            b = 2 * i + j
                            sp.dma_start(array[b * GROUPS:(b + 1) * GROUPS, :, :],
                                         buffer[:, j, :]).then_inc(arrays_in, 16)
                    sp.wait_ge(g_ready, i + 1)
                    sp.dma_start(g_rows[i], g_out[:]).then_inc(g_stored, 16)
                sp.wait_ge(g_stored, 16 * PAIRS)
                sp.wait_ge(arrays_in, 16 * 12 * PAIRS)

            @block.tensor
            def _(pe):
                pe.wait_ge(weights_in, 16 * 5)

                def pair(i, has_next):
                    pe.wait_ge(mix_ready, i + 1)
                    for w, kind in enumerate(items):
                        bank = core.bank[w % NB]
                        if not (isinstance(i, int) and w < NB):
                            pe.wait_ge(down[w % NB], i * (W // NB) + w // NB)
                        mixed = lambda n: mix[:, n].rearrange("p j t -> p (j t)")
                        if kind in ("w1", "a1"):
                            n = int(kind == "a1")
                            last = pe.matmul(bank[0:C // 2, :], low[:, n, :], mixed(4 if n else 1), start=True, stop=True)
                        elif kind in ("w2", "a2"):
                            n = int(kind == "a2")
                            pe.wait_ge(low_ready[n], i + 1)
                            last = pe.matmul(bank[:], high[:, n, :], bent_low[:, n, :], start=True, stop=True)
                        elif kind == "g2":
                            pe.wait_ge(low_ready[2], i + 1)
                            last = pe.matmul(bank[:], wide[:, 4, :], bent_g[:], start=True, stop=True)
                        else:
                            part = ("r", "k", "v", "g1").index(kind)
                            last = pe.matmul(bank[:], wide[:, part, :], mixed((0, 2, 3, 5)[part]), start=True, stop=True)
                        last.then_inc(up, 1)
                    if has_next:
                        attn.pe(pe, i + 1)

                attn.pe(pe, 0)
                pair(0, True)
                with pe.Fori(1, PAIRS - 1) as i:
                    pair(i, True)
                pair(PAIRS - 1, False)

            @block.scalar
            def _(act):
                act.wait_ge(weights_in, 16 * 5)
                def pad(i):
                    act.wait_ge(mix_ready, i)
                    attn.act(act, i, padded[:, :, 1:], cols[:, 0:1], cols[:, 1:2])
                    act.drain()
                    act.sem_inc(padded_ready, 1)

                def pair(i, has_next):
                    def take(kind, out, func, signal=None, rows=P, **more):
                        w = index[kind]
                        act.wait_ge(up, i * W + w + 1)
                        act.activation(out, core.bank[w % NB][0:rows, :], func, **more).then_inc(down[w % NB], 1)
                        if signal is not None:
                            act.drain()
                            act.sem_inc(signal, 1)

                    take("w1", bent_low[:, 0, :], ACT.Tanh, low_ready[0], rows=C // 2)
                    take("a1", bent_low[:, 1, :], ACT.Identity, low_ready[1], rows=C // 2)
                    take("g1", bent_g[:], ACT.Sigmoid, low_ready[2])
                    act.wait_ge(dve_ready, i)
                    take("k", k_raw[:], ACT.Identity)
                    act.wait_ge(arrays_in, i * 16 * 12)
                    take("a2", a_t, ACT.Sigmoid, a_ready, bias=cols[:, 9:10])
                    take("w2", d_t, ACT.Sigmoid, bias=cols[:, 8:9])
                    take("r", r_t, ACT.Identity)
                    take("v", v_t, ACT.Identity)
                    act.drain()
                    act.activation(d_t, d_t, ACT.Exp, scale=-DECAY)
                    act.drain()
                    act.sem_inc(act_ready, 1)
                    act.wait_ge(g_stored, i * 16)
                    take("g2", g_out[:], ACT.Identity, g_ready)
                    if has_next:
                        pad(i + 1)

                pad(0)
                with act.Fori(0, PAIRS - 1) as i:
                    pair(i, True)
                pair(PAIRS - 1, False)

            @block.gpsimd
            def _(pool):
                with pool.Fori(0, PAIRS) as i:
                    pre.power(pool, i)
                    attn.pool(pool, i)

            @block.vector
            def _(dve):
                dve.wait_ge(weights_in, 16 * 5)
                dve.memset(padded[:], 0.0)
                dve.drain()
                def normalise(i):
                    x1 = core.normed[:, bass.ds(i * PT, PT), :]
                    pre.find_moments(dve, lambda r: core.normed[:, i * PT + r, :])
                    pre.apply(dve, i, lambda r: rows[:, r, :], lambda r: core.normed[:, i * PT + r, :])
                    dve.drain()
                    dve.tensor_tensor(rows[:], rows[:], pre_rows[:, 0, :].unsqueeze(1).broadcast_to([P, PT, C]),
                                      ALU.mult)
                    dve.drain()
                    dve.tensor_tensor(x1, rows[:], pre_rows[:, 1, :].unsqueeze(1).broadcast_to([P, PT, C]), ALU.add)
                    dve.drain()
                    attn.norm.find_moments(dve, lambda r: core.normed[:, i * PT + r, :])

                def turn_rows(i):
                    attn.dve_rows(dve, i, lambda r: core.normed[:, i * PT + r, :])

                def pair(i, has_next):
                    dve.wait_ge(padded_ready, i + 1)
                    dve.wait_ge(up, i * W)
                    dve.tensor_tensor(delta[:], padded[:, :, 0:SEQ], padded[:, :, 1:], ALU.subtract)
                    dve.drain()
                    for n in range(6):
                        dve.scalar_tensor_tensor(mix[:, n], delta[:], cols[:, 2 + n:3 + n], padded[:, :, 1:],
                                                 ALU.mult, ALU.add)
                    dve.drain()
                    dve.sem_inc(mix_ready, 1)
                    if has_next:
                        normalise(i + 1)
                    wk = index["k"]
                    dve.wait_ge(down[wk % NB], i * (W // NB) + wk // NB + 1)
                    dve.wait_ge(arrays_in, i * 16 * 12)
                    dve.tensor_scalar(kk_t, k_raw[:], cols[:, 10:11], None, ALU.mult)
                    dve.wait_ge(a_ready, i + 1)
                    dve.tensor_scalar(lift[:], a_t, 1.0, cols[:, 11:12], ALU.subtract, ALU.mult)
                    dve.drain()
                    dve.scalar_tensor_tensor(k_t, lift[:], 1.0, k_raw[:], ALU.add, ALU.mult)
                    dve.drain()
                    dve.sem_inc(dve_ready, 1)
                    if has_next:
                        turn_rows(i + 1)

                normalise(0)
                turn_rows(0)
                with dve.Fori(0, PAIRS - 1) as i:
                    pair(i, True)
                pair(PAIRS - 1, False)

        with ExitStack() as inner:
            isb = lambda n, shape, dtype=F32: core.sb(f"{name}_{n}", shape, dtype, ctx=inner)
            CK = 16
            CHUNKS = SEQ // CK
            outer = isb("outer", [P, 2, CK, ST])
            states = isb("states", [P, 2, CK, ST])
            recalled = isb("recalled", [P, CK, ST])
            removed, decayed, added = (isb(n, [P, ST]) for n in ("removed", "decayed", "added"))
            sa, outputs = isb("sa", [P, PC]), isb("outputs", [P, CK, PC])
            stat, mean = isb("stat", [P, PH, SEQ]), isb("mean", [P, PH, SEQ])
            part_cols = isb("part_cols", [P, 3, PC])
            cols_in = sem("cols_in")
            squared, root_asked, rooted = sem("squared"), sem("root_asked"), sem("rooted")
            outer_ready, states_ready = sem("outer_ready"), sem("states_ready")
            recalled_ready, recalled_used = sem("recalled_ready"), sem("recalled_used")
            scan_done, bonus_ready, out_ready, x_back, out_sent = (sem(n) for n in (
                "scan_done", "bonus_ready", "out_ready", "x_back", "out_sent"))
            bonus_asked, centred = sem("bonus_asked"), sem("centred")
            square = states[:].rearrange("p a k s -> p (a k s)")
            block = inner.enter_context(nc.Block())

            def by_token(array, h):
                return array[:, h * HD:(h + 1) * HD, :].rearrange("p c t -> p t c")

            def rows_of(chunk, buffer, h):
                return buffer[:, :, h * HD * HD:(h + 1) * HD * HD].rearrange("p k (i j) -> p k i j", j=HD)

            full = [P, CK, HD, HD]

            @block.gpsimd
            def _(pool):
                flat = removal[:].rearrange("p c t -> p (c t)")
                pool.tensor_tensor(square, flat, flat, ALU.mult).then_inc(squared, 1)

                def outer_of(chunk, slot):
                    at = bass.ds(chunk * CK, CK)
                    for h in range(PH):
                        v = values[:, h * HD:(h + 1) * HD, at].rearrange("p c t -> p t c").unsqueeze(3)
                        k = keys[:, h * HD:(h + 1) * HD, at].rearrange("p c t -> p t c").unsqueeze(2)
                        last = pool.tensor_tensor(rows_of(chunk, outer[:, slot], h), v.broadcast_to(full),
                                                  k.broadcast_to(full), ALU.mult)
                    last.then_inc(outer_ready, 1)

                def recall(chunk, slot):
                    at = bass.ds(chunk * CK, CK)
                    pool.wait_ge(states_ready, chunk + 1)
                    pool.wait_ge(recalled_used, chunk)
                    for h in range(PH):
                        r = recv[:, h * HD:(h + 1) * HD, at].rearrange("p c t -> p t c").unsqueeze(2)
                        last = pool.tensor_tensor(rows_of(chunk, recalled, h), rows_of(chunk, states[:, slot], h),
                                                  r.broadcast_to(full), ALU.mult)
                    last.then_inc(recalled_ready, 1)

                outer_of(0, 0)
                outer_of(1, 1)
                with pool.Fori(0, CHUNKS // 2 - 1) as m:
                    for slot in range(2):
                        recall(m * 2 + slot, slot)
                        outer_of(m * 2 + slot + 2, slot)
                for slot in range(2):
                    recall(CHUNKS - 2 + slot, slot)
                pool.wait_ge(scan_done, 1)
                pool.wait_ge(cols_in, 16)
                pool.tensor_tensor(recv[:], recv[:], keys[:], ALU.mult)
                pool.drain()
                pool.tensor_tensor(recv[:], recv[:], part_cols[:, 0, :].unsqueeze(2).broadcast_to([P, PC, SEQ]),
                                   ALU.mult).then_inc(bonus_asked, 1)

            @block.scalar
            def _(act):
                act.wait_ge(root_asked, 1)
                act.activation(stat[:], stat[:], ACT.Sqrt).then_inc(rooted, 1)
                act.wait_ge(centred, 1)
                act.activation(square, removal[:].rearrange("p c t -> p (c t)"), ACT.Square).then_inc(squared, 1)
                act.wait_ge(root_asked, 2)
                act.activation(stat[:], stat[:], ACT.Sqrt).then_inc(rooted, 1)

            def by_head(array):
                return array.rearrange("p (h c) t -> p h c t", h=PH)

            def over_tokens(small):
                return small[:].unsqueeze(2).broadcast_to([P, PH, HD, SEQ])

            @block.vector
            def _(dve):
                def sum_channels(out, array):
                    dve.tensor_reduce(out[:], by_head(array).rearrange("p h c t -> p h t c"), AX.X, ALU.add)

                squares = square.rearrange("p (c t) -> p c t", c=PC)
                dve.wait_ge(squared, 1)
                sum_channels(stat, squares)
                dve.drain()
                dve.tensor_scalar(stat[:], stat[:], 1e-24, None, ALU.max)
                dve.drain()
                dve.sem_inc(root_asked, 1)
                dve.wait_ge(rooted, 1)
                dve.reciprocal(mean[:], stat[:])
                dve.drain()
                dve.tensor_scalar(stat[:], mean[:], -1.0, None, ALU.mult)
                dve.drain()
                dve.tensor_tensor(by_head(removal[:]), by_head(removal[:]), over_tokens(stat), ALU.mult)
                dve.drain()
                dve.scalar_tensor_tensor(rates.rearrange("p c t -> p (c t)"), removal[:].rearrange("p c t -> p (c t)"),
                                         -1.0, rates.rearrange("p c t -> p (c t)"), ALU.mult, ALU.mult)
                dve.memset(states[:, 1, CK - 1, :], 0.0)
                dve.drain()

                def row(array, t):
                    at = array[:, :, bass.ds(t, 1)].rearrange("p (h j) o -> p h (o j)", h=PH)
                    return at.unsqueeze(2).broadcast_to([P, PH, HD, HD])

                def square_of(flat):
                    return flat.rearrange("p (h i j) -> p h i j", h=PH, j=HD)

                def chunk(c, slot):
                    dve.wait_ge(outer_ready, c + 1)
                    if not (isinstance(c, int) and c < 2):
                        dve.wait_ge(recalled_ready, c - 1)
                    for k in range(CK):
                        t = c * CK + k
                        old = states[:, slot, k - 1, :] if k else states[:, 1 - slot, CK - 1, :]
                        dve.tensor_tensor(square_of(removed[:]), square_of(old), row(removal, t), ALU.mult)
                        dve.tensor_tensor(square_of(decayed[:]), square_of(old), row(decays, t), ALU.mult)
                        dve.drain()
                        dve.tensor_reduce(sa[:], removed[:].rearrange("p (c j) -> p c j", j=HD), AX.X, ALU.add)
                        dve.tensor_tensor(decayed[:], decayed[:], outer[:, slot, k, :], ALU.add)
                        dve.drain()
                        dve.tensor_tensor(square_of(added[:]),
                                          sa[:].rearrange("p (h i) -> p h i", h=PH).unsqueeze(3).broadcast_to(
                                              [P, PH, HD, HD]), row(rates, t), ALU.mult)
                        dve.drain()
                        last = dve.tensor_tensor(states[:, slot, k, :], decayed[:], added[:], ALU.add)
                        if k < CK - 1:
                            dve.drain()
                    last.then_inc(states_ready, 1)
                    dve.drain()

                def collect(c):
                    dve.wait_ge(recalled_ready, c + 1)
                    dve.tensor_reduce(outputs[:], recalled[:].rearrange("p k (c j) -> p k c j", j=HD), AX.X,
                                      ALU.add).then_inc(recalled_used, 1)
                    dve.drain()
                    dve.tensor_copy(removal[:, :, bass.ds(c * CK, CK)].rearrange("p c t -> p t c"), outputs[:])
                    dve.drain()

                chunk(0, 0)
                chunk(1, 1)
                collect(0)
                with dve.Fori(1, CHUNKS // 2) as m:
                    for slot in range(2):
                        chunk(m * 2 + slot, slot)
                        collect(m * 2 + slot - 1)
                collect(CHUNKS - 1)
                dve.drain()
                dve.sem_inc(scan_done, 1)
                out = removal[:]
                sum_channels(mean, out)
                dve.drain()
                dve.tensor_scalar(mean[:], mean[:], 1.0 / HD, None, ALU.mult)
                dve.drain()
                dve.tensor_tensor(by_head(out), by_head(out), over_tokens(mean), ALU.subtract)
                dve.drain()
                dve.sem_inc(centred, 1)
                dve.wait_ge(squared, 2)
                sum_channels(stat, squares)
                dve.drain()
                dve.tensor_scalar(stat[:], stat[:], 1.0 / HD, 0.00064, ALU.mult, ALU.add)
                dve.drain()
                dve.sem_inc(root_asked, 1)
                dve.wait_ge(bonus_asked, 1)
                sum_channels(mean, recv[:])
                dve.drain()
                dve.tensor_tensor(by_head(values[:]), by_head(values[:]), over_tokens(mean), ALU.mult)
                dve.wait_ge(rooted, 2)
                dve.drain()
                dve.reciprocal(mean[:], stat[:])
                dve.drain()
                dve.tensor_tensor(by_head(out), by_head(out), over_tokens(mean), ALU.mult)
                dve.wait_ge(cols_in, 16)
                dve.drain()
                for c in range(PC):
                    dve.tensor_scalar(removal[:, c, :], removal[:, c, :], part_cols[:, 1, c:c + 1],
                                      part_cols[:, 2, c:c + 1], ALU.mult, ALU.add)
                dve.drain()
                dve.tensor_tensor(out, out, values[:], ALU.add).then_inc(out_ready, 1)

            @block.sync
            def _(sp):
                sp.dma_start(part_cols[:], dram["rwkv_part_cols"]).then_inc(cols_in, 16)
                sp.wait_ge(scan_done, 1)
                sp.dma_start(core.x[:], x_dram.rearrange("b (h p) c -> p (b h) c", p=P)).then_inc(x_back, 16)
                sp.wait_ge(out_ready, 1)
                for b in range(SEQS):
                    sp.dma_start(core.normed_t[:, b * SEQ:(b + 1) * SEQ],
                                 removal[b * GROUPS:(b + 1) * GROUPS, :, :]).then_inc(out_sent, 16)
                sp.wait_ge(out_sent, 16 * SEQS)
                sp.wait_ge(x_back, 16)

    HC = 4
    with ExitStack() as inner:
        isb = lambda n, shape, dtype=F32: core.sb(f"{name}_{n}", shape, dtype, ctx=inner)
        ffn = TurnedNorm(core, "rwkv_ffn", inner, core.bank[1])
        cols, wo = isb("out_cols", [P, 3]), isb("wo", [P, C])
        w1, w2 = isb("w1", [P, HC * P]), isb("w2", [P, HC, C])
        g_in, gated = isb("g_in", [P, PN]), isb("gated", [P, PN])
        padded, delta, mix = isb("padded2", [P, 2, SEQ + 1]), isb("delta2", [P, 2, SEQ]), isb("mix2", [P, 2, SEQ])
        relu, hidden = isb("relu", [P, HC, PN]), isb("hidden", [P, HC, PN])
        weights_in, g_loaded, gated_ready = sem2(core, "weights_in"), sem2(core, "g_loaded"), sem2(core, "gated_ready")
        wo_up, wo_taken = sem2(core, "wo_up"), sem2(core, "wo_taken")
        padded_ready, mix_ready = sem2(core, "padded_ready"), sem2(core, "mix_ready")
        hidden_up, relu_done, hidden_done = sem2(core, "hidden_up"), sem2(core, "relu_done"), sem2(core, "hidden_done")
        out_up, out_taken = sem2(core, "out_up"), sem2(core, "out_taken")
        block = inner.enter_context(nc.Block())

        @block.sync
        def _(sp):
            for to, what in ((cols, "out_cols"), (wo, "wo"), (w1, "w1"), (w2, "w2")):
                sp.dma_start(to[:], dram[f"rwkv_{what}"]).then_inc(weights_in, 16)
            with sp.Fori(0, PAIRS) as i:
                sp.wait_ge(gated_ready, i)
                sp.dma_start(g_in[:], g_rows[bass.ds(i, 1)].rearrange("a p n -> (a p) n")).then_inc(g_loaded, 16)

        @block.tensor
        def _(pe):
            pe.wait_ge(weights_in, 64)

            def finish(i):
                pe.wait_ge(hidden_done, (i + 1) * HC)
                pe.wait_ge(out_taken, i)
                for t in range(PT):
                    for f in range(HC):
                        last = pe.matmul(core.bank[6][:, t * P:(t + 1) * P], hidden[:, f, t * P:(t + 1) * P],
                                         w2[:, f, :], start=(f == 0), stop=(f == HC - 1))
                last.then_inc(out_up, 1)

            def pair(i, has_tail):
                pe.wait_ge(gated_ready, i + 1)
                pe.wait_ge(wo_taken, i)
                for t in range(PT):
                    last = pe.matmul(core.bank[0][:, t * P:(t + 1) * P], gated[:, t * P:(t + 1) * P], wo[:],
                                     start=True, stop=True)
                last.then_inc(wo_up, 1)
                if has_tail:
                    finish(i - 1)
                ffn.pe(pe, i)
                pe.wait_ge(mix_ready, i + 1)
                pe.wait_ge(relu_done, i * HC)
                for f in range(HC):
                    pe.matmul(core.bank[2 + f][:], w1[:, f * P:(f + 1) * P], mix[:].rearrange("p j t -> p (j t)"),
                              start=True, stop=True).then_inc(hidden_up, 1)
                if has_tail:
                    tail.pe(pe, i - 1)

            pair(0, False)
            with pe.Fori(1, PAIRS) as i:
                pair(i, True)
            finish(PAIRS - 1)
            tail.pe(pe, PAIRS - 1)

        @block.scalar
        def _(act):
            act.wait_ge(weights_in, 64)

            def pair(i, has_tail):
                act.wait_ge(mix_ready, i)
                ffn.act(act, i, padded[:, :, 1:], cols[:, 0:1], cols[:, 1:2])
                act.drain()
                act.sem_inc(padded_ready, 1)
                act.wait_ge(hidden_done, i * HC)
                for f in range(HC):
                    act.wait_ge(hidden_up, i * HC + f + 1)
                    act.activation(relu[:, f, :], core.bank[2 + f][:], ACT.Relu).then_inc(relu_done, 1)
                if has_tail:
                    tail.act(act, i - 1)

            pair(0, False)
            with act.Fori(1, PAIRS) as i:
                pair(i, True)
            tail.act(act, PAIRS - 1)

        @block.gpsimd
        def _(pool):
            def pair(i, has_tail):
                ffn.pool(pool, i)
                if has_tail:
                    tail.pool(pool, i - 1)
                pool.wait_ge(out_up, i)
                for f in range(HC):
                    pool.wait_ge(relu_done, i * HC + f + 1)
                    pool.tensor_tensor(hidden[:, f, :], relu[:, f, :], relu[:, f, :], ALU.mult).then_inc(hidden_done, 1)

            pair(0, False)
            with pool.Fori(1, PAIRS) as i:
                pair(i, True)
            tail.pool(pool, PAIRS - 1)

        @block.vector
        def _(dve):
            dve.wait_ge(weights_in, 64)
            dve.memset(padded[:], 0.0)
            dve.drain()
            flat = core.branch[:].rearrange("p t c -> p (t c)")
            x1 = lambda i: core.normed[:, bass.ds(i * PT, PT), :].rearrange("p t c -> p (t c)")
            x1_row = lambda i: lambda r: core.normed[:, i * PT + r, :]

            def take_out(i):
                dve.wait_ge(out_up, i + 1)
                dve.tensor_tensor(flat, core.bank[6][:], x1(i), ALU.add)
                dve.drain()
                dve.sem_inc(out_taken, 1)
                tail.dve_branch(dve, i)

            def pair(i, has_tail):
                dve.wait_ge(g_loaded, (i + 1) * 16)
                dve.wait_ge(wo_up, i)
                dve.tensor_tensor(gated[:], g_in[:], core.normed_t[:, bass.ds(i * PN, PN)],
                                  ALU.mult).then_inc(gated_ready, 1)
                dve.wait_ge(wo_up, i + 1)
                dve.tensor_tensor(x1(i), core.bank[0][:], x1(i), ALU.add)
                dve.drain()
                dve.sem_inc(wo_taken, 1)
                ffn.norm.find_moments(dve, x1_row(i))
                if has_tail:
                    take_out(i - 1)
                ffn.dve_rows(dve, i, x1_row(i))
                if has_tail:
                    tail.dve_stream(dve, i - 1)
                dve.wait_ge(padded_ready, i + 1)
                dve.tensor_tensor(delta[:], padded[:, :, 0:SEQ], padded[:, :, 1:], ALU.subtract)
                dve.drain()
                dve.wait_ge(hidden_up, i * HC)
                dve.scalar_tensor_tensor(mix[:], delta[:], cols[:, 2:3], padded[:, :, 1:], ALU.mult,
                                         ALU.add).then_inc(mix_ready, 1)
                if has_tail:
                    tail.dve_fresh(dve, i - 1)

            pair(0, False)
            with dve.Fori(1, PAIRS) as i:
                pair(i, True)
            take_out(PAIRS - 1)
            tail.dve_stream(dve, PAIRS - 1)
            tail.dve_fresh(dve, PAIRS - 1)


def sem2(core, name):
    return core.sem(f"rwkv_out_{name}")


def build(nc, dram, out, blocks=("rwkv", "moe0", "wave", "local", "ssm", "moe2", "mamba", "attn3")):
    with ExitStack() as ctx:
        core = Core(nc, ctx, dram)
        capacity = -(-TILES * P * 2 * 5 // (EXPERTS * 4))
        prologue(core, dram["x"])
        core.end_of_block()
        if "rwkv" in blocks:
            rwkv_block(core, Tail(core, "rwkv", keep_rows=False, turned=True), dram["x"])
            core.end_of_block()
        if "moe0" in blocks:
            moe_block(core, "moe0", Tail(core, "moe0", keep_rows=False, turned=True), shared=True, bias=True,
                      normalised=True, chunks=4)
            core.end_of_block()
        if "wave" in blocks:
            wave_block(core, Tail(core, "wave", keep_rows=True, turned=True))
            core.end_of_block()
        if "local" in blocks:
            local_layer(core, 0, Carry(core, "local0", keep_rows=False, turned=True))
            core.end_of_block()
            local_layer(core, 1, Tail(core, "local1", keep_rows=False, turned=True))
            core.end_of_block()
        if "ssm" in blocks:
            ssm_block(core, "ssm", Tail(core, "ssm", keep_rows=False, turned=True), 16, False)
            core.end_of_block()
        if "moe2" in blocks:
            moe_block(core, "moe2", Tail(core, "moe2", keep_rows=True, turned=False), shared=False, bias=True,
                      normalised=False, chunks=4)
            core.end_of_block()
        if "mamba" in blocks:
            ssm_block(core, "mamba", Tail(core, "mamba", keep_rows=True, turned=False), 4, True)
            core.end_of_block()
        if "attn3" in blocks:
            attention_over_sequences(core)
            core.end_of_block()
            moe_block(core, "moe3", Tail(core, "moe3", keep_rows=False, turned=False, last=True), shared=False,
                      bias=False, normalised=True, chunks=2, capacity=capacity, base=core.normed)
            core.end_of_block()
        stored = core.sem("stored")
        with nc.Block() as block:
            @block.sync
            def _(sp):
                sp.dma_start(out.rearrange("b (h p) c -> p (b h) c", p=P), core.x[:]).then_inc(stored, 16)
                sp.wait_ge(stored, 16)


def arrange(inputs):
    a = {k: np.ascontiguousarray(v) for k, v in inputs.items()}
    t = np.arange(P)
    bf16 = mybir.dt.np(BF16)
    out = {
        "identity": np.eye(P, dtype=np.float32),
        "earlier": (t[:, None] < t[None, :]).astype(np.float32),
        "ones": np.ones((P, P), np.float32),
    }

    def moe(name, w1, w2, b1=None, b2=None):
        e, f, d = w1.shape
        out[f"{name}_w1"] = w1.transpose(2, 0, 1)
        out[f"{name}_w2"] = w2.reshape(e, d, f // P, P).transpose(3, 0, 2, 1)
        if b1 is not None:
            out[f"{name}_b1"] = b1.reshape(e, f // P, P).transpose(2, 0, 1).reshape(P, -1)
            out[f"{name}_b2"] = b2

    moe("moe0", np.concatenate([a["L0_ffn_shared_w1"][None], a["L0_ffn_spec_w1"]]),
        np.concatenate([a["L0_ffn_shared_w2"][None], a["L0_ffn_spec_w2"]]),
        np.concatenate([a["L0_ffn_shared_b1"][None], a["L0_ffn_spec_b1"]]),
        np.concatenate([a["L0_ffn_shared_b2"][None], a["L0_ffn_spec_b2"]]))
    out["moe0_router"] = a["L0_ffn_router_w"].T
    out["moe0_router_b"] = a["L0_ffn_router_b"][:, None]
    moe("moe2", a["L2_ffn_w1"].transpose(1, 0, 2), a["L2_ffn_w2"].transpose(1, 0, 2), a["L2_ffn_b1"], a["L2_ffn_b2"])
    out["moe2_router"] = a["L2_ffn_gate_w"].T
    moe("moe3", a["L3_ffn_moe_w1"].transpose(0, 2, 1), a["L3_ffn_moe_w2"].transpose(0, 2, 1))
    out["moe3_router"] = a["L3_ffn_router_weight"]

    def columns(*names):
        return np.stack([a[n].reshape(-1) for n in names], axis=1)

    out["attn_cols"] = columns("L3_ffn_ln1_weight", "L3_ffn_ln1_bias", "L3_ffn_ln2_weight", "L3_ffn_ln2_bias")
    out["attn_wqkv"] = a["L3_ffn_qkv_weight"].T
    out["attn_wproj"] = a["L3_ffn_proj_weight"].T

    def ssm(name, w_in, wx, wbc, wgate, wdt, w_out, taps, conv_b, heads, cols, head_cols):
        inner = 2 * C
        out[f"{name}_wx"], out[f"{name}_wdt"], out[f"{name}_wgate"] = w_in[:, wx], w_in[:, wdt], wgate
        out[f"{name}_wbc"] = wbc
        out[f"{name}_wout"] = w_out.reshape(inner // P, P, C).transpose(1, 0, 2)
        out[f"{name}_taps"] = np.concatenate([taps, conv_b[:, None]], axis=1).reshape(inner // P, P, 5).transpose(1, 0, 2)
        out[f"{name}_cols"], out[f"{name}_head_cols"] = cols, head_cols
        row = np.arange(96)
        mine = ((row % 32)[:, None] == np.arange(heads)[None, :])
        out[f"{name}_pick"] = np.broadcast_to(mine[:, :, None], (96, heads, P)).astype(bf16)
        out[f"{name}_unpick"] = (-mine.astype(np.float32)).astype(bf16)

    out["identity16"] = np.eye(P, dtype=bf16)
    out["future"] = np.where(t[:, None] <= t[None, :], 0.0, -BIG).astype(bf16)
    w_in, nw = a["L2_attn_W_in"], a["L2_attn_norm_w"]
    ssm("ssm", w_in, slice(0, 256), w_in[:, 256:2304].reshape(P, 16, P), a["L2_attn_W_gate"], slice(2304, 2320),
        a["L2_attn_W_out"], a["L2_attn_conv_w"], a["L2_attn_conv_b"], 16, nw.reshape(2, P).T,
        np.stack([a["L2_attn_delta_param"]] * 2, axis=1))
    w_in, ns = a["L3_attn_w_in"], a["L3_attn_norm_scale"]
    ssm("mamba", w_in, slice(256, 512), w_in[:, 516:644].reshape(P, 2, 64), w_in[:, 0:256], slice(512, 516),
        a["L3_attn_w_out"], a["L3_attn_conv_weight"].T, a["L3_attn_conv_bias"], 4, np.stack([ns, ns], axis=1),
        np.stack([a["L3_attn_dt_bias"], a["L3_attn_A_log"]], axis=1))

    hd, f32 = 64, np.float32
    half = np.arange(0, hd, 2, dtype=f32)
    pos = np.arange(SEQ, dtype=f32)
    freqs = pos[:, None] * (f32(1.0) / f32(10000.0) ** (half / f32(hd)))[None, :]
    freqs = np.concatenate([freqs, freqs], axis=1)
    base = (half + f32(0.4 * hd)) / f32(1.4 * hd)
    scale = base[None, :] ** ((pos - SEQ // 2) / f32(32.0))[:, None]
    scale = np.concatenate([scale, scale], axis=1)
    sign = np.where(np.arange(hd) < hd // 2, f32(-1.0), f32(1.0))
    tabs = np.stack([np.stack([np.cos(freqs) * scale * f32(8.0), np.sin(freqs) * sign * scale * f32(8.0)]),
                     np.stack([np.cos(freqs) / scale, np.sin(freqs) * sign / scale])])
    out["rotary"] = tabs.reshape(2, 2, 2, P, hd).transpose(3, 0, 2, 1, 4).astype(f32)
    blocks = []
    for q0, k0 in ((0, 0), (P, 0), (P, P)):
        gap = (t[:, None] + q0) - (t[None, :] + k0)
        blocks.append(np.where((gap >= 0) & (gap <= 64), 0.0, -BIG))
    out["window"] = np.concatenate(blocks, axis=1).astype(bf16)
    hid = a["L1_ffn_w2"].shape[1]
    fc = -(-hid // P)

    def padded(v):
        return np.concatenate([v, np.zeros((*v.shape[:-1], fc * P - hid), v.dtype)], axis=-1)

    for l in range(2):
        w1, b1 = a["L1_ffn_w1"][l], a["L1_ffn_b1"][l]
        out[f"local{l}_wqkv"] = a["L1_ffn_wqkv"][l]
        out[f"local{l}_wo"] = a["L1_ffn_wo"][l].reshape(4, P, C).transpose(1, 0, 2)
        both = np.stack([padded(w1[:, :hid]), padded(w1[:, hid:])])
        out[f"local{l}_w1"] = both.reshape(2, C, fc, P).transpose(1, 2, 0, 3)
        out[f"local{l}_w2"] = padded(a["L1_ffn_w2"][l].T).reshape(C, fc, P).transpose(2, 1, 0)
        out[f"local{l}_cols"] = np.concatenate(
            [a["L1_ffn_ln_g"][l][:, None], a["L1_ffn_ln_b"][l][:, None], padded(b1[:hid]).reshape(fc, P).T,
             padded(b1[hid:]).reshape(fc, P).T], axis=1)
        out[f"local{l}_b2"] = a["L1_ffn_b2"][l][None]
        own = np.stack([a["L1_ffn_q_scale"][l], a["L1_ffn_k_scale"][l]])
        other = np.concatenate([own[:, hd // 2:], own[:, :hd // 2]], axis=1)
        out[f"local{l}_scales"] = np.stack([own, other], axis=1).reshape(-1)

    out["wave_params"] = np.stack([a["L1_attn_wave_frequency"], a["L1_attn_wave_damping"],
                                   a["L1_attn_wave_phase"], a["L1_attn_wave_phase"]], axis=1)
    out["wave_time"] = np.broadcast_to(pos[None], (16, SEQ))
    out["wave_coupling"] = a["L1_attn_field_coupling"]
    out["wave_w"] = a["L1_attn_Wqkvg"].reshape(4, C, C).transpose(2, 0, 1)
    out["wave_cols"] = a["L1_attn_bqkvg"].reshape(4, C).T
    out["wave_wout"], out["wave_bout"] = a["L1_attn_Wout"].T, a["L1_attn_bout"][None]
    head, channel = np.arange(P) // 8, np.arange(P) % 8
    out["wave_spread"] = (np.arange(16)[:, None] == head[None, :]).astype(f32)
    out["wave_same"] = (channel[:, None] == channel[None, :]).astype(f32)

    L = lambda n: a["L0_attn_" + n]
    out["rwkv_pre_rows"] = np.concatenate([L("ln_pre_w"), L("ln_pre_b")])
    out["rwkv_cols"] = columns(*("L0_attn_" + n for n in (
        "ln_attn_w", "ln_attn_b", "x_r", "x_w", "x_k", "x_v", "x_a", "x_g", "w0", "a0", "k_k", "k_a")))
    out["rwkv_wide"] = np.stack([L("W_r"), L("W_k"), L("W_v"), L("g1"), L("g2")], axis=1)
    out["rwkv_low"] = np.stack([L("w1"), L("a1")], axis=1)
    out["rwkv_high"] = np.stack([L("w2"), L("a2")], axis=1)
    per_part = np.stack([L("r_k").reshape(8, 16), L("gn_w").reshape(8, 16), L("gn_b").reshape(8, 16)], axis=1)
    out["rwkv_part_cols"] = np.broadcast_to(per_part[None], (SEQS, 8, 3, 16)).reshape(P, 3, 16)
    out["rwkv_out_cols"] = columns("L0_attn_ln_ffn_w", "L0_attn_ln_ffn_b", "L0_attn_ffn_x_k")
    out["rwkv_wo"], out["rwkv_w1"] = L("W_o"), L("W_ffn1")
    out["rwkv_w2"] = L("W_ffn2").reshape(4, P, C).transpose(1, 0, 2)
    out = {k: np.ascontiguousarray(v) for k, v in out.items()}
    out["x"] = a["L0_attn_x"]
    return out


def kernel(**inputs):
    import concourse.bacc as bacc
    from concourse.bass_utils import run_bass_kernel_spmd

    nc = bacc.Bacc("TRN2", target_bir_lowering=False, num_devices=1)
    arrays, dram = {}, {}
    for name, array in arrange(inputs).items():
        arrays[f"in_{name}_dram"] = array
        dram[name] = nc.dram_tensor(f"in_{name}_dram", array.shape, mybir.dt.from_np(array.dtype),
                                    kind="ExternalInput").ap()
    out = nc.dram_tensor("out_dram", (SEQS, SEQ, C), F32, kind="ExternalOutput").ap()
    build(nc, dram, out)
    got = run_bass_kernel_spmd(nc, [arrays], core_ids=[0])
    return got.results[0]["out_dram"]
```
